# Optimizing a Trainium2 kernel written in Bass

```python
import numpy as np
import jax
import jax.numpy as jnp

def _softmax(x, axis=-1):
    return jax.nn.softmax(x, axis=axis)

def _gelu(x):
    return jax.nn.gelu(x, approximate=True)

def _silu(x):
    return jax.nn.silu(x)

def _sigmoid(x):
    return jax.nn.sigmoid(x)

def _layernorm(x, axis=-1, eps=1e-05):
    m = jnp.mean(x, axis=axis, keepdims=True)
    v = jnp.var(x, axis=axis, keepdims=True)
    return (x - m) / jnp.sqrt(v + eps)

def _scatter_add(tgt, idx, src, axis=0):
    return tgt.at[idx].add(src)

def _segment_sum(src, seg, n):
    return jax.ops.segment_sum(src, seg, n)
kernel_name = 'mk_decoder_postln_d1_seqx_r8_b8723d'

def setup_inputs(seed: int=0):
    np.random.seed(seed)
    _w = jnp.asarray

    def _rec_inputs():
        import jax
        import jax.numpy as jnp
        _rk = jax.random.key(seed)
        x = -0.0005207 + 1.001 * jax.random.normal(jax.random.fold_in(_rk, 1), (128, 64, 128), jnp.float32)
        _lenS = 64 - jax.random.randint(jax.random.fold_in(_rk, 7), (128,), 0, max(1, 64 // 4) + 1, jnp.int32)
        _lenS2 = 64 - jax.random.randint(jax.random.fold_in(_rk, 8), (128,), 0, max(1, 64 // 4) + 1, jnp.int32)
        _ctx_512P = jax.random.normal(jax.random.fold_in(_rk, 11), (128, 16, 64), jnp.float32)
        _ctx_512c = jax.random.dirichlet(jax.random.fold_in(_rk, 511), 0.3 * jnp.ones((16,), jnp.float32), (128, 64))
        _ctx_512t = jnp.einsum('bsk,bkd->bsd', _ctx_512c, _ctx_512P)
        _ctx_512t = _ctx_512t * jax.lax.rsqrt(jnp.mean(jnp.square(_ctx_512t)) + 1e-12) * 0.953939
        ctx_512 = 0.502058 + 0.29099 * (_ctx_512t + 0.3 * jax.random.normal(jax.random.fold_in(_rk, 611), (128, 64, 64), jnp.float32))
        itok_BxS2xS_0_7 = jax.random.randint(jax.random.fold_in(_rk, 12), (128, 64, 64), 0, 8, jnp.int32)
        return (x, ctx_512, itok_BxS2xS_0_7)
    x, ctx_512, itok_BxS2xS_0_7 = _rec_inputs()

    def _L0_attn_setup():
        import jax, jax.numpy as jnp
        import numpy as np
        DT_MAX = 10.0
        RATE_EPS = 0.0001

        def _ssm_forward(x, W_in, W_state, W_dt, b_dt, A_log, W_C, D, W_out):
            B, L, d_model = x.shape
            ug = jnp.einsum('bld,ed->ble', x, W_in)
            u, gate = jnp.split(ug, 2, axis=-1)
            b_t = jnp.einsum('bld,nd->bln', u, W_state)
            dt_t = jnp.minimum(jax.nn.softplus(jnp.einsum('bld,nd->bln', u, W_dt) + b_dt), DT_MAX)
            rate = jax.nn.softplus(A_log) + RATE_EPS
            decay = jnp.clip(jnp.exp(-dt_t * rate), 0.0, 1.0)

            def step(h, inp):
                d_t, bt = inp
                h = d_t * h + (1.0 - d_t) * bt
                return (h, h)
            h0 = jnp.zeros((B, b_t.shape[-1]), x.dtype)
            xs = (jnp.swapaxes(decay, 0, 1), jnp.swapaxes(b_t, 0, 1))
            _, hs = jax.lax.scan(step, h0, xs)
            hs = jnp.swapaxes(hs, 0, 1)
            y = jnp.einsum('bln,dn->bld', hs, W_C)
            z = y * jax.nn.silu(gate) + x * D
            return jnp.einsum('bld,ed->ble', z, W_out)
        key = jax.random.key(seed)
        ks = jax.random.split(key, 8)
        B, L, D_MODEL, D_STATE = (4, 256, 128, 128)
        s = lambda fan_in: 1.0 / np.sqrt(fan_in)
        return {'x': jax.random.normal(ks[0], (B, L, D_MODEL), jnp.float32), 'W_in': jax.random.normal(ks[1], (2 * D_MODEL, D_MODEL), jnp.float32) * s(D_MODEL), 'W_state': jax.random.normal(ks[2], (D_STATE, D_MODEL), jnp.float32) * s(D_MODEL), 'W_dt': jax.random.normal(ks[3], (D_STATE, D_MODEL), jnp.float32) * s(D_MODEL), 'b_dt': jax.random.normal(ks[4], (D_STATE,), jnp.float32) * s(D_MODEL), 'A_log': jnp.zeros((D_STATE,), jnp.float32), 'W_C': jax.random.normal(ks[5], (D_MODEL, D_STATE), jnp.float32) * s(D_STATE), 'D': jnp.ones((D_MODEL,), jnp.float32), 'W_out': jax.random.normal(ks[6], (D_MODEL, D_MODEL), jnp.float32) * s(D_MODEL)}
    _L0_attn_all = _L0_attn_setup()
    _L0_attn_in = {k: v for k, v in _L0_attn_all.items() if k in ('W_in', 'W_state', 'W_dt', 'b_dt', 'A_log', 'W_C', 'D', 'W_out')}
    del _L0_attn_all

    def _L0_xattn_setup():
        import jax, jax.numpy as jnp
        import numpy as np
        key = jax.random.key(seed)
        k1, k2, k3, k4, k5 = jax.random.split(key, 5)
        B, K, S, E, I, D = (4, 2, 64, 8, 128, 256)
        x = jax.random.normal(k1, (B, S, I), dtype=jnp.float32)
        weights = jax.random.uniform(k2, (B, K, S), dtype=jnp.float32)
        ensembles = jax.random.randint(k3, (B, K, S), 0, E, dtype=jnp.int64)
        lim1 = float(np.sqrt(6.0 / (D + I)))
        proj_in = jax.random.uniform(k4, (E, D, I), dtype=jnp.float32, minval=-lim1, maxval=lim1)
        proj_out = jax.random.uniform(k5, (E, I, D), dtype=jnp.float32, minval=-lim1, maxval=lim1)
        return {'x': x, 'weights': weights, 'ensembles': ensembles, 'proj_in': proj_in, 'proj_out': proj_out}
    _L0_xattn_all = _L0_xattn_setup()
    _L0_xattn_in = {k: v for k, v in _L0_xattn_all.items() if k in ('proj_in', 'proj_out')}
    del _L0_xattn_all

    def _L0_ffn_setup():
        import jax, jax.numpy as jnp
        import numpy as np
        B, T, D, H = (4, 256, 128, 256)
        E, S, K = (8, 2, 2)

        def _swiglu_stacked(x, w1, b1, w2, b2, w3, b3):
            p1 = jnp.einsum('btd,ndh->nbth', x, w1) + b1[:, None, None, :]
            p2 = jnp.einsum('btd,ndh->nbth', x, w2) + b2[:, None, None, :]
            glu = jax.nn.silu(p1) * p2
            return jnp.einsum('nbth,nhd->nbtd', glu, w3) + b3[:, None, None, :]
        key = jax.random.key(seed)
        ks = jax.random.split(key, 10)
        s = 0.02
        return {'x': jax.random.normal(ks[0], (B, T, D), jnp.float32), 'gate_w': jax.random.normal(ks[1], (D, E), jnp.float32) * s, 'gate_b': jnp.zeros((E,), jnp.float32), 'rw1': jax.random.normal(ks[2], (E, D, H), jnp.float32) * s, 'rb1': jnp.zeros((E, H), jnp.float32), 'rw2': jax.random.normal(ks[3], (E, D, H), jnp.float32) * s, 'rb2': jnp.zeros((E, H), jnp.float32), 'rw3': jax.random.normal(ks[4], (E, H, D), jnp.float32) * s, 'rb3': jnp.zeros((E, D), jnp.float32), 'sw1': jax.random.normal(ks[5], (S, D, H), jnp.float32) * s, 'sb1': jnp.zeros((S, H), jnp.float32), 'sw2': jax.random.normal(ks[6], (S, D, H), jnp.float32) * s, 'sb2': jnp.zeros((S, H), jnp.float32), 'sw3': jax.random.normal(ks[7], (S, H, D), jnp.float32) * s, 'sb3': jnp.zeros((S, D), jnp.float32)}
    _L0_ffn_all = _L0_ffn_setup()
    _L0_ffn_in = {k: v for k, v in _L0_ffn_all.items() if k in ('gate_w', 'gate_b', 'rw1', 'rb1', 'rw2', 'rb2', 'rw3', 'rb3', 'sw1', 'sb1', 'sw2', 'sb2', 'sw3', 'sb3')}
    del _L0_ffn_all
    return {'x': x, 'ctx_512': ctx_512, 'itok_BxS2xS_0_7': itok_BxS2xS_0_7, 'L0_attn_W_in': _L0_attn_in['W_in'], 'L0_attn_W_state': _L0_attn_in['W_state'], 'L0_attn_W_dt': _L0_attn_in['W_dt'], 'L0_attn_b_dt': _L0_attn_in['b_dt'], 'L0_attn_A_log': _L0_attn_in['A_log'], 'L0_attn_W_C': _L0_attn_in['W_C'], 'L0_attn_D': _L0_attn_in['D'], 'L0_attn_W_out': _L0_attn_in['W_out'], 'L0_xattn_proj_in': _L0_xattn_in['proj_in'], 'L0_xattn_proj_out': _L0_xattn_in['proj_out'], 'L0_ffn_gate_w': _L0_ffn_in['gate_w'], 'L0_ffn_gate_b': _L0_ffn_in['gate_b'], 'L0_ffn_rw1': _L0_ffn_in['rw1'], 'L0_ffn_rb1': _L0_ffn_in['rb1'], 'L0_ffn_rw2': _L0_ffn_in['rw2'], 'L0_ffn_rb2': _L0_ffn_in['rb2'], 'L0_ffn_rw3': _L0_ffn_in['rw3'], 'L0_ffn_rb3': _L0_ffn_in['rb3'], 'L0_ffn_sw1': _L0_ffn_in['sw1'], 'L0_ffn_sb1': _L0_ffn_in['sb1'], 'L0_ffn_sw2': _L0_ffn_in['sw2'], 'L0_ffn_sb2': _L0_ffn_in['sb2'], 'L0_ffn_sw3': _L0_ffn_in['sw3'], 'L0_ffn_sb3': _L0_ffn_in['sb3']}

def reference(x, ctx_512, itok_BxS2xS_0_7, L0_attn_W_in, L0_attn_W_state, L0_attn_W_dt, L0_attn_b_dt, L0_attn_A_log, L0_attn_W_C, L0_attn_D, L0_attn_W_out, L0_xattn_proj_in, L0_xattn_proj_out, L0_ffn_gate_w, L0_ffn_gate_b, L0_ffn_rw1, L0_ffn_rb1, L0_ffn_rw2, L0_ffn_rb2, L0_ffn_rw3, L0_ffn_rb3, L0_ffn_sw1, L0_ffn_sb1, L0_ffn_sw2, L0_ffn_sb2, L0_ffn_sw3, L0_ffn_sb3):
    import jax
    import jax.numpy as jnp

    def _L0_attn_ref(x, W_in, W_state, W_dt, b_dt, A_log, W_C, D, W_out):
        import jax, jax.numpy as jnp
        import numpy as np
        DT_MAX = 10.0
        RATE_EPS = 0.0001

        def _ssm_forward(x, W_in, W_state, W_dt, b_dt, A_log, W_C, D, W_out):
            B, L, d_model = x.shape
            ug = jnp.einsum('bld,ed->ble', x, W_in)
            u, gate = jnp.split(ug, 2, axis=-1)
            b_t = jnp.einsum('bld,nd->bln', u, W_state)
            dt_t = jnp.minimum(jax.nn.softplus(jnp.einsum('bld,nd->bln', u, W_dt) + b_dt), DT_MAX)
            rate = jax.nn.softplus(A_log) + RATE_EPS
            decay = jnp.clip(jnp.exp(-dt_t * rate), 0.0, 1.0)

            def step(h, inp):
                d_t, bt = inp
                h = d_t * h + (1.0 - d_t) * bt
                return (h, h)
            h0 = jnp.zeros((B, b_t.shape[-1]), x.dtype)
            xs = (jnp.swapaxes(decay, 0, 1), jnp.swapaxes(b_t, 0, 1))
            _, hs = jax.lax.scan(step, h0, xs)
            hs = jnp.swapaxes(hs, 0, 1)
            y = jnp.einsum('bln,dn->bld', hs, W_C)
            z = y * jax.nn.silu(gate) + x * D
            return jnp.einsum('bld,ed->ble', z, W_out)
        return _ssm_forward(x, W_in, W_state, W_dt, b_dt, A_log, W_C, D, W_out)

    def _L0_xattn_ref(x, weights, ensembles, proj_in, proj_out):
        import jax, jax.numpy as jnp
        import numpy as np
        E = proj_in.shape[0]
        h = jax.nn.relu(jnp.einsum('edi,bsi->bsed', proj_in, x))
        o = jnp.einsum('eid,bsed->bsei', proj_out, h)
        onehot = jax.nn.one_hot(ensembles, E, dtype=x.dtype)
        gate = jnp.einsum('bks,bkse->bse', weights, onehot)
        return jnp.einsum('bsei,bse->bsi', o, gate)

    def _L0_ffn_ref(x, gate_w, gate_b, rw1, rb1, rw2, rb2, rw3, rb3, sw1, sb1, sw2, sb2, sw3, sb3):
        import jax, jax.numpy as jnp
        import numpy as np
        B, T, D, H = (4, 256, 128, 256)
        E, S, K = (8, 2, 2)

        def _swiglu_stacked(x, w1, b1, w2, b2, w3, b3):
            p1 = jnp.einsum('btd,ndh->nbth', x, w1) + b1[:, None, None, :]
            p2 = jnp.einsum('btd,ndh->nbth', x, w2) + b2[:, None, None, :]
            glu = jax.nn.silu(p1) * p2
            return jnp.einsum('nbth,nhd->nbtd', glu, w3) + b3[:, None, None, :]
        scores = jax.nn.softmax(x @ gate_w + gate_b, axis=-1)
        weights, indices = jax.lax.top_k(scores, K)
        routed_all = _swiglu_stacked(x, rw1, rb1, rw2, rb2, rw3, rb3)
        out_bted = jnp.transpose(routed_all, (1, 2, 0, 3))
        gathered = jnp.take_along_axis(out_bted, indices[..., None], axis=2)
        routed = jnp.sum(weights[..., None] * gathered, axis=2)
        shared = _swiglu_stacked(x, sw1, sb1, sw2, sb2, sw3, sb3).mean(axis=0)
        return shared + routed
    x = _layernorm(x + _L0_attn_ref(x, L0_attn_W_in, L0_attn_W_state, L0_attn_W_dt, L0_attn_b_dt, L0_attn_A_log, L0_attn_W_C, L0_attn_D, L0_attn_W_out), axis=-1)
    x = _layernorm(x + _L0_xattn_ref(x, ctx_512, itok_BxS2xS_0_7, L0_xattn_proj_in, L0_xattn_proj_out), axis=-1)
    x = _layernorm(x + _L0_ffn_ref(x, L0_ffn_gate_w, L0_ffn_gate_b, L0_ffn_rw1, L0_ffn_rb1, L0_ffn_rw2, L0_ffn_rb2, L0_ffn_rw3, L0_ffn_rb3, L0_ffn_sw1, L0_ffn_sb1, L0_ffn_sw2, L0_ffn_sb2, L0_ffn_sw3, L0_ffn_sb3), axis=-1)
    return x

_drawn_inputs = setup_inputs


def setup_inputs(seed=0):
    import zlib

    import numpy as np

    out = dict(_drawn_inputs(seed))
    spreads = {'L0_attn_A_log': (0.0, 0.8),
     'L0_attn_D': (1.0, 0.2),
     'L0_ffn_gate_b': (0.0, 0.515),
     'L0_ffn_rb1': (0.0, 0.8),
     'L0_ffn_rb2': (0.0, 0.8),
     'L0_ffn_rb3': (0.0, 0.902),
     'L0_ffn_sb1': (0.0, 0.8),
     'L0_ffn_sb2': (0.0, 0.8),
     'L0_ffn_sb3': (0.0, 0.716)}
    factors = {'L0_attn_b_dt': 6.682,
     'L0_ffn_gate_w': 3.014,
     'L0_ffn_rw1': 8.0,
     'L0_ffn_rw2': 8.0,
     'L0_ffn_rw3': 8.0,
     'L0_ffn_sw1': 8.0,
     'L0_ffn_sw2': 8.0,
     'L0_ffn_sw3': 8.0}
    for name, (base, spread) in spreads.items():
        noise = np.random.default_rng([zlib.crc32(name.encode()), seed]).standard_normal(out[name].shape)
        drawn = base * np.exp(spread * noise) if base else spread * noise
        out[name] = jnp.asarray(drawn.astype(out[name].dtype))
    for name, factor in factors.items():
        out[name] = (out[name] * factor).astype(out[name].dtype)
    return out
```

```python
from contextlib import ExitStack

import concourse.bass as bass
from concourse import mybir

ALU = mybir.AluOpType
ACT = mybir.ActivationFunctionType
AX = mybir.AxisListType
F32 = mybir.dt.float32
F32R = mybir.dt.float32r
BF16 = mybir.dt.bfloat16
I32 = mybir.dt.int32
U32 = mybir.dt.uint32

P = 128


def decoder_layer(nc, a, out):
    xT, w_ctx, ens = a["xT"], a["w_ctx"], a["ens"]
    D, TOK = xT.shape
    K = w_ctx.shape[0]
    E = a["proj_in"].shape[1]
    H = a["w1"].shape[2]
    NS = a["sw1"].shape[1]
    SEQ = a["seq"]
    T = 512
    NT = TOK // T
    SUB = T // P
    HALF = H // P
    NE = a["w1"].shape[1]
    NROW = TOK // P
    NBLK = (2 * TOK + NE * (T - 1)) // T
    ROW = D + 2
    DEEP = 4
    EPS = 1e-5
    DT_MAX = 10.0
    RATE_EPS = 1e-4
    assert D == P and 2 * K == P and H == 2 * P and NS == 2 and NT % 2 == 0 and NBLK % DEEP == 3
    W3AT, B1AT, B2AT, B3AT = 4 * H, 4 * H + HALF * D, 4 * H + HALF * D + HALF, 4 * H + HALF * D + 2 * HALF
    PACK = B3AT + D

    x2_dram = nc.dram_tensor("x2_dram", (NT, P, T), F32).ap()
    pack_dram = nc.dram_tensor("pack_dram", (NE, P, PACK), F32).ap()
    sorted_dram = nc.dram_tensor("sorted_dram", (NBLK * T, ROW), F32).ap()
    routed_dram = nc.dram_tensor("routed_dram", (2 * TOK, D), F32).ap()

    with ExitStack() as ctx:
        def sb(name, shape, dt=F32):
            return ctx.enter_context(nc.sbuf_tensor(name, shape, dt))

        def sem(name):
            return ctx.enter_context(nc.semaphore(name))

        ps = ctx.enter_context(nc.psum_tensor("ps", [P, 8, T], F32))

        gate_proj = sb("gate_proj", [P, D])
        w_u = sb("w_u", [P, D])
        state_dt = sb("state_dt", [P, 2, D])
        from_u = sb("from_u", [P, 2, D])
        w_c = sb("w_c", [P, D])
        w_out = sb("w_out", [P, D])
        w_skip = sb("w_skip", [P, D])
        vecs = sb("vecs", [P, 16])
        sw = sb("sw", [P, NS, 2, H])
        sw_hi = sb("sw_hi", [P, NS, 2, H], F32R)
        sw_lo = sb("sw_lo", [P, NS, 2, H], F32R)
        sw3 = sb("sw3", [P, NS * HALF, D])
        sb12 = sb("sb12", [P, NS, 2, HALF])
        sb3 = sb("sb3", [P, NS, D])
        rw12 = sb("rw12", [P, 2, H])
        pack = sb("pack", [P, PACK])
        rw3 = sb("rw3", [P, NE * HALF, D])
        rb12 = sb("rb12", [P, NE, 2, HALF])
        rb3 = sb("rb3", [P, NE, D])
        router_w = sb("router_w", [P, NE])
        router_b = sb("router_b", [P, NE])
        means = sb("means", [P, 2 * 16])
        ident = sb("ident", [P, P])
        mean_mat = sb("mean_mat", [P, P])
        ones_r = sb("ones_r", [P, P], F32R)

        score = sb("score", [P, NROW, NE])
        best = sb("best", [P, 4, NROW])
        first = sb("first", [P, NROW, NE])
        second = sb("second", [P, NROW, NE])
        work = sb("work", [P, NROW, NE])
        chosen = sb("chosen", [P, NROW, NE], BF16)
        upto = sb("upto", [P, NROW, NE])
        prefer = sb("prefer", [P, NE])
        prefer_i = sb("prefer_i", [P, NE], I32)
        steps_i = sb("steps_i", [P, 64], I32)
        steps = sb("steps", [P, 64])
        above_i = sb("above_i", [P, P], I32)
        before = sb("before", [P, P], BF16)
        ones_b = sb("ones_b", [P, P], BF16)
        ones_f = sb("ones_f", [P, NROW])
        blocks = sb("blocks", [P, 4, NE])
        over = sb("over", [P, NE, 16])
        owner = sb("owner", [P, 40, NE])
        owner_f = sb("owner_f", [P, 40])
        owner_i = sb("owner_i", [P, 40], I32)
        slot_f = sb("slot_f", [P, NROW, 2])
        slot = sb("slot", [P, NROW, 2], U32)
        goes_to = sb("goes_to", [P, NROW, 2], U32)
        weight = sb("weight", [P, NROW, 2])
        blank = sb("blank", [P, ROW])

        over_a = ExitStack()

        def sb_a(name, shape, dt=F32):
            return over_a.enter_context(nc.sbuf_tensor(name, shape, dt))

        proj_in = sb_a("proj_in", [P, E, H])
        proj_in_hi = sb_a("proj_in_hi", [P, E, H], F32R)
        proj_in_lo = sb_a("proj_in_lo", [P, E, H], F32R)
        proj_out = sb_a("proj_out", [P, E * HALF, D])
        hid = sb_a("hid", [P, 2, HALF, T])
        masked = sb_a("masked", [P, 2, T], F32R)
        gsb = sb_a("gsb", [P, 2, T])
        xin = sb_a("xin", [P, 2, T])
        wraw = sb_a("wraw", [P, 2, T])
        eraw = sb_a("eraw", [P, 2, T], I32)
        wparts = sb_a("wparts", [P, T], F32R)
        e_dt = sb_a("e_dt", [P, T])
        decay = sb_a("decay", [P, T])
        drive = sb_a("drive", [P, T])
        states = sb_a("states", [P, T])
        e_gate = sb_a("e_gate", [P, T])
        sgate = sb_a("sgate", [P, T])
        mixed = sb_a("mixed", [P, T])
        square = sb_a("square", [P, T])
        logv = sb_a("logv", [P, T])
        rstd1 = sb_a("rstd1", [P, T])
        rstd2 = sb_a("rstd2", [P, T])
        x1 = sb_a("x1", [P, 2, T])
        x1_hi = sb_a("x1_hi", [P, 2, T], F32R)
        x1_lo = sb_a("x1_lo", [P, 2, T], F32R)
        x2c = sb_a("x2c", [P, T])
        x2 = sb_a("x2", [P, 2, T])
        over_a.close()

        xb = sb("xb", [P, 2, T])
        xs_hi = sb("xs_hi", [P, 2, T], F32R)
        xs_lo = sb("xs_lo", [P, 2, T], F32R)
        silu = sb("silu", [P, 2, T])
        glu = sb("glu", [P, 2, NS * HALF, T])
        rows = sb("rows", [P, 2, SUB, 2, ROW])
        based = sb("based", [P, T])
        total = sb("total", [P, NROW, D])
        wb = sb("wb", [P, DEEP, PACK], F32R)
        xr = sb("xr", [P, DEEP, SUB, ROW])
        res = sb("res", [P, T])
        weighed = sb("weighed", [P, 2, SUB, D])
        y1 = sb("y1", [P, 2, SUB, D])
        y2 = sb("y2", [P, 2, SUB, D])
        outb = sb("outb", [P, 2, SUB, D])
        sqc = sb("sqc", [P, SUB, P])
        slot_now = sb("slot_now", [P, 2, SUB * 2], U32)
        ssq = sb("ssq", [P, 4, SUB])

        RATE, FLOOR, BDT, DVEC, ALOG, EPSC, TMP, TMP2, TMP3 = (vecs[:, n:n + 1] for n in range(9))

        early_in = sem("early_in")
        late_in = sem("late_in")
        iotas = sem("iotas")
        consts = sem("consts")
        vec_exp = sem("vec_exp")
        vec_ln = sem("vec_ln")
        composed = sem("composed")
        weights_ready = sem("weights_ready")
        late_ready = sem("late_ready")
        s_dve = sem("dve_step")
        s_act = sem("act_step")
        x_in = [sem("x_in0"), sem("x_in1")]
        ctx_in = [sem("ctx_in0"), sem("ctx_in1")]
        mask_ready = sem("mask_ready")
        gate_ready = sem("gate_ready")
        gsb_ready = sem("gsb_ready")
        h_ready = sem("h_ready")
        hid_ready = sem("hid_ready")
        down_done = sem("down_done")
        x2c_ready = sem("x2c_ready")
        dt_ready = sem("dt_ready")
        zg_ready = sem("zg_ready")
        bt_ready = sem("bt_ready")
        edt_ready = sem("edt_ready")
        edt_held = sem("edt_held")
        soft_ready = sem("soft_ready")
        decay_ready = sem("decay_ready")
        egate_ready = sem("egate_ready")
        egate_held = sem("egate_held")
        lngate_ready = sem("lngate_ready")
        sig_ready = sem("sig_ready")
        states_ready = sem("states_ready")
        y_ready = sem("y_ready")
        mixed_ready = sem("mixed_ready")
        x1c_ready = sem("x1c_ready")
        sq1_ready = sem("sq1_ready")
        var1_ready = sem("var1_ready")
        ln1_ready = sem("ln1_ready")
        rstd1_ready = sem("rstd1_ready")
        x1_ready = sem("x1_ready")
        x1hi_ready = sem("x1hi_ready")
        x1lo_ready = sem("x1lo_ready")
        sq2_ready = sem("sq2_ready")
        var2_ready = sem("var2_ready")
        ln2_ready = sem("ln2_ready")
        rstd2_ready = sem("rstd2_ready")
        x2_ready = sem("x2_ready")
        x2_saved = [sem("x2_saved0"), sem("x2_saved1")]
        logits_ready = sem("logits_ready")
        logits_kept = sem("logits_kept")
        pack_step = sem("pack_step")
        raw12_in = sem("raw12_in")
        packed_out = sem("packed_out")
        blank_ready = sem("blank_ready")
        blanks_out = sem("blanks_out")
        shifted = sem("shifted")
        exp_done = sem("exp_done")
        chosen_ready = sem("chosen_ready")
        counted = sem("counted")
        slots_ready = sem("slots_ready")
        owners_ready = sem("owners_ready")
        xb_in = [sem("xb_in0"), sem("xb_in1")]
        t_ready = sem("t_ready")
        rows_ready = sem("rows_ready")
        based_ready = sem("based_ready")
        xhi_ready = sem("xhi_ready")
        xlo_ready = sem("xlo_ready")
        up_ready = sem("up_ready")
        silu_ready = sem("silu_ready")
        glu_ready = sem("glu_ready")
        sum_ready = sem("sum_ready")
        total_ready = sem("total_ready")
        tails_ready = sem("tails_ready")
        scattered = [sem("scattered0"), sem("scattered1")]
        slot_copied = sem("slot_copied")
        begun = sem("begun")
        wb_in = [sem(f"wb_in{u}") for u in range(DEEP)]
        xr_in = [sem(f"xr_in{u}") for u in range(DEEP)]
        r_t_ready = sem("r_t_ready")
        r_hi_ready = sem("r_hi_ready")
        r_lo_ready = sem("r_lo_ready")
        r_up_ready = sem("r_up_ready")
        r_silu_ready = sem("r_silu_ready")
        r_glu_ready = sem("r_glu_ready")
        r_sum_ready = sem("r_sum_ready")
        r_res_ready = sem("r_res_ready")
        r_weighed = sem("r_weighed")
        returned = [sem(f"returned{u}") for u in range(DEEP)]
        y_in = [sem("y_in0"), sem("y_in1")]
        added = sem("added")
        squared = sem("squared")
        c_ln = sem("c_ln")
        c_rstd = sem("c_rstd")
        scaled = sem("scaled")
        out_done = [sem("out_done0"), sem("out_done1")]

        G, ACC, ZG, BT, DT, MISC = 2, 3, 4, 5, 6, 7

        def bank(n):
            return ps[:, n, :]

        def sub3(ap):
            return ap.rearrange("p (s d) -> p s d", d=P)

        block = ctx.enter_context(nc.Block())

        @block.sync
        def _(sp):
            early = [(w_u[:], a["w_u"]), (from_u[:, 0], a["w_state"]), (from_u[:, 1], a["w_dt"]),
                     (gate_proj[:], a["w_gate"]), (w_c[:], a["w_c"]), (w_out[:], a["w_out"]),
                     (BDT, a["b_dt"].unsqueeze(1)), (DVEC, a["D"].unsqueeze(1)), (ALOG, a["A_log"].unsqueeze(1)),
                     (proj_in[:], a["proj_in"]), (proj_out[:], a["proj_out"].rearrange("p e h d -> p (e h) d")),
                     (router_w[:], a["gate_w"]), (router_b[:], a["gate_b"].unsqueeze(0).to_broadcast([P, NE]))]
            assert len(early) == N_EARLY

            def load_x(i, u):
                sp.dma_start(xin[:, u], xT[:, bass.ds(i * T, T)]).then_inc(x_in[u], 16)

            def load_ctx(i, u):
                for dst, src in ((wraw, w_ctx), (eraw, ens)):
                    for h in range(2):
                        sp.dma_start(dst[h * K:(h + 1) * K, u], src[:, bass.ds(i * T, T)]).then_inc(ctx_in[u], 16)

            load_x(0, 0)
            for dst, src in early:
                sp.dma_start(dst, src).then_inc(early_in, 16)
            load_ctx(0, 0)
            late = [(sw[:, :, 0], a["sw1"]), (sw[:, :, 1], a["sw2"]), (sw3[:], a["sw3"].rearrange("p e h d -> p (e h) d")),
                    (sb12[:, :, 0], a["sb1"]), (sb12[:, :, 1], a["sb2"]),
                    (sb3[:], a["sb3"].unsqueeze(0).to_broadcast([P, NS, D])),
                    (rw3[:], a["w3"].rearrange("p e h d -> p (e h) d")),
                    (rb12[:, :, 0], a["b1"]), (rb12[:, :, 1], a["b2"]),
                    (rb3[:], a["b3"].unsqueeze(0).to_broadcast([P, NE, D]))]
            assert len(late) == N_LATE
            for dst, src in late:
                sp.dma_start(dst, src).then_inc(late_in, 16)
            load_x(1, 1)
            load_ctx(1, 1)
            sp.wait_ge(blank_ready, 1)
            view = sorted_dram.rearrange("(n p) r -> p n r", p=P)
            for n in range(0, NBLK * SUB, 2 * SUB):
                m = min(2 * SUB, NBLK * SUB - n)
                sp.dma_start(view[:, n:n + m], blank[:].unsqueeze(1).to_broadcast([P, m, ROW])).then_inc(blanks_out, 16)

            def save_x2(i, u):
                dst = x2_dram[bass.ds(i, 1)].rearrange("a p t -> (a p) t")
                sp.wait_ge(x2_ready, i + 1)
                sp.dma_start(dst, x2[:, u]).then_inc(x2_saved[u], 16)

            def pack_one(e):
                sp.wait_ge(pack_step, 5 * (e + 1) + 1)
                sp.dma_start(pack_dram[e], pack[:]).then_inc(packed_out, 16)
                if e + 1 < NE:
                    load_raw(e + 1)

            def load_raw(e):
                sp.dma_start(rw12[:, 0], a["w1"][:, e]).then_inc(raw12_in, 16)
                sp.dma_start(rw12[:, 1], a["w2"][:, e]).then_inc(raw12_in, 16)

            load_raw(0)
            for e in range(NE):
                pack_one(e)
            for j in (2,):
                sp.wait_ge(x1c_ready, j - 1)
                load_x(j, 0)
                sp.wait_ge(mask_ready, E * (j - 1))
                load_ctx(j, 0)
            with sp.Fori(0, (NT - 4) // 2) as j:
                for v in range(2):
                    i = j * 2 + (3 + v)
                    u = (3 + v) % 2
                    src = i * T
                    sx = xT[:, bass.ds(src, T)]
                    sp.wait_ge(x1c_ready, i - 1)
                    sp.dma_start(xin[:, u], sx).then_inc(x_in[u], 16)
                    c0, c1 = w_ctx[:, bass.ds(src, T)], ens[:, bass.ds(src, T)]
                    sp.wait_ge(mask_ready, E * (i - 1))
                    for dst, s in ((wraw, c0), (eraw, c1)):
                        for h in range(2):
                            sp.dma_start(dst[h * K:(h + 1) * K, u], s).then_inc(ctx_in[u], 16)
                    save_x2(j * 2 + v, v)
            i = NT - 1
            sp.wait_ge(x1c_ready, i - 1)
            load_x(i, i % 2)
            sp.wait_ge(mask_ready, E * (i - 1))
            load_ctx(i, i % 2)
            for i in range(NT - 4, NT):
                save_x2(i, i % 2)

            for u in range(2):
                sp.wait_ge(x2_saved[u], 16 * (NT // 2))
            for i in range(2):
                sp.dma_start(xb[:, i], x2_dram[i]).then_inc(xb_in[i], 16)
            with sp.Fori(1, NT // 2) as j:
                for u in range(2):
                    i = j * 2 + u
                    src = x2_dram[bass.ds(i, 1)].rearrange("a p t -> (a p) t")
                    sp.wait_ge(t_ready, i - 1)
                    sp.wait_ge(xhi_ready, i - 1)
                    sp.wait_ge(xlo_ready, i - 1)
                    sp.dma_start(xb[:, u], src).then_inc(xb_in[u], 16)

            sp.wait_ge(owners_ready, 1)
            sp.wait_ge(packed_out, 16 * NE)

            def load_weights(j):
                e = sp.value_load(owner_i[0:1, bass.ds(j, 1)], min_val=0, max_val=NE - 1)
                return pack_dram[bass.ds(e, 1)].rearrange("a p r -> (a p) r")

            def block_rows(j):
                return sorted_dram[bass.ds(j * T, T)].rearrange("(s p) r -> p s r", p=P)

            def send_block(j, u, w_src, x_src):
                sp.dma_start(xr[:, u], x_src).then_inc(xr_in[u], 16)
                sp.dma_start(wb[:, u].bitcast(F32), w_src).then_inc(wb_in[u], 16)

            for u in range(2):
                sp.wait_ge(scattered[u], 16 * 2 * SUB * (NT // 2))
            for j in range(DEEP):
                send_block(j, j, load_weights(j), block_rows(j))
            with sp.Fori(1, NBLK // DEEP) as jj:
                for u in range(DEEP):
                    j = jj * DEEP + u
                    w_src, x_src = load_weights(j), block_rows(j)
                    sp.wait_ge(returned[u], jj * (16 * SUB))
                    sp.dma_start(xr[:, u], x_src).then_inc(xr_in[u], 16)
                    sp.dma_start(wb[:, u].bitcast(F32), w_src).then_inc(wb_in[u], 16)
            for j in range(NBLK // DEEP * DEEP, NBLK):
                u = j % DEEP
                w_src = load_weights(j)
                sp.wait_ge(returned[u], 16 * SUB * (NBLK // DEEP))
                send_block(j, u, w_src, block_rows(j))

            for u in range(DEEP):
                sp.wait_ge(returned[u], 16 * SUB * ((NBLK - 1 - u) // DEEP + 1))

            def routed_rows(k, i):
                return routed_dram[bass.ds(i * T + k * TOK, T)].rearrange("(s p) d -> p s d", p=P)

            def out_rows(i):
                return out[bass.ds(i * T, T)].rearrange("(s p) d -> p s d", p=P)

            for i in range(2):
                for k, y in ((0, y1), (1, y2)):
                    sp.dma_start(y[:, i], routed_rows(k, i)).then_inc(y_in[i], 16)
            with sp.Fori(0, NT // 2 - 1) as jj:
                for u in range(2):
                    i = jj * 2 + u
                    s1, s2, dst = routed_rows(0, i + 2), routed_rows(1, i + 2), out_rows(i)
                    sp.wait_ge(added, 2 * i + 2)
                    sp.dma_start(y1[:, u], s1).then_inc(y_in[u], 16)
                    sp.dma_start(y2[:, u], s2).then_inc(y_in[u], 16)
                    sp.wait_ge(scaled, i + 1)
                    sp.dma_start(dst, outb[:, u]).then_inc(out_done[u], 16)
            for i in range(NT - 2, NT):
                sp.wait_ge(scaled, i + 1)
                sp.dma_start(out_rows(i), outb[:, i % 2]).then_inc(out_done[i % 2], 16)
            for u in range(2):
                sp.wait_ge(out_done[u], 16 * (NT // 2))

        @block.gpsimd
        def _(pool):
            nc.gpsimd.iota(above_i[:], pattern=[[1, P]], base=0, channel_multiplier=-1).then_inc(iotas, 1)
            nc.gpsimd.iota(steps_i[:], pattern=[[1, 64]], base=0, channel_multiplier=0).then_inc(iotas, 1)
            nc.gpsimd.iota(prefer_i[:], pattern=[[-1, NE]], base=NE, channel_multiplier=0).then_inc(iotas, 1)
            nc.gpsimd.iota(goes_to[:], pattern=[[P, NROW], [TOK, 2]], base=0, channel_multiplier=1).then_inc(iotas, 1)
            nc.gpsimd.memset(blank[:], 0.0).then_inc(pack_step, 1)
            pool.wait_ge(pack_step, 1)
            nc.gpsimd.iota(blank[:, D:D + 1].bitcast(U32), pattern=[[0, 1]], base=2 * TOK, channel_multiplier=1).then_inc(blank_ready, 1)
            pool.wait_ge(late_ready, 1)
            for e in range(NE):
                raw = rw12[:].rearrange("p a h -> p (a h)")
                hi, lo = pack[:, 0:2 * H], pack[:, 2 * H:4 * H]
                n = 5 * e + 1
                pool.wait_ge(raw12_in, 32 * (e + 1))
                if e:
                    pool.wait_ge(packed_out, 16 * e)
                nc.gpsimd.tensor_copy(hi.bitcast(F32R), raw).then_inc(pack_step, 1)
                pool.wait_ge(pack_step, n + 1)
                nc.gpsimd.tensor_tensor(lo.bitcast(F32R), raw, hi, ALU.subtract).then_inc(pack_step, 1)
                nc.gpsimd.tensor_copy(pack[:, W3AT:B1AT], rw3[:, e * HALF:(e + 1) * HALF].rearrange("p h d -> p (h d)")).then_inc(pack_step, 1)
                nc.gpsimd.tensor_copy(pack[:, B1AT:B3AT], rb12[:, e].rearrange("p a h -> p (a h)")).then_inc(pack_step, 1)
                nc.gpsimd.tensor_copy(pack[:, B3AT:PACK], rb3[:, e]).then_inc(pack_step, 1)

            pool.wait_ge(tails_ready, 1)
            pool.wait_ge(blanks_out, 16 * N_BLANK)
            most = pool.to_reg(NBLK * T - 1)

            def scatter_tile(i, u, wait_free):
                now = slot[:, bass.ds(i * SUB, SUB), :]
                to = goes_to[:, bass.ds(i * SUB, SUB), :]
                wt = weight[:, bass.ds(i * SUB, SUB), :]
                if wait_free is not None:
                    pool.wait_ge(scattered[u], wait_free)
                nc.gpsimd.tensor_tensor(rows[:, u, :, :, D + 1], wt, ones_f[:, 0:2 * SUB].rearrange("p (s k) -> p s k", k=2), ALU.mult).then_inc(slot_copied, 1)
                nc.gpsimd.tensor_copy(rows[:, u, :, :, D].bitcast(U32), to).then_inc(slot_copied, 1)
                nc.gpsimd.tensor_copy(slot_now[:, u].rearrange("p (s k) -> p s k", k=2), now).then_inc(slot_copied, 1)
                pool.wait_ge(slot_copied, 3 * i + 3)
                pool.wait_ge(rows_ready, 2 * i + 2)
                pool.sem_inc(begun, 1)
                for s in range(SUB):
                    for k in range(2):
                        c = 2 * s + k
                        nc.gpsimd.indirect_dma_start(
                            out=sorted_dram, out_offset=bass.IndirectOffsetOnAxis(ap=slot_now[:, u, c:c + 1], axis=0),
                            in_=rows[:, u, s, k], in_offset=None, bounds_check=most, oob_is_err=False).then_inc(scattered[u], 16)

            scatter_tile(0, 0, None)
            scatter_tile(1, 1, None)
            with pool.Fori(1, NT // 2) as jj:
                for u in range(2):
                    scatter_tile(jj * 2 + u, u, jj * (16 * 2 * SUB))

            last = pool.to_reg(2 * TOK - 1)

            def return_block(j, u):
                pool.wait_ge(r_weighed, j + 1)
                pool.sem_inc(begun, 1)
                for s in range(SUB):
                    nc.gpsimd.indirect_dma_start(
                        out=routed_dram, out_offset=bass.IndirectOffsetOnAxis(ap=xr[:, u, s, D:D + 1].bitcast(U32), axis=0),
                        in_=weighed[:, u % 2, s], in_offset=None, bounds_check=last, oob_is_err=False).then_inc(returned[u], 16)

            with pool.Fori(0, NBLK // DEEP) as jj:
                for u in range(DEEP):
                    return_block(jj * DEEP + u, u)
            for j in range(NBLK // DEEP * DEEP, NBLK):
                return_block(j, j % DEEP)

        @block.scalar
        def _(act):
            act.wait_ge(vec_exp, 1)
            nc.scalar.activation(TMP2, TMP, ACT.Exp).then_inc(vec_ln, 1)
            act.wait_ge(vec_ln, 1)
            nc.scalar.activation(TMP3, TMP2, ACT.Ln, bias=1.0).then_inc(vec_ln, 1)
            act.wait_ge(vec_exp, 2)
            nc.scalar.activation(FLOOR, RATE, ACT.Exp, scale=DT_MAX).then_inc(vec_ln, 1)
            act.wait_ge(consts, 1)

            def mix_exps(n):
                act.wait_ge(dt_ready, n + 1)
                nc.scalar.activation(e_dt[:], bank(DT), ACT.Exp, bias=BDT).then_inc(edt_ready, 1)
                act.wait_ge(zg_ready, n + 1)
                nc.scalar.activation(e_gate[:], bank(ZG), ACT.Exp, scale=-1.0).then_inc(egate_ready, 1)

            def mix_decay(n):
                act.wait_ge(edt_held, n + 1)
                nc.scalar.activation(e_dt[:], e_dt[:], ACT.Ln, bias=1.0).then_inc(soft_ready, 1)
                act.wait_ge(egate_held, n + 1)
                nc.scalar.activation(e_gate[:], e_gate[:], ACT.Ln, bias=1.0).then_inc(lngate_ready, 1)
                act.wait_ge(soft_ready, n + 1)
                nc.scalar.activation(decay[:], e_dt[:], ACT.Exp, scale=RATE).then_inc(decay_ready, 1)
                act.wait_ge(lngate_ready, n + 1)
                nc.scalar.activation(sgate[:], e_gate[:], ACT.Exp, scale=-1.0).then_inc(sig_ready, 1)

            def norm1_square(n):
                act.wait_ge(x1c_ready, n + 1)
                nc.scalar.activation(square[:], bank(BT), ACT.Square).then_inc(sq1_ready, 1)

            def norm1_rstd(n):
                act.wait_ge(var1_ready, n + 1)
                nc.scalar.activation(logv[:], bank(MISC), ACT.Ln, bias=EPSC).then_inc(ln1_ready, 1)
                act.wait_ge(ln1_ready, n + 1)
                nc.scalar.activation(rstd1[:], logv[:], ACT.Exp, scale=-0.5).then_inc(rstd1_ready, 1)

            def x1_high(n, u):
                act.wait_ge(x1_ready, n + 1)
                nc.scalar.activation(x1_hi[:, u], x1[:, u], ACT.Identity).then_inc(x1hi_ready, 1)

            def gate_copy(i, e):
                if e >= 2 or not isinstance(i, int) or i > 0:
                    act.wait_ge(hid_ready, 16 * i + 2 * (e - 2) + 2)
                act.wait_ge(gate_ready, E * i + e + 1)
                nc.scalar.activation(gsb[:, e % 2], bank(G), ACT.Identity).then_inc(gsb_ready, 1)

            def norm2_square(i):
                act.wait_ge(x2c_ready, i + 1)
                nc.scalar.activation(square[:], x2c[:], ACT.Square).then_inc(sq2_ready, 1)

            def norm2_rstd(i):
                act.wait_ge(var2_ready, i + 1)
                nc.scalar.activation(logv[:], bank(MISC), ACT.Ln, bias=EPSC).then_inc(ln2_ready, 1)
                act.wait_ge(ln2_ready, i + 1)
                nc.scalar.activation(rstd2[:], logv[:], ACT.Exp, scale=-0.5).then_inc(rstd2_ready, 1)

            def body(i, u, mix, tail_of):
                for e in range(E):
                    gate_copy(i, e)
                    if e == 0 and mix:
                        mix_exps(i + 1)
                    if e == 1:
                        if mix:
                            mix_decay(i + 1)
                    if e == 2 and tail_of:
                        norm2_square(i - 1)
                    if e == 3 and tail_of:
                        norm2_rstd(i - 1)
                    if e == 5 and mix:
                        norm1_square(i + 1)
                    if e == 6 and mix:
                        norm1_rstd(i + 1)
                    if e == 7 and mix:
                        x1_high(i + 1, 1 - u)

            mix_exps(0)
            mix_decay(0)
            norm1_square(0)
            norm1_rstd(0)
            x1_high(0, 0)
            body(0, 0, True, False)
            with act.Fori(0, (NT - 2) // 2) as j:
                body(j * 2 + 1, 1, True, True)
                body(j * 2 + 2, 0, True, True)
            body(NT - 1, 1, False, True)
            norm2_square(NT - 1)
            norm2_rstd(NT - 1)

            act.wait_ge(shifted, 1)
            nc.scalar.activation(score[:], score[:], ACT.Exp).then_inc(exp_done, 1)

            def shared_silu(i, s, h):
                n = 4 * i + 2 * s + h
                b = 2 * ((2 * s + h) % 3)
                if not isinstance(i, int) or n >= 2:
                    act.wait_ge(glu_ready, n - 1)
                act.wait_ge(up_ready, n + 1)
                nc.scalar.activation(silu[:, h], bank(b), ACT.Silu, bias=sb12[:, s, 0, h:h + 1]).then_inc(silu_ready, 1)

            def shared_tile(i, u, free):
                if free is not None:
                    act.wait_ge(scattered[u], free)
                act.wait_ge(t_ready, i + 1)
                for k in range(2):
                    nc.scalar.activation(rows[:, u, :, k, 0:D], sub3(bank(6)), ACT.Identity).then_inc(rows_ready, 1)
                act.wait_ge(xb_in[u], (i - u) * 8 + 16)
                nc.scalar.activation(xs_hi[:, u], xb[:, u], ACT.Identity).then_inc(xhi_ready, 1)
                for s in range(NS):
                    for h in range(HALF):
                        shared_silu(i, s, h)

            shared_tile(0, 0, None)
            shared_tile(1, 1, None)
            with act.Fori(1, NT // 2) as jj:
                for u in range(2):
                    shared_tile(jj * 2 + u, u, jj * (16 * 2 * SUB))

            def block_high(j, u):
                act.wait_ge(r_t_ready, j + 1)
                nc.scalar.activation(xs_hi[:, u % 2], bank(6), ACT.Identity).then_inc(r_hi_ready, 1)

            def block_weigh(j, u, free):
                if free is not None:
                    act.wait_ge(returned[(u - 2) % DEEP], free)
                act.wait_ge(r_res_ready, j + 1)
                for s in range(SUB):
                    ins = nc.scalar.activation(weighed[:, u % 2, s], res[:, s * P:(s + 1) * P], ACT.Identity, scale=xr[:, u, s, D + 1:D + 2])
                ins.then_inc(r_weighed, 1)

            def block_silu(j, u, h):
                if not isinstance(j, int) or j > 0:
                    act.wait_ge(r_glu_ready, 2 * j + h - 1)
                act.wait_ge(r_up_ready, 2 * j + h + 1)
                nc.scalar.activation(silu[:, h], bank(2 * h), ACT.Silu, bias=wb[:, u, B1AT + h:B1AT + h + 1].bitcast(F32)).then_inc(r_silu_ready, 1)

            def routed(j, u, nxt, prev, free):
                block_silu(j, u, 0)
                if nxt:
                    block_high(j + 1, (u + 1) % DEEP)
                if prev:
                    block_weigh(j - 1, (u - 1) % DEEP, free)
                block_silu(j, u, 1)

            block_high(0, 0)
            routed(0, 0, True, False, None)
            routed(1, 1, True, True, None)
            routed(2, 2, True, True, None)
            routed(3, 3, True, True, 16 * SUB)
            with act.Fori(1, NBLK // DEEP) as jj:
                for u in range(DEEP):
                    routed(jj * DEEP + u, u, True, True, jj * (16 * SUB) + (16 * SUB if u == 3 else 0))
            for j in range(NBLK // DEEP * DEEP, NBLK):
                routed(j, j % DEEP, j + 1 < NBLK, True, 16 * SUB * ((j - 3) // DEEP + 1))
            block_weigh(NBLK - 1, (NBLK - 1) % DEEP, 16 * SUB * ((NBLK - 3) // DEEP + 1))

            def c_tile(i, u):
                act.wait_ge(added, 2 * i + 2)
                for s in range(SUB):
                    ins = nc.scalar.activation(sqc[:, s], total[:, bass.ds(i * SUB + s, 1), :].rearrange("p a d -> p (a d)"), ACT.Square, accum_out=ssq[:, u, s:s + 1])
                ins.then_inc(squared, 1)
                act.wait_ge(squared, i + 1)
                nc.scalar.activation(ssq[:, 2, :], ssq[:, u, :], ACT.Ln, bias=EPSC, scale=1.0 / D).then_inc(c_ln, 1)
                act.wait_ge(c_ln, i + 1)
                nc.scalar.activation(ssq[:, u, :], ssq[:, 2, :], ACT.Exp, scale=-0.5).then_inc(c_rstd, 1)

            with act.Fori(0, NT // 2) as jj:
                for u in range(2):
                    c_tile(jj * 2 + u, u)

        @block.vector
        def _(dve):
            v = nc.vector
            steps_done = [0]

            def link(ins):
                steps_done[0] += 1
                ins.then_inc(s_dve, 1)
                dve.wait_ge(s_dve, steps_done[0])

            link(v.memset(ones_f[:], 1.0))
            link(v.memset(mean_mat[:], 1.0 / D))
            link(v.tensor_scalar(ones_r[:], mean_mat[:], float(D), None, ALU.mult))
            link(v.memset(ones_b[:], 1.0))
            link(v.memset(EPSC, EPS))
            dve.wait_ge(iotas, 4)
            link(v.tensor_scalar(ident[:], above_i[:], 0.0, None, ALU.is_equal))
            link(v.tensor_scalar(before[:], above_i[:], 0.0, None, ALU.is_gt))
            link(v.tensor_copy(steps[:], steps_i[:]))
            link(v.tensor_copy(prefer[:], prefer_i[:]))
            dve.wait_ge(early_in, 16 * N_EARLY)
            link(v.tensor_scalar(TMP2, ALOG, -1.0, None, ALU.mult))
            v.tensor_tensor(TMP, ALOG, TMP2, ALU.min).then_inc(vec_exp, 1)
            link(v.scalar_tensor_tensor(out=w_skip[:], in0=w_out[:], scalar=DVEC, in1=ident[:], op0=ALU.mult, op1=ALU.add))

            def center(w, n, scale=1.0):
                m = means[:, 0:n]
                link(v.tensor_reduce(m, w, axis=AX.X, op=ALU.add))
                link(v.tensor_scalar(m, m, 1.0 / D, None, ALU.mult))
                link(v.tensor_tensor(w, w, m.unsqueeze(2).to_broadcast([P, n, D]), ALU.subtract))
                if scale != 1.0:
                    link(v.tensor_scalar(w, w, scale, None, ALU.mult))

            center(w_skip[:].unsqueeze(1), 1)
            center(w_out[:].unsqueeze(1), 1)
            dve.wait_ge(vec_ln, 2)
            link(v.scalar_tensor_tensor(out=RATE, in0=ALOG, scalar=0.0, in1=TMP3, op0=ALU.max, op1=ALU.add))
            link(v.tensor_scalar(RATE, RATE, -1.0, -RATE_EPS, ALU.mult, ALU.add))
            v.memset(TMP3, 0.0).then_inc(vec_exp, 1)
            dve.wait_ge(composed, 1)
            v.tensor_copy(state_dt[:], ps[:, 0, 0:2 * D].rearrange("p (a d) -> p a d", d=D)).then_inc(consts, 1)
            link(v.tensor_copy(proj_in_hi[:], proj_in[:]))
            link(v.tensor_tensor(proj_in_lo[:], proj_in[:], proj_in_hi[:].bitcast(F32), ALU.subtract))
            center(proj_out[:], E * HALF)
            v.memset(TMP2, 0.0).then_inc(weights_ready, 1)
            dve.wait_ge(vec_ln, 3)

            def mix_hold(n):
                dve.wait_ge(edt_ready, n + 1)
                v.tensor_scalar(e_dt[:], e_dt[:], 2.0 ** 30, None, ALU.min).then_inc(edt_held, 1)
                dve.wait_ge(egate_ready, n + 1)
                v.tensor_scalar(e_gate[:], e_gate[:], 2.0 ** 62, None, ALU.min).then_inc(egate_held, 1)

            def mix_drive(n, c):
                dve.wait_ge(decay_ready, n + 1)
                v.tensor_scalar(decay[:], decay[:], FLOOR, 1.0, ALU.max, ALU.min).then_inc(s_dve, 1)
                dve.wait_ge(s_dve, c + 1)
                dve.wait_ge(bt_ready, n + 1)
                v.scalar_tensor_tensor(out=drive[:], in0=decay[:], scalar=1.0, in1=bank(BT), op0=ALU.subtract, op1=ALU.mult).then_inc(s_dve, 1)
                dve.wait_ge(s_dve, c + 2)
                v.memset(decay[:].rearrange("p (b s) -> p b s", s=SEQ)[:, :, 0:1], 0.0).then_inc(s_dve, 1)
                dve.wait_ge(sig_ready, n + 1)
                v.tensor_tensor(sgate[:], sgate[:], bank(ZG), ALU.mult).then_inc(s_dve, 1)
                dve.wait_ge(s_dve, c + 4)

            def mix_scan(n):
                v.tensor_tensor_scan(out=states[:], data0=decay[:], data1=drive[:], initial=0.0,
                                     op0=ALU.mult, op1=ALU.subtract).then_inc(states_ready, 1)

            def mix_gate(n):
                dve.wait_ge(y_ready, n + 1)
                v.tensor_tensor(mixed[:], sgate[:], bank(DT), ALU.mult).then_inc(mixed_ready, 1)

            def norm1(n, u):
                dve.wait_ge(rstd1_ready, n + 1)
                v.tensor_tensor(x1[:, u], rstd1[:], bank(BT), ALU.mult).then_inc(x1_ready, 1)

            def x1_low(n, u):
                dve.wait_ge(x1hi_ready, n + 1)
                v.tensor_tensor(x1_lo[:, u], x1[:, u], x1_hi[:, u].bitcast(F32), ALU.subtract).then_inc(x1lo_ready, 1)

            def mask(i, e, u):
                if not isinstance(i, int) or E * i + e >= 2:
                    dve.wait_ge(gate_ready, E * i + e - 1)
                v.scalar_tensor_tensor(out=masked[:, e % 2], in0=eraw[:, u], scalar=float(e), in1=wparts[:].bitcast(F32),
                                       op0=ALU.is_equal, op1=ALU.mult).then_inc(mask_ready, 1)

            def context(i, u, c):
                dve.wait_ge(ctx_in[u], (i - u) * 32 + 64)
                v.tensor_copy(wparts[:], wraw[:, u]).then_inc(s_dve, 1)
                dve.wait_ge(s_dve, c + 1)
                v.tensor_tensor(wparts[K:2 * K], wraw[K:2 * K, u], wparts[K:2 * K].bitcast(F32), ALU.subtract).then_inc(s_dve, 1)
                dve.wait_ge(s_dve, c + 2)

            def expert(i, e):
                for h in range(HALF):
                    dve.wait_ge(h_ready, 16 * i + 2 * e + h + 1)
                    if h == 0:
                        dve.wait_ge(gsb_ready, E * i + e + 1)
                        if e >= 2 or not isinstance(i, int) or i > 0:
                            dve.wait_ge(down_done, E * i + e - 1)
                    v.scalar_tensor_tensor(out=hid[:, e % 2, h], in0=bank(h), scalar=0.0, in1=gsb[:, e % 2],
                                           op0=ALU.max, op1=ALU.mult).then_inc(hid_ready, 1)

            def residual2(i, u):
                dve.wait_ge(down_done, E * i + E)
                v.tensor_tensor(x2c[:], x1[:, u], bank(ACC), ALU.add).then_inc(x2c_ready, 1)

            def norm2(i, u, free):
                dve.wait_ge(rstd2_ready, i + 1)
                if free is not None:
                    dve.wait_ge(x2_saved[u], free)
                v.tensor_tensor(x2[:, u], x2c[:], rstd2[:], ALU.mult).then_inc(x2_ready, 1)

            def logits(i):
                dve.wait_ge(logits_ready, i + 1)
                v.tensor_tensor(score[:, bass.ds(i * SUB, SUB), :], bank(ZG)[:, 0:SUB * NE].rearrange("p (s e) -> p s e", e=NE),
                                router_b[:].unsqueeze(1).to_broadcast([P, SUB, NE]), ALU.add).then_inc(logits_kept, 1)

            STEPS = 6

            def body(i, u, mix, tail_of, free, c):
                for e in range(E):
                    expert(i, e)
                    if e < E - 1:
                        mask(i, e + 1, u)
                    if e == 0 and mix:
                        mix_hold(i + 1)
                    if e == 0 and tail_of:
                        residual2(i - 1, 1 - u)
                    if e == 1 and mix:
                        mix_drive(i + 1, c)
                    if e == 2 and mix:
                        mix_scan(i + 1)
                    if e == 3 and mix:
                        mix_gate(i + 1)
                    if e == 4 and tail_of:
                        norm2(i - 1, 1 - u, free)
                    if e == 6:
                        if mix:
                            norm1(i + 1, 1 - u)
                        if tail_of:
                            logits(i - 1)
                    if e == 7 and mix:
                        context(i + 1, 1 - u, c + 4)
                        mask(i + 1, 0, 1 - u)
                        x1_low(i + 1, 1 - u)

            c0 = steps_done[0]
            mix_hold(0)
            mix_drive(0, c0)
            mix_scan(0)
            mix_gate(0)
            norm1(0, 0)
            context(0, 0, c0 + 4)
            mask(0, 0, 0)
            x1_low(0, 0)
            steps_done[0] += STEPS
            dve.wait_ge(late_in, 16 * N_LATE)
            center(rw3[:], NE * HALF)
            center(rb3[:], NE)
            v.memset(TMP, 0.0).then_inc(late_ready, 1)
            body(0, 0, True, False, None, steps_done[0])
            steps_done[0] += STEPS
            c1 = steps_done[0]
            body(1, 1, True, True, None, c1)
            body(2, 0, True, True, None, c1 + STEPS)
            with dve.Fori(1, (NT - 2) // 2) as j:
                body(j * 2 + 1, 1, True, True, j * 16, j * (2 * STEPS) + c1)
                body(j * 2 + 2, 0, True, True, j * 16, j * (2 * STEPS) + (c1 + STEPS))
            steps_done[0] += STEPS * (NT - 2)
            body(NT - 1, 1, False, True, 16 * (NT // 2 - 1), None)
            residual2(NT - 1, 1)
            norm2(NT - 1, 1, 16 * (NT // 2 - 1))
            logits(NT - 1)
            dve.wait_ge(logits_kept, NT)

            def over_e(ap):
                return ap.unsqueeze(2).to_broadcast([P, NROW, NE])

            MX, W1, W2, SUMS = (best[:, n] for n in range(4))
            each = prefer[:].unsqueeze(1).to_broadcast([P, NROW, NE])
            link(v.tensor_reduce(MX, score[:], axis=AX.X, op=ALU.max))
            v.tensor_tensor(score[:], score[:], over_e(MX), ALU.subtract).then_inc(shifted, 1)
            link(v.tensor_copy(sw_hi[:], sw[:]))
            link(v.tensor_tensor(sw_lo[:], sw[:], sw_hi[:].bitcast(F32), ALU.subtract))
            center(sw3[:], NS * HALF, 1.0 / NS)
            center(sb3[:], NS, 1.0 / NS)
            link(v.tensor_tensor(sb3[:, 0], sb3[:, 0], sb3[:, 1], ALU.add))
            dve.wait_ge(exp_done, 1)
            link(v.tensor_reduce(SUMS, score[:], axis=AX.X, op=ALU.add))
            link(v.reciprocal(MX, SUMS))
            link(v.tensor_tensor(score[:], score[:], over_e(MX), ALU.mult))
            for w, hot in ((W1, first), (W2, second)):
                link(v.tensor_reduce(w, score[:], axis=AX.X, op=ALU.max))
                link(v.tensor_tensor(work[:], score[:], over_e(w), ALU.is_equal))
                link(v.tensor_tensor(work[:], work[:], each, ALU.mult))
                link(v.tensor_reduce(MX, work[:], axis=AX.X, op=ALU.max))
                link(v.tensor_tensor(hot[:], work[:], over_e(MX), ALU.is_equal))
                if hot is first:
                    link(v.scalar_tensor_tensor(out=score[:].rearrange("p n e -> p (n e)"), in0=hot[:].rearrange("p n e -> p (n e)"), scalar=-2.0,
                                                in1=score[:].rearrange("p n e -> p (n e)"), op0=ALU.mult, op1=ALU.add))
            v.tensor_tensor(chosen[:], first[:], second[:], ALU.add).then_inc(chosen_ready, 1)
            dve.wait_ge(counted, 1)
            link(v.tensor_copy(work[:].rearrange("p n e -> p (n e)"), bank(1)))
            for e in range(NE):
                link(v.tensor_tensor_scan(out=upto[:, :, e], data0=ones_f[:], data1=work[:, :, e], initial=0.0,
                                          op0=ALU.mult, op1=ALU.add))
            link(v.tensor_copy(blocks[:, 0], upto[:, NROW - 1, :]))
            link(v.tensor_scalar(blocks[:, 0], blocks[:, 0], 1.0 / T, None, ALU.mult))
            link(v.tensor_tensor(over[:], blocks[:, 0].unsqueeze(2).to_broadcast([P, NE, 16]),
                                 steps[:, 0:16].unsqueeze(1).to_broadcast([P, NE, 16]), ALU.is_gt))
            link(v.tensor_reduce(blocks[:, 1], over[:], axis=AX.X, op=ALU.add))
            link(v.tensor_tensor_scan(out=blocks[:, 2], data0=ones_f[:, 0:NE], data1=blocks[:, 1], initial=0.0, op0=ALU.mult, op1=ALU.add))
            link(v.tensor_tensor(blocks[:, 3], blocks[:, 2], blocks[:, 1], ALU.subtract))
            link(v.tensor_scalar(blocks[:, 3], blocks[:, 3], float(T), None, ALU.mult))
            link(v.tensor_tensor(owner[:], blocks[:, 2].unsqueeze(1).to_broadcast([P, 40, NE]),
                                 steps[:, 0:40].unsqueeze(2).to_broadcast([P, 40, NE]), ALU.is_le))
            link(v.tensor_reduce(owner_f[:], owner[:], axis=AX.X, op=ALU.add))
            link(v.tensor_scalar(owner_f[:], owner_f[:], float(NE - 1), None, ALU.min))
            v.tensor_copy(owner_i[:], owner_f[:]).then_inc(owners_ready, 1)
            link(v.tensor_tensor(upto[:], upto[:], work[:], ALU.subtract))
            link(v.tensor_tensor(upto[:], upto[:], blocks[:, 3].unsqueeze(1).to_broadcast([P, NROW, NE]), ALU.add))
            link(v.tensor_tensor(upto[:].rearrange("p n e -> p (n e)"), upto[:].rearrange("p n e -> p (n e)"), bank(0), ALU.add))
            for k, hot in enumerate((first, second)):
                link(v.tensor_tensor(work[:], upto[:], hot[:], ALU.mult))
                link(v.tensor_reduce(slot_f[:, :, k], work[:], axis=AX.X, op=ALU.add))
            link(v.tensor_copy(slot[:], slot_f[:]))
            link(v.tensor_copy(weight[:, :, 0], W1))
            v.tensor_copy(weight[:, :, 1], W2).then_inc(tails_ready, 1)

            def shared_sum(i):
                dve.wait_ge(sum_ready, i + 1)
                v.tensor_tensor(total[:, bass.ds(i * SUB, SUB), :], sub3(based[:]), sub3(bank(7)), ALU.add).then_inc(total_ready, 1)

            def shared_based(i):
                dve.wait_ge(t_ready, i + 1)
                v.tensor_tensor(sub3(based[:]), sub3(bank(6)), sb3[:, 0].unsqueeze(1).to_broadcast([P, SUB, D]), ALU.add).then_inc(based_ready, 1)

            def shared_tile(i, u, prev):
                dve.wait_ge(xhi_ready, i + 1)
                v.tensor_tensor(xs_lo[:, u], xb[:, u], xs_hi[:, u].bitcast(F32), ALU.subtract).then_inc(xlo_ready, 1)
                for n in range(NS * HALF):
                    s, h = n // HALF, n % HALF
                    dve.wait_ge(silu_ready, 4 * i + n + 1)
                    v.scalar_tensor_tensor(out=glu[:, u, n], in0=bank(2 * (n % 3) + 1), scalar=sb12[:, s, 1, h:h + 1], in1=silu[:, h],
                                           op0=ALU.add, op1=ALU.mult).then_inc(glu_ready, 1)
                    if n == 1:
                        if prev:
                            shared_sum(i - 1)
                            dve.wait_ge(total_ready, i)
                        shared_based(i)

            shared_tile(0, 0, False)
            shared_tile(1, 1, True)
            with dve.Fori(1, NT // 2) as jj:
                for u in range(2):
                    shared_tile(jj * 2 + u, u, True)
            dve.wait_ge(based_ready, NT)
            shared_sum(NT - 1)

            def block_low(j, u):
                dve.wait_ge(r_hi_ready, j + 1)
                v.tensor_tensor(xs_lo[:, u % 2], bank(6), xs_hi[:, u % 2].bitcast(F32), ALU.subtract).then_inc(r_lo_ready, 1)

            def block_glu(j, u, h):
                dve.wait_ge(r_silu_ready, 2 * j + h + 1)
                v.scalar_tensor_tensor(out=glu[:, u % 2, h], in0=bank(2 * h + 1), scalar=wb[:, u, B2AT + h:B2AT + h + 1].bitcast(F32), in1=silu[:, h],
                                       op0=ALU.add, op1=ALU.mult).then_inc(r_glu_ready, 1)

            def block_bias(j, u):
                if not isinstance(j, int) or j > 0:
                    dve.wait_ge(r_weighed, j)
                dve.wait_ge(r_sum_ready, j + 1)
                v.tensor_tensor(sub3(res[:]), sub3(bank(7)), wb[:, u, B3AT:PACK].bitcast(F32).unsqueeze(1).to_broadcast([P, SUB, D]),
                                ALU.add).then_inc(r_res_ready, 1)

            def routed(j, u, nxt, prev):
                block_glu(j, u, 0)
                if nxt:
                    block_low(j + 1, (u + 1) % DEEP)
                if prev:
                    block_bias(j - 1, (u - 1) % DEEP)
                block_glu(j, u, 1)

            block_low(0, 0)
            for j in range(DEEP):
                routed(j, j, True, j > 0)
            with dve.Fori(1, NBLK // DEEP) as jj:
                for u in range(DEEP):
                    routed(jj * DEEP + u, u, True, True)
            for j in range(NBLK // DEEP * DEEP, NBLK):
                routed(j, j % DEEP, j + 1 < NBLK, True)
            block_bias(NBLK - 1, (NBLK - 1) % DEEP)

            def c_add(i, u):
                mine = total[:, bass.ds(i * SUB, SUB), :]
                dve.wait_ge(y_in[u], (i - u) * 16 + 32)
                v.tensor_tensor(mine, mine, y1[:, u], ALU.add).then_inc(added, 1)
                dve.wait_ge(added, 2 * i + 1)
                v.tensor_tensor(mine, mine, y2[:, u], ALU.add).then_inc(added, 1)

            def c_scale(i, u, free):
                if free is not None:
                    dve.wait_ge(out_done[u], free)
                dve.wait_ge(c_rstd, i + 1)
                v.tensor_tensor(outb[:, u], total[:, bass.ds(i * SUB, SUB), :],
                                ssq[:, u, :].unsqueeze(2).to_broadcast([P, SUB, D]), ALU.mult).then_inc(scaled, 1)

            c_add(0, 0)
            c_add(1, 1)
            c_scale(0, 0, None)
            c_add(2, 0)
            c_scale(1, 1, None)
            with dve.Fori(1, NT // 2 - 1) as jj:
                c_add(jj * 2 + 1, 1)
                c_scale(jj * 2, 0, jj * 16)
                c_add(jj * 2 + 2, 0)
                c_scale(jj * 2 + 1, 1, jj * 16)
            c_add(NT - 1, 1)
            c_scale(NT - 2, 0, 16 * (NT // 2 - 1))
            c_scale(NT - 1, 1, 16 * (NT // 2 - 1))

        @block.tensor
        def _(pe):
            def mm(o, w, x, start=True, stop=True):
                return nc.tensor.matmul(o, w, x, start=start, stop=stop)

            def split_mm(o, w_hi, w_lo, x_hi, x_lo):
                mm(o, w_hi, x_hi, True, False)
                mm(o, w_lo, x_hi, False, False)
                return mm(o, w_hi, x_lo, False, True)

            pe.wait_ge(early_in, 16 * N_EARLY)
            mm(ps[:, 0, 0:D], w_u[:], from_u[:, 0])
            mm(ps[:, 0, D:2 * D], w_u[:], from_u[:, 1]).then_inc(composed, 1)
            pe.wait_ge(consts, 1)

            def mix_in(n, u):
                pe.wait_ge(x_in[u], (n - u) * 8 + 16)
                mm(bank(DT), state_dt[:, 1], xin[:, u]).then_inc(dt_ready, 1)
                mm(bank(ZG), gate_proj[:], xin[:, u]).then_inc(zg_ready, 1)
                mm(bank(BT), state_dt[:, 0], xin[:, u]).then_inc(bt_ready, 1)

            def mix_y(n):
                pe.wait_ge(states_ready, n + 1)
                mm(bank(DT), w_c[:], states[:]).then_inc(y_ready, 1)

            def mix_out(n, u):
                mm(bank(BT), w_skip[:], xin[:, u], True, False)
                pe.wait_ge(mixed_ready, n + 1)
                mm(bank(BT), w_out[:], mixed[:], False, True).then_inc(x1c_ready, 1)

            def var1(n):
                pe.wait_ge(sq1_ready, n + 1)
                mm(bank(MISC), mean_mat[:], square[:]).then_inc(var1_ready, 1)

            def var2(i):
                pe.wait_ge(sq2_ready, i + 1)
                mm(bank(MISC), mean_mat[:], square[:]).then_inc(var2_ready, 1)

            def up(i, e, u):
                pe.wait_ge(mask_ready, E * i + e + 1)
                if not isinstance(i, int) or E * i + e > 0:
                    pe.wait_ge(gsb_ready, E * i + e)
                mm(bank(G), ones_r[:], masked[:, e % 2]).then_inc(gate_ready, 1)
                if e == 0:
                    pe.wait_ge(x1hi_ready, i + 1)
                    pe.wait_ge(x1lo_ready, i + 1)
                for h in range(HALF):
                    if not isinstance(i, int) or E * i + e > 0:
                        pe.wait_ge(hid_ready, 16 * i + 2 * e + h - 1)
                    c = slice(h * P, (h + 1) * P)
                    split_mm(bank(h), proj_in_hi[:, e, c], proj_in_lo[:, e, c], x1_hi[:, u], x1_lo[:, u]).then_inc(h_ready, 1)

            def down(i, e):
                if e == 0 and (not isinstance(i, int) or i > 0):
                    pe.wait_ge(x2c_ready, i)
                for h in range(HALF):
                    pe.wait_ge(hid_ready, 16 * i + 2 * e + h + 1)
                    last = mm(bank(ACC), proj_out[:, e * HALF + h], hid[:, e % 2, h], e + h == 0, e * HALF + h == E * HALF - 1)
                last.then_inc(down_done, 1)

            def logit(i, u):
                pe.wait_ge(x2_ready, i + 1)
                for s in range(SUB):
                    last = mm(bank(ZG)[:, s * NE:(s + 1) * NE], x2[:, u, s * P:(s + 1) * P], router_w[:])
                last.then_inc(logits_ready, 1)

            def body(i, u, mix, tail_of):
                for e in range(E):
                    up(i, e, u)
                    if e == 0:
                        if tail_of:
                            down(i - 1, E - 1)
                        if mix:
                            if tail_of and (not isinstance(i, int) or i > 1):
                                pe.wait_ge(logits_kept, i - 1)
                            mix_in(i + 1, 1 - u)
                    else:
                        down(i, e - 1)
                    if e == 3:
                        if mix:
                            mix_y(i + 1)
                        if tail_of:
                            var2(i - 1)
                    if e == 4 and mix:
                        mix_out(i + 1, 1 - u)
                    if e == 5:
                        if mix:
                            if tail_of:
                                pe.wait_ge(ln2_ready, i)
                            var1(i + 1)
                        if tail_of:
                            logit(i - 1, 1 - u)

            mix_in(0, 0)
            mix_y(0)
            mix_out(0, 0)
            var1(0)
            pe.wait_ge(weights_ready, 1)
            body(0, 0, True, False)
            body(1, 1, True, True)
            body(2, 0, True, True)
            with pe.Fori(1, (NT - 2) // 2) as j:
                body(j * 2 + 1, 1, True, True)
                body(j * 2 + 2, 0, True, True)
            body(NT - 1, 1, False, True)
            down(NT - 1, E - 1)
            var2(NT - 1)
            pe.wait_ge(logits_kept, NT - 1)
            logit(NT - 1, 1)

            pe.wait_ge(chosen_ready, 1)
            flat = chosen[:].rearrange("p n e -> p (n e)")
            mm(bank(0), before[:], flat)
            mm(bank(1), ones_b[:], flat).then_inc(counted, 1)
            pe.wait_ge(tails_ready, 1)

            def transpose_tile(i, u):
                pe.wait_ge(xb_in[u], (i - u) * 8 + 16)
                if not isinstance(i, int) or i > 0:
                    pe.wait_ge(rows_ready, 2 * i)
                    pe.wait_ge(based_ready, i)
                for s in range(SUB):
                    last = nc.tensor.transpose(bank(6)[:, s * P:(s + 1) * P], xb[:, u, s * P:(s + 1) * P], ident[:])
                last.then_inc(t_ready, 1)

            def shared_down(i, u):
                pe.wait_ge(glu_ready, 4 * i + 4)
                if not isinstance(i, int) or i > 0:
                    pe.wait_ge(total_ready, i)
                for s in range(SUB):
                    for n in range(NS * HALF):
                        last = mm(bank(7)[:, s * P:(s + 1) * P], glu[:, u, n, s * P:(s + 1) * P], sw3[:, n], n == 0, n == NS * HALF - 1)
                last.then_inc(sum_ready, 1)

            def shared_tile(i, u, prev):
                transpose_tile(i, u)
                pe.wait_ge(xhi_ready, i + 1)
                pe.wait_ge(xlo_ready, i + 1)
                for n in range(NS * HALF):
                    s, h = n // HALF, n % HALF
                    if n < 3:
                        if not isinstance(i, int) or i > 0:
                            pe.wait_ge(glu_ready, 4 * i if n == 0 else 4 * i - 3 + n)
                    else:
                        pe.wait_ge(glu_ready, 4 * i + 1)
                    c = slice(h * P, (h + 1) * P)
                    for k in range(2):
                        last = split_mm(bank(2 * (n % 3) + k), sw_hi[:, s, k, c], sw_lo[:, s, k, c], xs_hi[:, u], xs_lo[:, u])
                    last.then_inc(up_ready, 1)
                    if n == 1 and prev:
                        shared_down(i - 1, 1 - u)

            shared_tile(0, 0, False)
            shared_tile(1, 1, True)
            with pe.Fori(1, NT // 2) as jj:
                for u in range(2):
                    shared_tile(jj * 2 + u, u, True)
            shared_down(NT - 1, 1)
            pe.wait_ge(total_ready, NT)

            def block_turn(j, u):
                pe.wait_ge(xr_in[u], (j - u) * (16 // DEEP) + 16)
                if not isinstance(j, int) or j > 0:
                    pe.wait_ge(r_lo_ready, j)
                for s in range(SUB):
                    last = nc.tensor.transpose(bank(6)[:, s * P:(s + 1) * P], xr[:, u, s, 0:D], ident[:])
                last.then_inc(r_t_ready, 1)

            def block_up(j, u, h):
                if h == 0:
                    pe.wait_ge(wb_in[u], (j - u) * (16 // DEEP) + 16)
                    pe.wait_ge(r_hi_ready, j + 1)
                    pe.wait_ge(r_lo_ready, j + 1)
                if not isinstance(j, int) or j > 0:
                    pe.wait_ge(r_glu_ready, 2 * j - 1 + h)
                for k in range(2):
                    c = slice(k * H + h * P, k * H + (h + 1) * P)
                    d = slice(2 * H + k * H + h * P, 2 * H + k * H + (h + 1) * P)
                    last = split_mm(bank(2 * h + k), wb[:, u, c], wb[:, u, d], xs_hi[:, u % 2], xs_lo[:, u % 2])
                last.then_inc(r_up_ready, 1)

            def block_down(j, u):
                pe.wait_ge(r_glu_ready, 2 * j + 2)
                if not isinstance(j, int) or j > 0:
                    pe.wait_ge(r_res_ready, j)
                for s in range(SUB):
                    for h in range(HALF):
                        last = mm(bank(7)[:, s * P:(s + 1) * P], glu[:, u % 2, h, s * P:(s + 1) * P],
                                  wb[:, u, W3AT + h * D:W3AT + (h + 1) * D].bitcast(F32), h == 0, h == HALF - 1)
                last.then_inc(r_sum_ready, 1)

            def routed(j, u, nxt, prev):
                block_up(j, u, 0)
                if nxt:
                    block_turn(j + 1, (u + 1) % DEEP)
                if prev:
                    block_down(j - 1, (u - 1) % DEEP)
                block_up(j, u, 1)

            block_turn(0, 0)
            for j in range(DEEP):
                routed(j, j, True, j > 0)
            with pe.Fori(1, NBLK // DEEP) as jj:
                for u in range(DEEP):
                    routed(jj * DEEP + u, u, True, True)
            for j in range(NBLK // DEEP * DEEP, NBLK):
                routed(j, j % DEEP, j + 1 < NBLK, True)
            block_down(NBLK - 1, (NBLK - 1) % DEEP)


N_EARLY = 13
N_LATE = 10
N_BLANK = 20


def kernel(**inputs):
    import numpy as np
    import concourse.bacc as bacc
    from concourse.bass_utils import run_bass_kernel_spmd

    def lay(x):
        return np.ascontiguousarray(x)

    g = {k: np.asarray(v) for k, v in inputs.items()}
    B, S, D = g["x"].shape
    NE, _, H = g["L0_ffn_rw1"].shape
    E = g["L0_xattn_proj_in"].shape[0]
    K = g["ctx_512"].shape[1]
    W_in = g["L0_attn_W_in"]

    def up(w):
        return lay(w.transpose(1, 0, 2))

    def down(w):
        n, h, d = w.shape
        return lay(w.reshape(n, h // 128, 128, d).transpose(2, 0, 1, 3))

    def bias(b):
        n, h = b.shape
        return lay(b.reshape(n, h // 128, 128).transpose(2, 0, 1))

    arrays = {
        "xT": lay(g["x"].reshape(B * S, D).T),
        "w_ctx": lay(g["ctx_512"].transpose(1, 0, 2).reshape(K, B * S)),
        "ens": lay(g["itok_BxS2xS_0_7"].transpose(1, 0, 2).reshape(K, B * S)),
        "w_u": lay(W_in[:D]),
        "w_gate": lay(W_in[D:].T),
        "w_state": lay(g["L0_attn_W_state"].T),
        "w_dt": lay(g["L0_attn_W_dt"].T),
        "w_c": lay(g["L0_attn_W_C"].T),
        "w_out": lay(g["L0_attn_W_out"].T),
        "b_dt": g["L0_attn_b_dt"], "D": g["L0_attn_D"], "A_log": g["L0_attn_A_log"],
        "proj_in": lay(g["L0_xattn_proj_in"].transpose(2, 0, 1)),
        "proj_out": down(lay(g["L0_xattn_proj_out"].transpose(0, 2, 1))),
        "gate_w": g["L0_ffn_gate_w"], "gate_b": g["L0_ffn_gate_b"],
        "w1": up(g["L0_ffn_rw1"]), "w2": up(g["L0_ffn_rw2"]), "w3": down(g["L0_ffn_rw3"]),
        "b1": bias(g["L0_ffn_rb1"]), "b2": bias(g["L0_ffn_rb2"]), "b3": g["L0_ffn_rb3"],
        "sw1": up(g["L0_ffn_sw1"]), "sw2": up(g["L0_ffn_sw2"]), "sw3": down(g["L0_ffn_sw3"]),
        "sb1": bias(g["L0_ffn_sb1"]), "sb2": bias(g["L0_ffn_sb2"]), "sb3": g["L0_ffn_sb3"],
    }
    nc = bacc.Bacc("TRN2", target_bir_lowering=False, num_devices=1)
    aps = {n: nc.dram_tensor(f"in_{n}", x.shape, mybir.dt.from_np(x.dtype), kind="ExternalInput").ap() for n, x in arrays.items()}
    aps["seq"] = S
    out = nc.dram_tensor("out_0", (B * S, D), F32, kind="ExternalOutput").ap()
    decoder_layer(nc, aps, out)
    r = run_bass_kernel_spmd(nc, [{f"in_{n}": x for n, x in arrays.items()}], core_ids=[0])
    return r.results[0]["out_0"].reshape(B, S, D)
```

```python
from contextlib import ExitStack

import concourse.bass as bass
from concourse import mybir

ALU = mybir.AluOpType
ACT = mybir.ActivationFunctionType
AX = mybir.AxisListType
F32 = mybir.dt.float32
F32R = mybir.dt.float32r
BF16 = mybir.dt.bfloat16
I32 = mybir.dt.int32
U32 = mybir.dt.uint32

P = 128


def decoder_layer(nc, a, out):
    xT, w_ctx, ens = a["xT"], a["w_ctx"], a["ens"]
    D, TOK = xT.shape
    K = w_ctx.shape[0]
    E = a["proj_in"].shape[1]
    H = a["w1"].shape[2]
    NS = a["sw1"].shape[1]
    SEQ = a["seq"]
    T = 512
    NT = TOK // T
    SUB = T // P
    HALF = H // P
    NE = a["w1"].shape[1]
    NROW = TOK // P
    NBLK = (2 * TOK + NE * (T - 1)) // T
    ROW = D + 2
    DEEP = 6
    EPS = 1e-5
    DT_MAX = 10.0
    RATE_EPS = 1e-4
    assert D == P and 2 * K == P and H == 2 * P and NS == 2 and NT % 2 == 0 and NBLK % DEEP == 3
    W3AT, B1AT, B2AT, B3AT = 4 * H, 4 * H + HALF * D, 4 * H + HALF * D + HALF, 4 * H + HALF * D + 2 * HALF
    PACK = B3AT + D

    x2_dram = nc.dram_tensor("x2_dram", (NT, P, T), F32).ap()
    pack_dram = nc.dram_tensor("pack_dram", (NE, P, PACK), F32).ap()
    sorted_dram = nc.dram_tensor("sorted_dram", (NBLK * T, ROW), F32).ap()
    routed_dram = nc.dram_tensor("routed_dram", (2 * TOK, D), F32).ap()

    with ExitStack() as ctx:
        def sb(name, shape, dt=F32):
            return ctx.enter_context(nc.sbuf_tensor(name, shape, dt))

        def sem(name):
            return ctx.enter_context(nc.semaphore(name))

        ps = ctx.enter_context(nc.psum_tensor("ps", [P, 8, T], F32))

        gate_proj = sb("gate_proj", [P, D])
        w_u = sb("w_u", [P, D])
        state_dt = sb("state_dt", [P, 2, D])
        from_u = sb("from_u", [P, 2, D])
        w_c = sb("w_c", [P, D])
        w_out = sb("w_out", [P, D])
        w_skip = sb("w_skip", [P, D])
        vecs = sb("vecs", [P, 16])
        sw = sb("sw", [P, NS, 2, H])
        sw_hi = sb("sw_hi", [P, NS, 2, H], F32R)
        sw_lo = sb("sw_lo", [P, NS, 2, H], F32R)
        sw3 = sb("sw3", [P, NS * HALF, D])
        sb12 = sb("sb12", [P, NS, 2, HALF])
        sb3 = sb("sb3", [P, NS, D])
        rw12 = sb("rw12", [P, 2, H])
        pack = sb("pack", [P, 4 * H])
        rw3 = sb("rw3", [P, NE * HALF, D])
        rb12 = sb("rb12", [P, NE, 2, HALF])
        rb3 = sb("rb3", [P, NE, D])
        router_w = sb("router_w", [P, NE])
        router_b = sb("router_b", [P, NE])
        means = sb("means", [P, 2 * 16])
        ident = sb("ident", [P, P])
        mean_mat = sb("mean_mat", [P, P])
        ones_r = sb("ones_r", [P, P], F32R)

        score = sb("score", [P, NROW, NE])
        best = sb("best", [P, 4, NROW])
        first = sb("first", [P, NROW, NE])
        second = sb("second", [P, NROW, NE])
        work = sb("work", [P, NROW, NE])
        chosen = sb("chosen", [P, NROW, NE], BF16)
        upto = sb("upto", [P, NROW, NE])
        inrow = sb("inrow", [P, NROW, NE])
        prefer = sb("prefer", [P, NE])
        prefer_i = sb("prefer_i", [P, NE], I32)
        steps_i = sb("steps_i", [P, 64], I32)
        steps = sb("steps", [P, 64])
        above_i = sb("above_i", [P, P], I32)
        before = sb("before", [P, P], BF16)
        ones_b = sb("ones_b", [P, P], BF16)
        ones_f = sb("ones_f", [P, NROW])
        blocks = sb("blocks", [P, 4, NE])
        over = sb("over", [P, NE, 16])
        owner = sb("owner", [P, 40, NE])
        owner_f = sb("owner_f", [P, 40])
        owner_i = sb("owner_i", [P, 40], I32)
        slot_f = sb("slot_f", [P, NROW, 2])
        slot = sb("slot", [P, NROW, 2], U32)
        goes_to = sb("goes_to", [P, NROW, 2], U32)
        weight = sb("weight", [P, NROW, 2])
        blank = sb("blank", [P, ROW])

        xb = sb("xb", [P, 2, T])
        over_a = ExitStack()

        def sb_a(name, shape, dt=F32):
            return over_a.enter_context(nc.sbuf_tensor(name, shape, dt))

        proj_in_hi = sb_a("proj_in_hi", [P, E, H], F32R)
        proj_in_lo = sb_a("proj_in_lo", [P, E, H], F32R)
        proj_out_hi = sb_a("proj_out_hi", [P, E * HALF, D], F32R)
        proj_out_lo = sb_a("proj_out_lo", [P, E * HALF, D], F32R)
        masked = sb_a("masked", [P, 2, T], F32R)
        gsb = sb_a("gsb", [P, 2, T])
        xin = sb_a("xin", [P, 2, T])
        wraw = sb_a("wraw", [P, 2, T])
        eraw = sb_a("eraw", [P, 2, T], I32)
        wparts = sb_a("wparts", [P, T], F32R)
        e_dt = sb_a("e_dt", [P, T])
        decay = sb_a("decay", [P, T])
        drive = sb_a("drive", [P, T])
        states = sb_a("states", [P, T])
        e_gate = sb_a("e_gate", [P, T])
        sgate = sb_a("sgate", [P, T])
        mixed = sb_a("mixed", [P, T])
        square = sb_a("square", [P, T])
        logv = sb_a("logv", [P, T])
        rstd1 = sb_a("rstd1", [P, T])
        rstd2 = sb_a("rstd2", [P, T])
        x1 = sb_a("x1", [P, 2, T])
        x1_hi = sb_a("x1_hi", [P, 2, T], F32R)
        x1_lo = sb_a("x1_lo", [P, 2, T], F32R)
        x2c = sb_a("x2c", [P, T])
        x2 = sb_a("x2", [P, 2, T])
        with nc.sbuf_tensor("proj_in", [P, E, H], F32) as proj_in, nc.sbuf_tensor("proj_out", [P, E * HALF, D], F32) as proj_out:
            pass
        hid = sb_a("hid", [P, 2, HALF, T])
        hid_hi = sb_a("hid_hi", [P, 4, HALF, T], F32R)
        hid_lo = sb_a("hid_lo", [P, 4, HALF, T], F32R)
        over_a.close()

        xs_hi = sb("xs_hi", [P, 2, T], F32R)
        xs_lo = sb("xs_lo", [P, 2, T], F32R)
        silu = sb("silu", [P, 2, T])
        glu = sb("glu", [P, 2, NS * HALF, T])
        rows = sb("rows", [P, 2, SUB, 2, ROW])
        based = sb("based", [P, T])
        total = sb("total", [P, NROW, D])
        wb = sb("wb", [P, DEEP, PACK], F32R)
        xr = sb("xr", [P, DEEP, SUB, ROW])
        res = sb("res", [P, T])
        weighed = sb("weighed", [P, 2, SUB, D])
        y1 = sb("y1", [P, 4, SUB, D])
        y2 = sb("y2", [P, 4, SUB, D])
        outb = sb("outb", [P, 2, SUB, D])
        sqc = sb("sqc", [P, SUB, P])
        slot_now = sb("slot_now", [P, 2, SUB * 2], U32)
        ssq = sb("ssq", [P, 4, SUB])

        RATE, FLOOR, BDT, DVEC, ALOG, EPSC, TMP, TMP2, TMP3 = (vecs[:, n:n + 1] for n in range(9))

        early_in = sem("early_in")
        late_in = sem("late_in")
        iotas = sem("iotas")
        consts = sem("consts")
        vec_exp = sem("vec_exp")
        vec_ln = sem("vec_ln")
        composed = sem("composed")
        weights_ready = sem("weights_ready")
        late_ready = sem("late_ready")
        s_dve = sem("dve_step")
        s_act = sem("act_step")
        x_in = [sem("x_in0"), sem("x_in1")]
        ctx_in = [sem("ctx_in0"), sem("ctx_in1")]
        mask_ready = sem("mask_ready")
        gate_ready = sem("gate_ready")
        gsb_ready = sem("gsb_ready")
        h_ready = sem("h_ready")
        hid_ready = sem("hid_ready")
        down_done = sem("down_done")
        x2c_ready = sem("x2c_ready")
        dt_ready = sem("dt_ready")
        zg_ready = sem("zg_ready")
        bt_ready = sem("bt_ready")
        edt_ready = sem("edt_ready")
        edt_held = sem("edt_held")
        soft_ready = sem("soft_ready")
        decay_ready = sem("decay_ready")
        egate_ready = sem("egate_ready")
        egate_held = sem("egate_held")
        lngate_ready = sem("lngate_ready")
        sig_ready = sem("sig_ready")
        states_ready = sem("states_ready")
        y_ready = sem("y_ready")
        mixed_ready = sem("mixed_ready")
        x1c_ready = sem("x1c_ready")
        sq1_ready = sem("sq1_ready")
        var1_ready = sem("var1_ready")
        ln1_ready = sem("ln1_ready")
        rstd1_ready = sem("rstd1_ready")
        x1_ready = sem("x1_ready")
        x1hi_ready = sem("x1hi_ready")
        x1lo_ready = sem("x1lo_ready")
        sq2_ready = sem("sq2_ready")
        var2_ready = sem("var2_ready")
        ln2_ready = sem("ln2_ready")
        rstd2_ready = sem("rstd2_ready")
        x2_ready = sem("x2_ready")
        x2_saved = [sem("x2_saved0"), sem("x2_saved1")]
        logits_ready = sem("logits_ready")
        logits_kept = sem("logits_kept")
        split_step = sem("split_step")
        blank_zero = sem("blank_zero")
        mixer_in = sem("mixer_in")
        hid_hi_ready = sem("hid_hi_ready")
        hid_lo_ready = sem("hid_lo_ready")
        tails_out = sem("tails_out")
        taken = sem("taken")
        raw12_in = sem("raw12_in")
        packed_out = sem("packed_out")
        blank_ready = sem("blank_ready")
        blanks_out = sem("blanks_out")
        shifted = sem("shifted")
        exp_done = sem("exp_done")
        chosen_ready = sem("chosen_ready")
        counted = sem("counted")
        slots_ready = sem("slots_ready")
        owners_ready = sem("owners_ready")
        xb_in = [sem("xb_in0"), sem("xb_in1")]
        t_ready = sem("t_ready")
        rows_ready = sem("rows_ready")
        based_ready = sem("based_ready")
        xhi_ready = sem("xhi_ready")
        xlo_ready = sem("xlo_ready")
        up_ready = sem("up_ready")
        silu_ready = sem("silu_ready")
        glu_ready = sem("glu_ready")
        sum_ready = sem("sum_ready")
        total_ready = sem("total_ready")
        tails_ready = sem("tails_ready")
        scattered = [sem("scattered0"), sem("scattered1")]
        slot_copied = sem("slot_copied")
        begun = sem("begun")
        wb_in = [sem(f"wb_in{u}") for u in range(DEEP)]
        xr_in = [sem(f"xr_in{u}") for u in range(DEEP)]
        r_t_ready = sem("r_t_ready")
        r_hi_ready = sem("r_hi_ready")
        r_lo_ready = sem("r_lo_ready")
        r_up_ready = sem("r_up_ready")
        r_silu_ready = sem("r_silu_ready")
        r_glu_ready = sem("r_glu_ready")
        r_sum_ready = sem("r_sum_ready")
        r_res_ready = sem("r_res_ready")
        r_weighed = sem("r_weighed")
        returned = [sem(f"returned{u}") for u in range(DEEP)]
        y_in = [sem(f"y_in{u}") for u in range(4)]
        added = sem("added")
        squared = sem("squared")
        c_ln = sem("c_ln")
        c_rstd = sem("c_rstd")
        scaled = sem("scaled")
        out_done = [sem("out_done0"), sem("out_done1")]

        G, ACC, ZG, BT, DT, MISC = 2, 3, 4, 5, 6, 7

        def bank(n):
            return ps[:, n, :]

        def sub3(ap):
            return ap.rearrange("p (s d) -> p s d", d=P)

        block = ctx.enter_context(nc.Block())

        @block.sync
        def _(sp):
            mixer = [(w_u[:], a["w_u"]), (from_u[:, 0], a["w_state"]), (from_u[:, 1], a["w_dt"]),
                     (gate_proj[:], a["w_gate"]), (w_c[:], a["w_c"]), (w_out[:], a["w_out"]),
                     (BDT, a["b_dt"].unsqueeze(1)), (DVEC, a["D"].unsqueeze(1)), (ALOG, a["A_log"].unsqueeze(1))]
            early = [(proj_in[:], a["proj_in"]), (proj_out[:], a["proj_out"].rearrange("p e h d -> p (e h) d")),
                     (router_w[:], a["gate_w"]), (router_b[:], a["gate_b"].unsqueeze(0).to_broadcast([P, NE]))]
            late = [(sw[:, :, 0], a["sw1"]), (sw[:, :, 1], a["sw2"]), (sw3[:], a["sw3"].rearrange("p e h d -> p (e h) d")),
                    (sb12[:, :, 0], a["sb1"]), (sb12[:, :, 1], a["sb2"]),
                    (sb3[:], a["sb3"].unsqueeze(0).to_broadcast([P, NS, D])),
                    (rw3[:], a["w3"].rearrange("p e h d -> p (e h) d")),
                    (rb12[:, :, 0], a["b1"]), (rb12[:, :, 1], a["b2"]),
                    (rb3[:], a["b3"].unsqueeze(0).to_broadcast([P, NE, D]))]
            assert len(mixer) == N_MIXER and len(early) == N_EARLY and len(late) == N_LATE

            def load_x(i, u):
                sp.dma_start(xin[:, u], xT[:, bass.ds(i * T, T)]).then_inc(x_in[u], 16)

            def load_ctx(i, u):
                for dst, src in ((wraw, w_ctx), (eraw, ens)):
                    for h in range(2):
                        sp.dma_start(dst[h * K:(h + 1) * K, u], src[:, bass.ds(i * T, T)]).then_inc(ctx_in[u], 16)

            for dst, src in mixer:
                sp.dma_start(dst, src).then_inc(mixer_in, 16)
            load_x(0, 0)
            for dst, src in early:
                sp.dma_start(dst, src).then_inc(early_in, 16)
            load_ctx(0, 0)
            load_x(1, 1)
            load_ctx(1, 1)
            for dst, src in late:
                sp.dma_start(dst, src).then_inc(late_in, 16)
            sp.wait_ge(late_ready, 1)
            packed = pack_dram.rearrange("e p c -> p e c")
            sp.dma_start(packed[:, :, W3AT:B1AT], rw3[:].rearrange("p (e h) d -> p e (h d)", h=HALF)).then_inc(tails_out, 16)
            sp.dma_start(packed[:, :, B1AT:B3AT], rb12[:].rearrange("p e k h -> p e (k h)")).then_inc(tails_out, 16)
            sp.dma_start(packed[:, :, B3AT:PACK], rb3[:]).then_inc(tails_out, 16)

            def save_x2(i, u):
                dst = x2_dram[bass.ds(i, 1)].rearrange("a p t -> (a p) t")
                sp.wait_ge(x2_ready, i + 1)
                sp.dma_start(dst, x2[:, u]).then_inc(x2_saved[u], 16)

            for j in (2,):
                sp.wait_ge(x1c_ready, j - 1)
                load_x(j, 0)
                sp.wait_ge(mask_ready, E * (j - 1))
                load_ctx(j, 0)
            with sp.Fori(0, (NT - 4) // 2) as j:
                for v in range(2):
                    i = j * 2 + (3 + v)
                    u = (3 + v) % 2
                    src = i * T
                    sx = xT[:, bass.ds(src, T)]
                    sp.wait_ge(x1c_ready, i - 1)
                    sp.dma_start(xin[:, u], sx).then_inc(x_in[u], 16)
                    c0, c1 = w_ctx[:, bass.ds(src, T)], ens[:, bass.ds(src, T)]
                    sp.wait_ge(mask_ready, E * (i - 1))
                    for dst, s in ((wraw, c0), (eraw, c1)):
                        for h in range(2):
                            sp.dma_start(dst[h * K:(h + 1) * K, u], s).then_inc(ctx_in[u], 16)
                    save_x2(j * 2 + v, v)
            i = NT - 1
            sp.wait_ge(x1c_ready, i - 1)
            load_x(i, i % 2)
            sp.wait_ge(mask_ready, E * (i - 1))
            load_ctx(i, i % 2)
            for i in range(2):
                sp.wait_ge(x2_saved[i], 16)
                sp.dma_start(xb[:, i], x2_dram[i]).then_inc(xb_in[i], 16)
            for i in range(NT - 4, NT):
                save_x2(i, i % 2)
            for u in range(2):
                sp.wait_ge(x2_saved[u], 16 * (NT // 2))
            with sp.Fori(1, NT // 2) as j:
                for u in range(2):
                    i = j * 2 + u
                    src = x2_dram[bass.ds(i, 1)].rearrange("a p t -> (a p) t")
                    sp.wait_ge(t_ready, i - 1)
                    sp.wait_ge(xhi_ready, i - 1)
                    sp.wait_ge(xlo_ready, i - 1)
                    sp.dma_start(xb[:, u], src).then_inc(xb_in[u], 16)

            sp.wait_ge(owners_ready, 1)
            sp.wait_ge(packed_out, 16 * NE)
            sp.wait_ge(tails_out, 16 * 3)

            def load_weights(j):
                e = sp.value_load(owner_i[0:1, bass.ds(j, 1)], min_val=0, max_val=NE - 1)
                return pack_dram[bass.ds(e, 1)].rearrange("a p r -> (a p) r")

            def block_rows(j):
                return sorted_dram[bass.ds(j * T, T)].rearrange("(s p) r -> p s r", p=P)

            def send_block(j, u, w_src, x_src):
                sp.dma_start(xr[:, u], x_src).then_inc(xr_in[u], 16)
                sp.dma_start(wb[:, u].bitcast(F32), w_src).then_inc(wb_in[u], 16)

            for u in range(2):
                sp.wait_ge(scattered[u], 16 * 2 * SUB * (NT // 2))
            for j in range(DEEP):
                send_block(j, j, load_weights(j), block_rows(j))
            with sp.Fori(1, NBLK // DEEP) as jj:
                for u in range(DEEP):
                    j = jj * DEEP + u
                    w_src, x_src = load_weights(j), block_rows(j)
                    sp.wait_ge(returned[u], jj * (16 * SUB))
                    sp.dma_start(xr[:, u], x_src).then_inc(xr_in[u], 16)
                    sp.dma_start(wb[:, u].bitcast(F32), w_src).then_inc(wb_in[u], 16)
            for j in range(NBLK // DEEP * DEEP, NBLK):
                u = j % DEEP
                w_src = load_weights(j)
                sp.wait_ge(returned[u], 16 * SUB * (NBLK // DEEP))
                send_block(j, u, w_src, block_rows(j))

            for u in range(DEEP):
                sp.wait_ge(returned[u], 16 * SUB * ((NBLK - 1 - u) // DEEP + 1))

            def routed_rows(k, i):
                return routed_dram[bass.ds(i * T + k * TOK, T)].rearrange("(s p) d -> p s d", p=P)

            def out_rows(i):
                return out[bass.ds(i * T, T)].rearrange("(s p) d -> p s d", p=P)

            for i in range(4):
                for k, y in ((0, y1), (1, y2)):
                    sp.dma_start(y[:, i], routed_rows(k, i)).then_inc(y_in[i], 16)
            with sp.Fori(0, NT // 4 - 1) as jj:
                for u in range(4):
                    i = jj * 4 + u
                    s1, s2, dst = routed_rows(0, i + 4), routed_rows(1, i + 4), out_rows(i)
                    sp.wait_ge(added, 2 * i + 2)
                    sp.dma_start(y1[:, u], s1).then_inc(y_in[u], 16)
                    sp.dma_start(y2[:, u], s2).then_inc(y_in[u], 16)
                    sp.wait_ge(scaled, i + 1)
                    sp.dma_start(dst, outb[:, u % 2]).then_inc(out_done[u % 2], 16)
            for i in range(NT - 4, NT):
                sp.wait_ge(scaled, i + 1)
                sp.dma_start(out_rows(i), outb[:, i % 2]).then_inc(out_done[i % 2], 16)
            for u in range(2):
                sp.wait_ge(out_done[u], 16 * (NT // 2))

        @block.gpsimd
        def _(pool):
            nc.gpsimd.iota(above_i[:], pattern=[[1, P]], base=0, channel_multiplier=-1).then_inc(iotas, 1)
            nc.gpsimd.iota(steps_i[:], pattern=[[1, 64]], base=0, channel_multiplier=0).then_inc(iotas, 1)
            nc.gpsimd.iota(prefer_i[:], pattern=[[-1, NE]], base=NE, channel_multiplier=0).then_inc(iotas, 1)
            nc.gpsimd.iota(goes_to[:], pattern=[[P, NROW], [TOK, 2]], base=0, channel_multiplier=1).then_inc(iotas, 1)
            nc.gpsimd.memset(blank[:], 0.0).then_inc(blank_zero, 1)
            pool.wait_ge(blank_zero, 1)
            nc.gpsimd.iota(blank[:, D:D + 1].bitcast(U32), pattern=[[0, 1]], base=2 * TOK, channel_multiplier=1).then_inc(blank_ready, 1)

            def split_weights(e, out_before):
                w1, w2 = (a[n][:, bass.ds(e, 1)].rearrange("p a h -> p (a h)") for n in ("w1", "w2"))
                dst = pack_dram[bass.ds(e, 1)].rearrange("a p c -> (a p) c")[:, 0:4 * H]
                raw = rw12[:].rearrange("p a h -> p (a h)")
                hi, lo = pack[:, 0:2 * H], pack[:, 2 * H:4 * H]
                if out_before is not None:
                    pool.wait_ge(packed_out, out_before)
                    pool.sem_inc(begun, 1)
                pool.dma_start(rw12[:, 0], w1).then_inc(raw12_in, 16)
                pool.dma_start(rw12[:, 1], w2).then_inc(raw12_in, 16)
                yield
                pool.wait_ge(raw12_in, 32 * (e + 1))
                pool.sem_inc(begun, 1)
                nc.gpsimd.tensor_copy(hi.bitcast(F32R), raw).then_inc(split_step, 1)
                yield
                pool.wait_ge(split_step, 2 * e + 1)
                nc.gpsimd.tensor_tensor(lo.bitcast(F32R), raw, hi, ALU.subtract).then_inc(split_step, 1)
                yield
                pool.wait_ge(split_step, 2 * e + 2)
                pool.sem_inc(begun, 1)
                pool.dma_start(dst, pack[:]).then_inc(packed_out, 16)

            def hid_low(i, e):
                if e >= 4 or not isinstance(i, int) or i > 0:
                    pool.wait_ge(down_done, E * i + e - 3)
                for h in range(HALF):
                    pool.wait_ge(hid_hi_ready, 16 * i + 2 * e + h + 1)
                    nc.gpsimd.tensor_tensor(hid_lo[:, e % 4, h], hid[:, e % 2, h], hid_hi[:, e % 4, h].bitcast(F32), ALU.subtract).then_inc(hid_lo_ready, 1)

            def expert_tile(i, split):
                for e in range(E):
                    hid_low(i, e)
                    if split is not None and e in (0, 2, 4, 6):
                        next(split, None)

            expert_tile(0, split_weights(0, None))
            expert_tile(1, split_weights(1, 16))
            expert_tile(2, None)
            with pool.Fori(1, (NT - 2) // 2) as j:
                expert_tile(j * 2 + 1, split_weights(j + 1, j * 16 + 16))
                expert_tile(j * 2 + 2, None)
            expert_tile(NT - 1, None)

            pool.wait_ge(tails_ready, 1)
            pool.wait_ge(blanks_out, 16 * N_BLANK)
            most = pool.to_reg(NBLK * T - 1)

            def scatter_tile(i, u, wait_free):
                now = slot[:, bass.ds(i * SUB, SUB), :]
                to = goes_to[:, bass.ds(i * SUB, SUB), :]
                wt = weight[:, bass.ds(i * SUB, SUB), :]
                if wait_free is not None:
                    pool.wait_ge(scattered[u], wait_free)
                nc.gpsimd.tensor_tensor(rows[:, u, :, :, D + 1], wt, ones_f[:, 0:2 * SUB].rearrange("p (s k) -> p s k", k=2), ALU.mult).then_inc(slot_copied, 1)
                nc.gpsimd.tensor_copy(rows[:, u, :, :, D].bitcast(U32), to).then_inc(slot_copied, 1)
                nc.gpsimd.tensor_copy(slot_now[:, u].rearrange("p (s k) -> p s k", k=2), now).then_inc(slot_copied, 1)
                pool.wait_ge(slot_copied, 3 * i + 3)
                pool.wait_ge(rows_ready, 2 * i + 2)
                pool.sem_inc(begun, 1)
                for s in range(SUB):
                    for k in range(2):
                        c = 2 * s + k
                        nc.gpsimd.indirect_dma_start(
                            out=sorted_dram, out_offset=bass.IndirectOffsetOnAxis(ap=slot_now[:, u, c:c + 1], axis=0),
                            in_=rows[:, u, s, k], in_offset=None, bounds_check=most, oob_is_err=False).then_inc(scattered[u], 16)

            scatter_tile(0, 0, None)
            scatter_tile(1, 1, None)
            with pool.Fori(1, NT // 2) as jj:
                for u in range(2):
                    scatter_tile(jj * 2 + u, u, jj * (16 * 2 * SUB))

            last = pool.to_reg(2 * TOK - 1)

            def return_block(j, u):
                pool.wait_ge(r_weighed, j + 1)
                pool.sem_inc(begun, 1)
                for s in range(SUB):
                    nc.gpsimd.indirect_dma_start(
                        out=routed_dram, out_offset=bass.IndirectOffsetOnAxis(ap=xr[:, u, s, D:D + 1].bitcast(U32), axis=0),
                        in_=weighed[:, u % 2, s], in_offset=None, bounds_check=last, oob_is_err=False).then_inc(returned[u], 16)

            with pool.Fori(0, NBLK // DEEP) as jj:
                for u in range(DEEP):
                    return_block(jj * DEEP + u, u)
            for j in range(NBLK // DEEP * DEEP, NBLK):
                return_block(j, j % DEEP)

        @block.scalar
        def _(act):
            act.preload_act_table_set("natural_log_exp_and_others")
            act.wait_ge(vec_exp, 1)
            nc.scalar.activation(TMP2, TMP, ACT.Exp).then_inc(vec_ln, 1)
            act.wait_ge(vec_ln, 1)
            nc.scalar.activation(TMP3, TMP2, ACT.Ln, bias=1.0).then_inc(vec_ln, 1)
            act.wait_ge(vec_exp, 2)
            nc.scalar.activation(FLOOR, RATE, ACT.Exp, scale=DT_MAX).then_inc(vec_ln, 1)
            act.wait_ge(consts, 1)

            def mix_exps(n):
                act.wait_ge(dt_ready, n + 1)
                nc.scalar.activation(e_dt[:], bank(DT), ACT.Exp, bias=BDT).then_inc(edt_ready, 1)
                act.wait_ge(zg_ready, n + 1)
                nc.scalar.activation(e_gate[:], bank(ZG), ACT.Exp, scale=-1.0).then_inc(egate_ready, 1)

            def mix_decay(n):
                act.wait_ge(edt_held, n + 1)
                nc.scalar.activation(e_dt[:], e_dt[:], ACT.Ln, bias=1.0).then_inc(soft_ready, 1)
                act.wait_ge(egate_held, n + 1)
                nc.scalar.activation(e_gate[:], e_gate[:], ACT.Ln, bias=1.0).then_inc(lngate_ready, 1)
                act.wait_ge(soft_ready, n + 1)
                nc.scalar.activation(decay[:], e_dt[:], ACT.Exp, scale=RATE).then_inc(decay_ready, 1)
                act.wait_ge(lngate_ready, n + 1)
                nc.scalar.activation(sgate[:], e_gate[:], ACT.Exp, scale=-1.0).then_inc(sig_ready, 1)

            def norm1_square(n):
                act.wait_ge(x1c_ready, n + 1)
                nc.scalar.activation(square[:], bank(BT), ACT.Square).then_inc(sq1_ready, 1)

            def norm1_rstd(n):
                act.wait_ge(var1_ready, n + 1)
                nc.scalar.activation(logv[:], bank(MISC), ACT.Ln, bias=EPSC).then_inc(ln1_ready, 1)
                act.wait_ge(ln1_ready, n + 1)
                nc.scalar.activation(rstd1[:], logv[:], ACT.Exp, scale=-0.5).then_inc(rstd1_ready, 1)

            def x1_high(n, u):
                act.wait_ge(x1_ready, n + 1)
                nc.scalar.activation(x1_hi[:, u], x1[:, u], ACT.Identity).then_inc(x1hi_ready, 1)

            def gate_copy(i, e):
                if e >= 2 or not isinstance(i, int) or i > 0:
                    act.wait_ge(hid_ready, 16 * i + 2 * (e - 2) + 2)
                act.wait_ge(gate_ready, E * i + e + 1)
                nc.scalar.activation(gsb[:, e % 2], bank(G), ACT.Identity).then_inc(gsb_ready, 1)

            def hid_high(i, e):
                for h in range(HALF):
                    if h == 0 and (e >= 4 or not isinstance(i, int) or i > 0):
                        act.wait_ge(down_done, E * i + e - 3)
                    act.wait_ge(hid_ready, 16 * i + 2 * e + h + 1)
                    nc.scalar.activation(hid_hi[:, e % 4, h], hid[:, e % 2, h], ACT.Identity).then_inc(hid_hi_ready, 1)

            def blank_rows(m):
                act.wait_ge(blank_ready, 1)
                view = sorted_dram.rearrange("(n p) r -> p n r", p=P)
                n, to = m * BLANK, min((m + 1) * BLANK, NBLK * SUB)
                act.dma_start(view[:, n:to], blank[:].unsqueeze(1).to_broadcast([P, to - n, ROW])).then_inc(blanks_out, 16)

            def norm2_square(i):
                act.wait_ge(x2c_ready, i + 1)
                nc.scalar.activation(square[:], x2c[:], ACT.Square).then_inc(sq2_ready, 1)

            def norm2_rstd(i):
                act.wait_ge(var2_ready, i + 1)
                nc.scalar.activation(logv[:], bank(MISC), ACT.Ln, bias=EPSC).then_inc(ln2_ready, 1)
                act.wait_ge(ln2_ready, i + 1)
                nc.scalar.activation(rstd2[:], logv[:], ACT.Exp, scale=-0.5).then_inc(rstd2_ready, 1)

            def body(i, u, mix, tail_of, blanks=()):
                for e in range(E):
                    gate_copy(i, e)
                    if e == 0 and mix:
                        mix_exps(i + 1)
                    if e == 1 and mix:
                        mix_decay(i + 1)
                    if e == 3 and tail_of:
                        norm2_square(i - 1)
                    if e == 5 and mix:
                        norm1_square(i + 1)
                    hid_high(i, e)
                    if e == 4 and tail_of:
                        norm2_rstd(i - 1)
                    if e == 6 and mix:
                        norm1_rstd(i + 1)
                    if e == 7 and mix:
                        x1_high(i + 1, 1 - u)
                    for m in blanks[2 * e:2 * e + 2]:
                        blank_rows(m)

            mix_exps(0)
            mix_decay(0)
            norm1_square(0)
            norm1_rstd(0)
            x1_high(0, 0)
            body(0, 0, True, False)
            body(1, 1, True, True, range(0, N_BLANK // 2))
            body(2, 0, True, True, range(N_BLANK // 2, N_BLANK))
            with act.Fori(1, (NT - 2) // 2) as j:
                body(j * 2 + 1, 1, True, True)
                body(j * 2 + 2, 0, True, True)
            body(NT - 1, 1, False, True)
            norm2_square(NT - 1)
            norm2_rstd(NT - 1)

            act.wait_ge(shifted, 1)
            nc.scalar.activation(score[:], score[:], ACT.Exp).then_inc(exp_done, 1)

            def shared_silu(i, s, h):
                n = 4 * i + 2 * s + h
                b = 2 * ((2 * s + h) % 3)
                if not isinstance(i, int) or n >= 2:
                    act.wait_ge(glu_ready, n - 1)
                act.wait_ge(up_ready, n + 1)
                nc.scalar.activation(silu[:, h], bank(b), ACT.Silu, bias=sb12[:, s, 0, h:h + 1]).then_inc(silu_ready, 1)

            def tile_high(i, u):
                act.wait_ge(xb_in[u], (i - u) * 8 + 16)
                if not isinstance(i, int) or i >= 2:
                    act.wait_ge(up_ready, 4 * i - 4)
                nc.scalar.activation(xs_hi[:, u], xb[:, u], ACT.Identity).then_inc(xhi_ready, 1)

            def tile_rows(i, u, k):
                act.wait_ge(t_ready, i + 1)
                nc.scalar.activation(rows[:, u, :, k, 0:D], sub3(bank(6)), ACT.Identity).then_inc(rows_ready, 1)

            def shared_tile(i, u, free, nxt):
                shared_silu(i, 0, 0)
                if nxt:
                    tile_high(i + 1, 1 - u)
                shared_silu(i, 0, 1)
                if free is not None:
                    act.wait_ge(scattered[u], free)
                tile_rows(i, u, 0)
                shared_silu(i, 1, 0)
                tile_rows(i, u, 1)
                shared_silu(i, 1, 1)

            tile_high(0, 0)
            shared_tile(0, 0, None, True)
            shared_tile(1, 1, None, True)
            with act.Fori(1, NT // 2 - 1) as jj:
                for u in range(2):
                    shared_tile(jj * 2 + u, u, jj * (16 * 2 * SUB), True)
            for i in range(NT - 2, NT):
                shared_tile(i, i % 2, 16 * 2 * SUB * (NT // 2 - 1), i + 1 < NT)

            def block_high(j, u):
                act.wait_ge(r_t_ready, j + 1)
                nc.scalar.activation(xs_hi[:, u % 2], bank(6), ACT.Identity).then_inc(r_hi_ready, 1)

            def block_weigh(j, u, free):
                if free is not None:
                    act.wait_ge(returned[(u - 2) % DEEP], free)
                act.wait_ge(r_res_ready, j + 1)
                for s in range(SUB):
                    ins = nc.scalar.activation(weighed[:, u % 2, s], res[:, s * P:(s + 1) * P], ACT.Identity, scale=xr[:, u, s, D + 1:D + 2])
                ins.then_inc(r_weighed, 1)

            def block_silu(j, u, h):
                if not isinstance(j, int) or j > 0:
                    act.wait_ge(r_glu_ready, 2 * j + h - 1)
                act.wait_ge(r_up_ready, 2 * j + h + 1)
                nc.scalar.activation(silu[:, h], bank(2 * h), ACT.Silu, bias=wb[:, u, B1AT + h:B1AT + h + 1].bitcast(F32)).then_inc(r_silu_ready, 1)

            def routed(j, u, nxt, prev, free):
                block_silu(j, u, 0)
                if nxt:
                    block_high(j + 1, (u + 1) % DEEP)
                if prev:
                    block_weigh(j - 1, (u - 1) % DEEP, free)
                block_silu(j, u, 1)

            block_high(0, 0)
            for j in range(DEEP):
                routed(j, j, True, j > 0, 16 * SUB if j >= 3 else None)
            with act.Fori(1, NBLK // DEEP) as jj:
                for u in range(DEEP):
                    routed(jj * DEEP + u, u, True, True, jj * (16 * SUB) + (16 * SUB if u >= 3 else 0))
            for j in range(NBLK // DEEP * DEEP, NBLK):
                routed(j, j % DEEP, j + 1 < NBLK, True, 16 * SUB * ((j - 3) // DEEP + 1))
            block_weigh(NBLK - 1, (NBLK - 1) % DEEP, 16 * SUB * ((NBLK - 3) // DEEP + 1))

            def c_tile(i, u):
                act.wait_ge(added, 2 * i + 2)
                for s in range(SUB):
                    ins = nc.scalar.activation(sqc[:, s], total[:, bass.ds(i * SUB + s, 1), :].rearrange("p a d -> p (a d)"), ACT.Square, accum_out=ssq[:, u, s:s + 1])
                ins.then_inc(squared, 1)
                act.wait_ge(squared, i + 1)
                nc.scalar.activation(ssq[:, 2, :], ssq[:, u, :], ACT.Ln, bias=EPSC, scale=1.0 / D).then_inc(c_ln, 1)
                act.wait_ge(c_ln, i + 1)
                nc.scalar.activation(ssq[:, u, :], ssq[:, 2, :], ACT.Exp, scale=-0.5).then_inc(c_rstd, 1)

            act.preload_act_table_set("natural_log_exp_and_others")
            with act.Fori(0, NT // 2) as jj:
                for u in range(2):
                    c_tile(jj * 2 + u, u)

        @block.vector
        def _(dve):
            v = nc.vector
            steps_done = [0]

            def link(ins):
                steps_done[0] += 1
                ins.then_inc(s_dve, 1)
                dve.wait_ge(s_dve, steps_done[0])

            link(v.memset(mean_mat[:], 1.0 / D))
            link(v.tensor_scalar(ones_r[:], mean_mat[:], float(D), None, ALU.mult))
            link(v.memset(EPSC, EPS))
            dve.wait_ge(iotas, 4)
            link(v.tensor_scalar(ident[:], above_i[:], 0.0, None, ALU.is_equal))
            dve.wait_ge(mixer_in, 16 * N_MIXER)
            link(v.tensor_scalar(TMP2, ALOG, -1.0, None, ALU.mult))
            v.tensor_tensor(TMP, ALOG, TMP2, ALU.min).then_inc(vec_exp, 1)
            link(v.scalar_tensor_tensor(out=w_skip[:], in0=w_out[:], scalar=DVEC, in1=ident[:], op0=ALU.mult, op1=ALU.add))

            def center(w, n, scale=1.0):
                m = means[:, 0:n]
                link(v.tensor_reduce(m, w, axis=AX.X, op=ALU.add))
                link(v.tensor_scalar(m, m, 1.0 / D, None, ALU.mult))
                link(v.tensor_tensor(w, w, m.unsqueeze(2).to_broadcast([P, n, D]), ALU.subtract))
                if scale != 1.0:
                    link(v.tensor_scalar(w, w, scale, None, ALU.mult))

            center(w_skip[:].unsqueeze(1), 1)
            center(w_out[:].unsqueeze(1), 1)
            dve.wait_ge(vec_ln, 2)
            link(v.scalar_tensor_tensor(out=RATE, in0=ALOG, scalar=0.0, in1=TMP3, op0=ALU.max, op1=ALU.add))
            link(v.tensor_scalar(RATE, RATE, -1.0, -RATE_EPS, ALU.mult, ALU.add))
            v.memset(TMP3, 0.0).then_inc(vec_exp, 1)
            dve.wait_ge(composed, 1)
            v.tensor_copy(state_dt[:], ps[:, 0, 0:2 * D].rearrange("p (a d) -> p a d", d=D)).then_inc(consts, 1)
            dve.wait_ge(vec_ln, 3)

            def mix_hold(n):
                dve.wait_ge(edt_ready, n + 1)
                v.tensor_scalar(e_dt[:], e_dt[:], 2.0 ** 30, None, ALU.min).then_inc(edt_held, 1)
                dve.wait_ge(egate_ready, n + 1)
                v.tensor_scalar(e_gate[:], e_gate[:], 2.0 ** 62, None, ALU.min).then_inc(egate_held, 1)

            def mix_drive(n, c):
                dve.wait_ge(decay_ready, n + 1)
                v.tensor_scalar(decay[:], decay[:], FLOOR, 1.0, ALU.max, ALU.min).then_inc(s_dve, 1)
                dve.wait_ge(s_dve, c + 1)
                dve.wait_ge(bt_ready, n + 1)
                v.scalar_tensor_tensor(out=drive[:], in0=decay[:], scalar=1.0, in1=bank(BT), op0=ALU.subtract, op1=ALU.mult).then_inc(s_dve, 1)
                dve.wait_ge(s_dve, c + 2)
                v.memset(decay[:].rearrange("p (b s) -> p b s", s=SEQ)[:, :, 0:1], 0.0).then_inc(s_dve, 1)
                dve.wait_ge(sig_ready, n + 1)
                v.tensor_tensor(sgate[:], sgate[:], bank(ZG), ALU.mult).then_inc(s_dve, 1)
                dve.wait_ge(s_dve, c + 4)

            def mix_scan(n):
                v.tensor_tensor_scan(out=states[:], data0=decay[:], data1=drive[:], initial=0.0,
                                     op0=ALU.mult, op1=ALU.subtract).then_inc(states_ready, 1)

            def mix_gate(n):
                dve.wait_ge(y_ready, n + 1)
                v.tensor_tensor(mixed[:], sgate[:], bank(DT), ALU.mult).then_inc(mixed_ready, 1)

            def norm1(n, u):
                dve.wait_ge(rstd1_ready, n + 1)
                v.tensor_tensor(x1[:, u], rstd1[:], bank(BT), ALU.mult).then_inc(x1_ready, 1)

            def x1_low(n, u):
                dve.wait_ge(x1hi_ready, n + 1)
                v.tensor_tensor(x1_lo[:, u], x1[:, u], x1_hi[:, u].bitcast(F32), ALU.subtract).then_inc(x1lo_ready, 1)

            def mask(i, e, u):
                if not isinstance(i, int) or E * i + e >= 2:
                    dve.wait_ge(gate_ready, E * i + e - 1)
                v.scalar_tensor_tensor(out=masked[:, e % 2], in0=eraw[:, u], scalar=float(e), in1=wparts[:].bitcast(F32),
                                       op0=ALU.is_equal, op1=ALU.mult).then_inc(mask_ready, 1)

            def context(i, u, c):
                dve.wait_ge(ctx_in[u], (i - u) * 32 + 64)
                v.tensor_copy(wparts[:], wraw[:, u]).then_inc(s_dve, 1)
                dve.wait_ge(s_dve, c + 1)
                v.tensor_tensor(wparts[K:2 * K], wraw[K:2 * K, u], wparts[K:2 * K].bitcast(F32), ALU.subtract).then_inc(s_dve, 1)
                dve.wait_ge(s_dve, c + 2)

            def expert(i, e):
                for h in range(HALF):
                    dve.wait_ge(h_ready, 16 * i + 2 * e + h + 1)
                    if h == 0:
                        dve.wait_ge(gsb_ready, E * i + e + 1)
                        if e >= 2 or not isinstance(i, int) or i > 0:
                            dve.wait_ge(hid_lo_ready, 16 * i + 2 * e - 2)
                    v.scalar_tensor_tensor(out=hid[:, e % 2, h], in0=bank(h), scalar=0.0, in1=gsb[:, e % 2],
                                           op0=ALU.max, op1=ALU.mult).then_inc(hid_ready, 1)

            def residual2(i, u):
                dve.wait_ge(down_done, E * i + E)
                v.tensor_tensor(x2c[:], x1[:, u], bank(ACC), ALU.add).then_inc(x2c_ready, 1)

            def norm2(i, u, free):
                dve.wait_ge(rstd2_ready, i + 1)
                if free is not None:
                    dve.wait_ge(x2_saved[u], free)
                v.tensor_tensor(x2[:, u], x2c[:], rstd2[:], ALU.mult).then_inc(x2_ready, 1)

            def logits(i):
                dve.wait_ge(logits_ready, i + 1)
                v.tensor_tensor(score[:, bass.ds(i * SUB, SUB), :], bank(ZG)[:, 0:SUB * NE].rearrange("p (s e) -> p s e", e=NE),
                                router_b[:].unsqueeze(1).to_broadcast([P, SUB, NE]), ALU.add).then_inc(logits_kept, 1)

            STEPS = 6

            def body(i, u, mix, tail_of, free, c):
                for e in range(E):
                    expert(i, e)
                    if e < E - 1:
                        mask(i, e + 1, u)
                    if e == 0 and mix:
                        mix_hold(i + 1)
                    if e == 1 and mix:
                        mix_drive(i + 1, c)
                    if e == 1 and tail_of:
                        residual2(i - 1, 1 - u)
                    if e == 2 and mix:
                        mix_scan(i + 1)
                    if e == 3 and mix:
                        mix_gate(i + 1)
                    if e == 5 and tail_of:
                        norm2(i - 1, 1 - u, free)
                    if e == 6 and mix:
                        norm1(i + 1, 1 - u)
                    if e == 7:
                        if mix:
                            context(i + 1, 1 - u, c + 4)
                            mask(i + 1, 0, 1 - u)
                            x1_low(i + 1, 1 - u)
                        if tail_of:
                            logits(i - 1)

            c0 = steps_done[0]
            mix_hold(0)
            mix_drive(0, c0)
            mix_scan(0)
            mix_gate(0)
            norm1(0, 0)
            context(0, 0, c0 + 4)
            mask(0, 0, 0)
            x1_low(0, 0)
            steps_done[0] += STEPS
            dve.wait_ge(early_in, 16 * N_EARLY)
            link(v.tensor_copy(proj_in_hi[:], proj_in[:]))
            v.tensor_tensor(proj_in_lo[:], proj_in[:], proj_in_hi[:].bitcast(F32), ALU.subtract).then_inc(weights_ready, 1)
            center(proj_out[:], E * HALF)
            link(v.tensor_copy(proj_out_hi[:], proj_out[:]))
            v.tensor_tensor(proj_out_lo[:], proj_out[:], proj_out_hi[:].bitcast(F32), ALU.subtract).then_inc(weights_ready, 1)
            body(0, 0, True, False, None, steps_done[0])
            steps_done[0] += STEPS
            dve.wait_ge(late_in, 16 * N_LATE)
            center(rw3[:], NE * HALF)
            center(rb3[:], NE)
            v.memset(TMP, 0.0).then_inc(late_ready, 1)
            link(v.tensor_copy(sw_hi[:], sw[:]))
            link(v.tensor_tensor(sw_lo[:], sw[:], sw_hi[:].bitcast(F32), ALU.subtract))
            center(sw3[:], NS * HALF, 1.0 / NS)
            center(sb3[:], NS, 1.0 / NS)
            link(v.tensor_tensor(sb3[:, 0], sb3[:, 0], sb3[:, 1], ALU.add))
            link(v.memset(ones_f[:], 1.0))
            link(v.memset(ones_b[:], 1.0))
            link(v.tensor_scalar(before[:], above_i[:], 0.0, None, ALU.is_gt))
            link(v.tensor_copy(steps[:], steps_i[:]))
            link(v.tensor_copy(prefer[:], prefer_i[:]))
            c1 = steps_done[0]
            body(1, 1, True, True, None, c1)
            body(2, 0, True, True, None, c1 + STEPS)
            with dve.Fori(1, (NT - 2) // 2) as j:
                body(j * 2 + 1, 1, True, True, j * 16, j * (2 * STEPS) + c1)
                body(j * 2 + 2, 0, True, True, j * 16, j * (2 * STEPS) + (c1 + STEPS))
            steps_done[0] += STEPS * (NT - 2)
            body(NT - 1, 1, False, True, 16 * (NT // 2 - 1), None)
            residual2(NT - 1, 1)
            norm2(NT - 1, 1, 16 * (NT // 2 - 1))
            logits(NT - 1)
            dve.wait_ge(logits_kept, NT)

            def sort_tokens():
                def over_e(ap):
                    return ap.unsqueeze(2).to_broadcast([P, NROW, NE])

                MX, W1, W2, SUMS = (best[:, n] for n in range(4))
                each = prefer[:].unsqueeze(1).to_broadcast([P, NROW, NE])
                link(v.tensor_reduce(MX, score[:], axis=AX.X, op=ALU.max))
                v.tensor_tensor(score[:], score[:], over_e(MX), ALU.subtract).then_inc(shifted, 1)
                yield
                dve.wait_ge(exp_done, 1)
                link(v.tensor_reduce(SUMS, score[:], axis=AX.X, op=ALU.add))
                link(v.reciprocal(MX, SUMS))
                link(v.tensor_tensor(score[:], score[:], over_e(MX), ALU.mult))
                yield
                for w, hot in ((W1, first), (W2, second)):
                    link(v.tensor_reduce(w, score[:], axis=AX.X, op=ALU.max))
                    link(v.tensor_tensor(work[:], score[:], over_e(w), ALU.is_equal))
                    link(v.tensor_tensor(work[:], work[:], each, ALU.mult))
                    link(v.tensor_reduce(MX, work[:], axis=AX.X, op=ALU.max))
                    link(v.tensor_tensor(hot[:], work[:], over_e(MX), ALU.is_equal))
                    if hot is first:
                        link(v.scalar_tensor_tensor(out=score[:].rearrange("p n e -> p (n e)"), in0=hot[:].rearrange("p n e -> p (n e)"), scalar=-2.0,
                                                    in1=score[:].rearrange("p n e -> p (n e)"), op0=ALU.mult, op1=ALU.add))
                yield
                v.tensor_tensor(chosen[:], first[:], second[:], ALU.add).then_inc(chosen_ready, 1)
                yield
                dve.wait_ge(counted, 1)
                v.tensor_copy(inrow[:].rearrange("p n e -> p (n e)"), bank(7)).then_inc(taken, 1)
                dve.wait_ge(counted, 2)
                v.tensor_copy(work[:].rearrange("p n e -> p (n e)"), bank(7)).then_inc(taken, 1)
                dve.wait_ge(taken, 2)
                yield
                for e in range(NE):
                    link(v.tensor_tensor_scan(out=upto[:, :, e], data0=ones_f[:], data1=work[:, :, e], initial=0.0,
                                              op0=ALU.mult, op1=ALU.add))
                yield
                link(v.tensor_copy(blocks[:, 0], upto[:, NROW - 1, :]))
                link(v.tensor_scalar(blocks[:, 0], blocks[:, 0], 1.0 / T, None, ALU.mult))
                link(v.tensor_tensor(over[:], blocks[:, 0].unsqueeze(2).to_broadcast([P, NE, 16]),
                                     steps[:, 0:16].unsqueeze(1).to_broadcast([P, NE, 16]), ALU.is_gt))
                link(v.tensor_reduce(blocks[:, 1], over[:], axis=AX.X, op=ALU.add))
                link(v.tensor_tensor_scan(out=blocks[:, 2], data0=ones_f[:, 0:NE], data1=blocks[:, 1], initial=0.0, op0=ALU.mult, op1=ALU.add))
                link(v.tensor_tensor(blocks[:, 3], blocks[:, 2], blocks[:, 1], ALU.subtract))
                link(v.tensor_scalar(blocks[:, 3], blocks[:, 3], float(T), None, ALU.mult))
                link(v.tensor_tensor(owner[:], blocks[:, 2].unsqueeze(1).to_broadcast([P, 40, NE]),
                                     steps[:, 0:40].unsqueeze(2).to_broadcast([P, 40, NE]), ALU.is_le))
                link(v.tensor_reduce(owner_f[:], owner[:], axis=AX.X, op=ALU.add))
                link(v.tensor_scalar(owner_f[:], owner_f[:], float(NE - 1), None, ALU.min))
                v.tensor_copy(owner_i[:], owner_f[:]).then_inc(owners_ready, 1)
                yield
                link(v.tensor_tensor(upto[:], upto[:], work[:], ALU.subtract))
                link(v.tensor_tensor(upto[:], upto[:], blocks[:, 3].unsqueeze(1).to_broadcast([P, NROW, NE]), ALU.add))
                link(v.tensor_tensor(upto[:].rearrange("p n e -> p (n e)"), upto[:].rearrange("p n e -> p (n e)"), inrow[:].rearrange("p n e -> p (n e)"), ALU.add))
                yield
                for k, hot in enumerate((first, second)):
                    link(v.tensor_tensor(work[:], upto[:], hot[:], ALU.mult))
                    link(v.tensor_reduce(slot_f[:, :, k], work[:], axis=AX.X, op=ALU.add))
                link(v.tensor_copy(slot[:], slot_f[:]))
                link(v.tensor_copy(weight[:, :, 0], W1))
                v.tensor_copy(weight[:, :, 1], W2).then_inc(tails_ready, 1)

            def shared_sum(i):
                dve.wait_ge(sum_ready, i + 1)
                v.tensor_tensor(total[:, bass.ds(i * SUB, SUB), :], sub3(based[:]), sub3(bank(7)), ALU.add).then_inc(total_ready, 1)

            def shared_based(i, u):
                dve.wait_ge(rows_ready, 2 * i + 1)
                v.tensor_tensor(sub3(based[:]), rows[:, u, :, 0, 0:D], sb3[:, 0].unsqueeze(1).to_broadcast([P, SUB, D]), ALU.add).then_inc(based_ready, 1)

            def tile_low(i, u):
                dve.wait_ge(xhi_ready, i + 1)
                v.tensor_tensor(xs_lo[:, u], xb[:, u], xs_hi[:, u].bitcast(F32), ALU.subtract).then_inc(xlo_ready, 1)

            def shared_tile(i, u, prev, nxt, sort=None):
                for n in range(NS * HALF):
                    s, h = n // HALF, n % HALF
                    dve.wait_ge(silu_ready, 4 * i + n + 1)
                    if not isinstance(i, int) or i >= 2:
                        dve.wait_ge(sum_ready, i - 1)
                    v.scalar_tensor_tensor(out=glu[:, u, n], in0=bank(2 * (n % 3) + 1), scalar=sb12[:, s, 1, h:h + 1], in1=silu[:, h],
                                           op0=ALU.add, op1=ALU.mult).then_inc(glu_ready, 1)
                    if n == 0 and nxt:
                        tile_low(i + 1, 1 - u)
                    if n == 1 and prev:
                        shared_sum(i - 1)
                        dve.wait_ge(total_ready, i)
                    if n == 2:
                        shared_based(i, u)
                    if sort:
                        next(sort, None)

            sort = sort_tokens()
            next(sort)
            tile_low(0, 0)
            shared_tile(0, 0, False, True, sort)
            shared_tile(1, 1, True, True, sort)
            for _ in sort:
                pass
            with dve.Fori(1, NT // 2 - 1) as jj:
                for u in range(2):
                    shared_tile(jj * 2 + u, u, True, True)
            for i in range(NT - 2, NT):
                shared_tile(i, i % 2, True, i + 1 < NT)
            dve.wait_ge(based_ready, NT)
            shared_sum(NT - 1)

            def block_low(j, u):
                dve.wait_ge(r_hi_ready, j + 1)
                v.tensor_tensor(xs_lo[:, u % 2], bank(6), xs_hi[:, u % 2].bitcast(F32), ALU.subtract).then_inc(r_lo_ready, 1)

            def block_glu(j, u, h):
                dve.wait_ge(r_silu_ready, 2 * j + h + 1)
                v.scalar_tensor_tensor(out=glu[:, u % 2, h], in0=bank(2 * h + 1), scalar=wb[:, u, B2AT + h:B2AT + h + 1].bitcast(F32), in1=silu[:, h],
                                       op0=ALU.add, op1=ALU.mult).then_inc(r_glu_ready, 1)

            def block_bias(j, u):
                if not isinstance(j, int) or j > 0:
                    dve.wait_ge(r_weighed, j)
                dve.wait_ge(r_sum_ready, j + 1)
                v.tensor_tensor(sub3(res[:]), sub3(bank(7)), wb[:, u, B3AT:PACK].bitcast(F32).unsqueeze(1).to_broadcast([P, SUB, D]),
                                ALU.add).then_inc(r_res_ready, 1)

            def routed(j, u, nxt, prev):
                block_glu(j, u, 0)
                if nxt:
                    block_low(j + 1, (u + 1) % DEEP)
                if prev:
                    block_bias(j - 1, (u - 1) % DEEP)
                block_glu(j, u, 1)

            block_low(0, 0)
            for j in range(DEEP):
                routed(j, j, True, j > 0)
            with dve.Fori(1, NBLK // DEEP) as jj:
                for u in range(DEEP):
                    routed(jj * DEEP + u, u, True, True)
            for j in range(NBLK // DEEP * DEEP, NBLK):
                routed(j, j % DEEP, j + 1 < NBLK, True)
            block_bias(NBLK - 1, (NBLK - 1) % DEEP)

            def c_add(i, u):
                mine = total[:, bass.ds(i * SUB, SUB), :]
                dve.wait_ge(y_in[u], (i - u) * 8 + 32)
                v.tensor_tensor(mine, mine, y1[:, u], ALU.add).then_inc(added, 1)
                dve.wait_ge(added, 2 * i + 1)
                v.tensor_tensor(mine, mine, y2[:, u], ALU.add).then_inc(added, 1)

            def c_scale(i, u, free):
                if free is not None:
                    dve.wait_ge(out_done[u], free)
                dve.wait_ge(c_rstd, i + 1)
                v.tensor_tensor(outb[:, u], total[:, bass.ds(i * SUB, SUB), :],
                                ssq[:, u, :].unsqueeze(2).to_broadcast([P, SUB, D]), ALU.mult).then_inc(scaled, 1)

            c_add(0, 0)
            for i in range(1, 4):
                c_add(i, i)
                c_scale(i - 1, (i - 1) % 2, 16 if i == 3 else None)
            with dve.Fori(1, NT // 4) as jj:
                for u in range(4):
                    c_add(jj * 4 + u, u)
                    c_scale(jj * 4 + (u - 1), (u - 1) % 2, jj * 32 + (-16, 0, 0, 16)[u])
            c_scale(NT - 1, 1, 16 * (NT // 2 - 1))

        @block.tensor
        def _(pe):
            def mm(o, w, x, start=True, stop=True):
                return nc.tensor.matmul(o, w, x, start=start, stop=stop)

            def split_mm(o, w_hi, w_lo, x_hi, x_lo):
                mm(o, w_hi, x_hi, True, False)
                mm(o, w_lo, x_hi, False, False)
                return mm(o, w_hi, x_lo, False, True)

            pe.wait_ge(mixer_in, 16 * N_MIXER)
            mm(ps[:, 0, 0:D], w_u[:], from_u[:, 0])
            mm(ps[:, 0, D:2 * D], w_u[:], from_u[:, 1]).then_inc(composed, 1)
            pe.wait_ge(consts, 1)

            def mix_in(n, u):
                pe.wait_ge(x_in[u], (n - u) * 8 + 16)
                mm(bank(DT), state_dt[:, 1], xin[:, u]).then_inc(dt_ready, 1)
                mm(bank(ZG), gate_proj[:], xin[:, u]).then_inc(zg_ready, 1)
                mm(bank(BT), state_dt[:, 0], xin[:, u]).then_inc(bt_ready, 1)

            def mix_y(n):
                pe.wait_ge(states_ready, n + 1)
                mm(bank(DT), w_c[:], states[:]).then_inc(y_ready, 1)

            def mix_out(n, u):
                mm(bank(BT), w_skip[:], xin[:, u], True, False)
                pe.wait_ge(mixed_ready, n + 1)
                mm(bank(BT), w_out[:], mixed[:], False, True).then_inc(x1c_ready, 1)

            def var1(n):
                pe.wait_ge(sq1_ready, n + 1)
                mm(bank(MISC), mean_mat[:], square[:]).then_inc(var1_ready, 1)

            def var2(i):
                pe.wait_ge(sq2_ready, i + 1)
                mm(bank(MISC), mean_mat[:], square[:]).then_inc(var2_ready, 1)

            def up(i, e, u):
                pe.wait_ge(mask_ready, E * i + e + 1)
                if not isinstance(i, int) or E * i + e > 0:
                    pe.wait_ge(gsb_ready, E * i + e)
                mm(bank(G), ones_r[:], masked[:, e % 2]).then_inc(gate_ready, 1)
                if e == 0:
                    pe.wait_ge(x1hi_ready, i + 1)
                    pe.wait_ge(x1lo_ready, i + 1)
                for h in range(HALF):
                    if not isinstance(i, int) or E * i + e > 0:
                        pe.wait_ge(hid_ready, 16 * i + 2 * e + h - 1)
                    c = slice(h * P, (h + 1) * P)
                    split_mm(bank(h), proj_in_hi[:, e, c], proj_in_lo[:, e, c], x1_hi[:, u], x1_lo[:, u]).then_inc(h_ready, 1)

            def down(i, e):
                if e == 0 and (not isinstance(i, int) or i > 0):
                    pe.wait_ge(x2c_ready, i)
                for h in range(HALF):
                    n = e * HALF + h
                    pe.wait_ge(hid_hi_ready, 16 * i + 2 * e + h + 1)
                    mm(bank(ACC), proj_out_hi[:, n], hid_hi[:, e % 4, h], n == 0, False)
                    mm(bank(ACC), proj_out_lo[:, n], hid_hi[:, e % 4, h], False, False)
                    pe.wait_ge(hid_lo_ready, 16 * i + 2 * e + h + 1)
                    last = mm(bank(ACC), proj_out_hi[:, n], hid_lo[:, e % 4, h], False, n == E * HALF - 1)
                last.then_inc(down_done, 1)

            def logit(i, u):
                pe.wait_ge(x2_ready, i + 1)
                for s in range(SUB):
                    last = mm(bank(ZG)[:, s * NE:(s + 1) * NE], x2[:, u, s * P:(s + 1) * P], router_w[:])
                last.then_inc(logits_ready, 1)

            def body(i, u, mix, tail_of):
                for e in range(E):
                    up(i, e, u)
                    if e >= 2:
                        down(i, e - 2)
                    elif tail_of:
                        down(i - 1, E - 2 + e)
                    if e == 0 and mix:
                        if tail_of and (not isinstance(i, int) or i > 1):
                            pe.wait_ge(logits_kept, i - 1)
                        mix_in(i + 1, 1 - u)
                    if e == 3 and mix:
                        mix_y(i + 1)
                    if e == 4:
                        if tail_of:
                            var2(i - 1)
                        if mix:
                            mix_out(i + 1, 1 - u)
                    if e == 5 and mix:
                        if tail_of:
                            pe.wait_ge(ln2_ready, i)
                        var1(i + 1)
                    if e == 6 and tail_of:
                        logit(i - 1, 1 - u)

            mix_in(0, 0)
            mix_y(0)
            mix_out(0, 0)
            var1(0)
            pe.wait_ge(weights_ready, 2)
            body(0, 0, True, False)
            body(1, 1, True, True)
            body(2, 0, True, True)
            with pe.Fori(1, (NT - 2) // 2) as j:
                body(j * 2 + 1, 1, True, True)
                body(j * 2 + 2, 0, True, True)
            body(NT - 1, 1, False, True)
            down(NT - 1, E - 2)
            down(NT - 1, E - 1)
            var2(NT - 1)
            pe.wait_ge(logits_kept, NT - 1)
            logit(NT - 1, 1)

            def count():
                pe.wait_ge(chosen_ready, 1)
                flat = chosen[:].rearrange("p n e -> p (n e)")
                mm(bank(7), before[:], flat).then_inc(counted, 1)
                pe.wait_ge(taken, 1)
                mm(bank(7), ones_b[:], flat).then_inc(counted, 1)
                pe.wait_ge(taken, 2)

            def transpose_tile(i, u):
                pe.wait_ge(xb_in[u], (i - u) * 8 + 16)
                if not isinstance(i, int) or i > 0:
                    pe.wait_ge(rows_ready, 2 * i)
                for s in range(SUB):
                    last = nc.tensor.transpose(bank(6)[:, s * P:(s + 1) * P], xb[:, u, s * P:(s + 1) * P], ident[:])
                last.then_inc(t_ready, 1)

            def shared_down(i, u):
                pe.wait_ge(glu_ready, 4 * i + 4)
                if not isinstance(i, int) or i > 0:
                    pe.wait_ge(total_ready, i)
                for s in range(SUB):
                    for n in range(NS * HALF):
                        last = mm(bank(7)[:, s * P:(s + 1) * P], glu[:, u, n, s * P:(s + 1) * P], sw3[:, n], n == 0, n == NS * HALF - 1)
                last.then_inc(sum_ready, 1)

            def shared_tile(i, u, prev):
                pe.wait_ge(xhi_ready, i + 1)
                pe.wait_ge(xlo_ready, i + 1)
                for n in range(NS * HALF):
                    s, h = n // HALF, n % HALF
                    if n == 3:
                        pe.wait_ge(glu_ready, 4 * i + 1)
                    elif not isinstance(i, int) or i > 0:
                        pe.wait_ge(glu_ready, 4 * i if n == 0 else 4 * i - 3 + n)
                    c = slice(h * P, (h + 1) * P)
                    for k in range(2):
                        last = split_mm(bank(2 * (n % 3) + k), sw_hi[:, s, k, c], sw_lo[:, s, k, c], xs_hi[:, u], xs_lo[:, u])
                    last.then_inc(up_ready, 1)
                    if n == 0:
                        transpose_tile(i, u)
                    if n == 1 and prev:
                        shared_down(i - 1, 1 - u)

            pe.wait_ge(logits_kept, NT)
            shared_tile(0, 0, False)
            count()
            shared_tile(1, 1, True)
            with pe.Fori(1, NT // 2) as jj:
                for u in range(2):
                    shared_tile(jj * 2 + u, u, True)
            shared_down(NT - 1, 1)
            pe.wait_ge(total_ready, NT)

            def block_turn(j, u, round):
                pe.wait_ge(xr_in[u], round * 16 + 16)
                if not isinstance(j, int) or j > 0:
                    pe.wait_ge(r_lo_ready, j)
                for s in range(SUB):
                    last = nc.tensor.transpose(bank(6)[:, s * P:(s + 1) * P], xr[:, u, s, 0:D], ident[:])
                last.then_inc(r_t_ready, 1)

            def block_up(j, u, round, h):
                if h == 0:
                    pe.wait_ge(wb_in[u], round * 16 + 16)
                    pe.wait_ge(r_hi_ready, j + 1)
                    pe.wait_ge(r_lo_ready, j + 1)
                if not isinstance(j, int) or j > 0:
                    pe.wait_ge(r_glu_ready, 2 * j - 1 + h)
                for k in range(2):
                    c = slice(k * H + h * P, k * H + (h + 1) * P)
                    d = slice(2 * H + k * H + h * P, 2 * H + k * H + (h + 1) * P)
                    last = split_mm(bank(2 * h + k), wb[:, u, c], wb[:, u, d], xs_hi[:, u % 2], xs_lo[:, u % 2])
                last.then_inc(r_up_ready, 1)

            def block_down(j, u):
                pe.wait_ge(r_glu_ready, 2 * j + 2)
                if not isinstance(j, int) or j > 0:
                    pe.wait_ge(r_res_ready, j)
                for s in range(SUB):
                    for h in range(HALF):
                        last = mm(bank(7)[:, s * P:(s + 1) * P], glu[:, u % 2, h, s * P:(s + 1) * P],
                                  wb[:, u, W3AT + h * D:W3AT + (h + 1) * D].bitcast(F32), h == 0, h == HALF - 1)
                last.then_inc(r_sum_ready, 1)

            def routed(j, u, round, nxt, prev):
                block_up(j, u, round, 0)
                if nxt:
                    block_turn(j + 1, (u + 1) % DEEP, round + (u + 1) // DEEP)
                if prev:
                    block_down(j - 1, (u - 1) % DEEP)
                block_up(j, u, round, 1)

            block_turn(0, 0, 0)
            for j in range(DEEP):
                routed(j, j, 0, True, j > 0)
            with pe.Fori(1, NBLK // DEEP) as jj:
                for u in range(DEEP):
                    routed(jj * DEEP + u, u, jj, True, True)
            for j in range(NBLK // DEEP * DEEP, NBLK):
                routed(j, j % DEEP, j // DEEP, j + 1 < NBLK, True)
            block_down(NBLK - 1, (NBLK - 1) % DEEP)


N_MIXER = 9
N_EARLY = 4
N_LATE = 10
N_BLANK = 20
BLANK = 8


def kernel(**inputs):
    import numpy as np
    import concourse.bacc as bacc
    from concourse.bass_utils import run_bass_kernel_spmd

    def lay(x):
        return np.ascontiguousarray(x)

    g = {k: np.asarray(v) for k, v in inputs.items()}
    B, S, D = g["x"].shape
    NE, _, H = g["L0_ffn_rw1"].shape
    E = g["L0_xattn_proj_in"].shape[0]
    K = g["ctx_512"].shape[1]
    W_in = g["L0_attn_W_in"]

    def up(w):
        return lay(w.transpose(1, 0, 2))

    def down(w):
        n, h, d = w.shape
        return lay(w.reshape(n, h // 128, 128, d).transpose(2, 0, 1, 3))

    def bias(b):
        n, h = b.shape
        return lay(b.reshape(n, h // 128, 128).transpose(2, 0, 1))

    arrays = {
        "xT": lay(g["x"].reshape(B * S, D).T),
        "w_ctx": lay(g["ctx_512"].transpose(1, 0, 2).reshape(K, B * S)),
        "ens": lay(g["itok_BxS2xS_0_7"].transpose(1, 0, 2).reshape(K, B * S)),
        "w_u": lay(W_in[:D]),
        "w_gate": lay(W_in[D:].T),
        "w_state": lay(g["L0_attn_W_state"].T),
        "w_dt": lay(g["L0_attn_W_dt"].T),
        "w_c": lay(g["L0_attn_W_C"].T),
        "w_out": lay(g["L0_attn_W_out"].T),
        "b_dt": g["L0_attn_b_dt"], "D": g["L0_attn_D"], "A_log": g["L0_attn_A_log"],
        "proj_in": lay(g["L0_xattn_proj_in"].transpose(2, 0, 1)),
        "proj_out": down(lay(g["L0_xattn_proj_out"].transpose(0, 2, 1))),
        "gate_w": g["L0_ffn_gate_w"], "gate_b": g["L0_ffn_gate_b"],
        "w1": up(g["L0_ffn_rw1"]), "w2": up(g["L0_ffn_rw2"]), "w3": down(g["L0_ffn_rw3"]),
        "b1": bias(g["L0_ffn_rb1"]), "b2": bias(g["L0_ffn_rb2"]), "b3": g["L0_ffn_rb3"],
        "sw1": up(g["L0_ffn_sw1"]), "sw2": up(g["L0_ffn_sw2"]), "sw3": down(g["L0_ffn_sw3"]),
        "sb1": bias(g["L0_ffn_sb1"]), "sb2": bias(g["L0_ffn_sb2"]), "sb3": g["L0_ffn_sb3"],
    }
    nc = bacc.Bacc("TRN2", target_bir_lowering=False, num_devices=1)
    aps = {n: nc.dram_tensor(f"in_{n}", x.shape, mybir.dt.from_np(x.dtype), kind="ExternalInput").ap() for n, x in arrays.items()}
    aps["seq"] = S
    out = nc.dram_tensor("out_0", (B * S, D), F32, kind="ExternalOutput").ap()
    decoder_layer(nc, aps, out)
    r = run_bass_kernel_spmd(nc, [{f"in_{n}": x for n, x in arrays.items()}], core_ids=[0])
    return r.results[0]["out_0"].reshape(B, S, D)
```

```python
from contextlib import ExitStack

import concourse.bass as bass
from concourse import mybir

ALU = mybir.AluOpType
ACT = mybir.ActivationFunctionType
AX = mybir.AxisListType
F32 = mybir.dt.float32
F32R = mybir.dt.float32r
BF16 = mybir.dt.bfloat16
I32 = mybir.dt.int32
U32 = mybir.dt.uint32

P = 128


def decoder_layer(nc, a, out):
    xT, w_ctx, ens = a["xT"], a["w_ctx"], a["ens"]
    D, TOK = xT.shape
    K = w_ctx.shape[0]
    E = a["proj_in"].shape[1]
    H = a["w1"].shape[2]
    NS = a["sw1"].shape[1]
    SEQ = a["seq"]
    T = 512
    NT = TOK // T
    SUB = T // P
    HALF = H // P
    NE = a["w1"].shape[1]
    NROW = TOK // P
    NBLK = (2 * TOK + NE * (T - 1)) // T
    ROW = D + 2
    DEEP = 6
    EARLY_WB = 3
    assert NT // 2 == NE
    EPS = 1e-5
    DT_MAX = 10.0
    RATE_EPS = 1e-4
    assert SUB == 4 and D == P and 2 * K == P and H == 2 * P and NS == 2 and NT % 2 == 0 and NBLK % DEEP == 3
    W3AT, B1AT, B2AT, B3AT = 4 * H, 4 * H + HALF * D, 4 * H + HALF * D + HALF, 4 * H + HALF * D + 2 * HALF
    PACK = B3AT + D

    x2_dram = nc.dram_tensor("x2_dram", (NT, P, T), F32).ap()
    pack_dram = nc.dram_tensor("pack_dram", (NE, P, PACK), F32).ap()
    CAP = TOK + T
    sorted_dram = nc.dram_tensor("sorted_dram", (NE * CAP + T, ROW), F32).ap()
    routed_dram = nc.dram_tensor("routed_dram", (2 * TOK, D), F32).ap()

    with ExitStack() as ctx:
        def sb(name, shape, dt=F32):
            return ctx.enter_context(nc.sbuf_tensor(name, shape, dt))

        def sem(name):
            return ctx.enter_context(nc.semaphore(name))

        ps = ctx.enter_context(nc.psum_tensor("ps", [P, 8, T], F32))

        mix_w = sb("mix_w", [P, 4, D])
        mix_hi = sb("mix_hi", [P, 4, D], F32R)
        mix_lo = sb("mix_lo", [P, 4, D], F32R)
        w_c = sb("w_c", [P, D])
        w_out = sb("w_out", [P, D])
        vecs = sb("vecs", [P, 16])
        sw = sb("sw", [P, NS, 2, H])
        sw_hi = sb("sw_hi", [P, NS, 2, H], F32R)
        sw_lo = sb("sw_lo", [P, NS, 2, H], F32R)
        sw3 = sb("sw3", [P, NS * HALF, D])
        sw3_hi = sb("sw3_hi", [P, NS * HALF, D], F32R)
        sw3_lo = sb("sw3_lo", [P, NS * HALF, D], F32R)
        sb12 = sb("sb12", [P, NS, 2, HALF])
        sb3 = sb("sb3", [P, NS, D])
        rw12 = sb("rw12", [P, 2, H])
        pack = sb("pack", [P, 4 * H])
        rw3 = sb("rw3", [P, NE * HALF, D])
        rb12 = sb("rb12", [P, NE, 2, HALF])
        rb3 = sb("rb3", [P, NE, D])
        router_w = sb("router_w", [P, NE])
        router_b = sb("router_b", [P, NE])
        means = sb("means", [P, 2 * 16])
        ident = sb("ident", [P, P])
        mean_mat = sb("mean_mat", [P, P])
        ones_r = sb("ones_r", [P, P], F32R)

        fresh = sb("fresh", [P, SUB, NE])
        score = sb("score", [P, 2, SUB, NE])
        best = sb("best", [P, SUB])
        rest = sb("rest", [P, SUB, NE])
        held = sb("held", [P, SUB, NE])
        hot = sb("hot", [P, 2, SUB, 2, NE])
        chosen = sb("chosen", [P, 2, SUB, NE], BF16)
        top = sb("top", [P, 2, SUB, 2])
        tally = sb("tally", [P, 2, 2, SUB, NE])
        reach = sb("reach", [P, SUB + 1, NE])
        place_of = sb("place_of", [P, SUB, NE])
        spread = sb("spread", [P, SUB, 2, NE])
        place_f = sb("place_f", [P, SUB, 2])
        slots = sb("slots", [P, 4, SUB, 2], U32)
        exps = sb("exps", [P, 2, SUB, NE])
        top_exps = sb("top_exps", [P, 2, SUB, 2])
        sums = sb("sums", [P, 2, SUB])
        starts_i = sb("starts_i", [P, NE], I32)
        starts = sb("starts", [P, NE])
        ends_i = sb("ends_i", [P, NE], I32)
        source_i = sb("source_i", [P, 40], I32)
        shift = sb("shift", [P, NE])
        prefer = sb("prefer", [P, NE])
        prefer_i = sb("prefer_i", [P, NE], I32)
        steps_i = sb("steps_i", [P, 64], I32)
        steps = sb("steps", [P, 64])
        above_i = sb("above_i", [P, P], I32)
        before = sb("before", [P, P], BF16)
        ones_b = sb("ones_b", [P, P], BF16)
        ones_f = sb("ones_f", [P, NROW])
        blocks = sb("blocks", [P, 4, NE])
        owner_i = sb("owner_i", [P, 40], I32)
        goes_to = sb("goes_to", [P, NROW, 2], U32)
        rows = sb("rows", [P, 2, SUB, 2, ROW])
        blank = sb("blank", [P, ROW])

        xb = sb("xb", [P, 2, T])
        over_a = ExitStack()

        def sb_a(name, shape, dt=F32):
            return over_a.enter_context(nc.sbuf_tensor(name, shape, dt))

        proj_in_hi = sb_a("proj_in_hi", [P, E, H], F32R)
        proj_in_lo = sb_a("proj_in_lo", [P, E, H], F32R)
        proj_out_hi = sb_a("proj_out_hi", [P, E * HALF, D], F32R)
        proj_out_lo = sb_a("proj_out_lo", [P, E * HALF, D], F32R)
        masked = sb_a("masked", [P, 2, T], F32R)
        gsb = sb_a("gsb", [P, 2, T])
        xin = sb_a("xin", [P, 2, T])
        x2 = sb_a("x2", [P, 2, T])
        xin_hi = sb_a("xin_hi", [P, 2, T], F32R)
        xin_lo = sb_a("xin_lo", [P, 2, T], F32R)
        wraw = sb_a("wraw", [P, 2, T])
        eraw = sb_a("eraw", [P, 2, T], I32)
        wparts = sb_a("wparts", [P, 2, T], F32R)
        e_dt = sb_a("e_dt", [P, T])
        decay = sb_a("decay", [P, T])
        drive = sb_a("drive", [P, T])
        states = sb_a("states", [P, T])
        e_gate = sb_a("e_gate", [P, T])
        sgate = sb_a("sgate", [P, T])
        mixed = sb_a("mixed", [P, T])
        square = sb_a("square", [P, T])
        rstd1 = sb_a("rstd1", [P, T])
        rstd2 = sb_a("rstd2", [P, T])
        x1 = sb_a("x1", [P, 2, T])
        x1_hi = sb_a("x1_hi", [P, 2, T], F32R)
        x1_lo = sb_a("x1_lo", [P, 2, T], F32R)
        x2c = sb_a("x2c", [P, T])
        with nc.sbuf_tensor("proj_in", [P, E, H], F32) as proj_in, nc.sbuf_tensor("proj_out", [P, E * HALF, D], F32) as proj_out, \
                nc.sbuf_tensor("w_u", [P, D], F32) as w_u, nc.sbuf_tensor("from_u", [P, 2, D], F32) as from_u:
            pass
        hid = sb_a("hid", [P, 2, HALF, T])
        hid_lo = sb_a("hid_lo", [P, 4, HALF, T], F32R)
        hid_hi = sb_a("hid_hi", [P, 4, HALF, T], F32R)
        over_a.close()

        xs_hi = sb("xs_hi", [P, 2, T], F32R)
        xs_lo = sb("xs_lo", [P, 2, T], F32R)
        silu = sb("silu", [P, 2, T])
        glu = sb("glu", [P, NS * HALF, T])
        over = sb("over", [P, NE, 16])
        owner = sb("owner", [P, 40, NE])
        owner_f = sb("owner_f", [P, 40])
        source_f = sb("source_f", [P, 3, 40])
        inside = sb("inside", [P, 40, NE])
        rows_more = sb("rows_more", [P, 2, SUB, 2, ROW])
        xb_more = sb("xb_more", [P, 2, T])
        y_sum = sb("y_sum", [P, 2, T])
        total = sb("total", [P, NROW, D])
        wb = sb("wb", [P, EARLY_WB, PACK], F32R)
        xr = sb("xr", [P, DEEP, SUB, ROW])
        with nc.sbuf_tensor("glu_hi", [P, 2, NS * HALF, T], F32R) as glu_hi, nc.sbuf_tensor("glu_lo", [P, 2, NS * HALF, T], F32R) as glu_lo:
            pass
        wb_more = sb("wb_more", [P, DEEP - EARLY_WB, PACK], F32R)
        wbs = [wb[:, u] if u < EARLY_WB else wb_more[:, u - EARLY_WB] for u in range(DEEP)]
        res = sb("res", [P, T])
        weighed = sb("weighed", [P, 2, SUB, D])
        y12 = sb("y12", [P, 4, 2, SUB, D])
        outb = sb("outb", [P, 2, SUB, D])
        ssq = sb("ssq", [P, 5, SUB])

        row_bufs = [rows[:, 0], rows[:, 1], rows_more[:, 0], rows_more[:, 1]]
        xbs = [xb[:, 0], xb[:, 1], xb_more[:, 0], xb_more[:, 1]]

        STATE, DELTA, GATE, SKIP = range(4)
        RATE, FLOOR, BDT, DVEC, ALOG, EPSC, TMP, TMP2, TMP3 = (vecs[:, n:n + 1] for n in range(9))

        early_in = sem("early_in")
        proj_out_in = sem("proj_out_in")
        skip_ready = sem("skip_ready")
        late_in = sem("late_in")
        iotas = sem("iotas")
        consts = sem("consts")
        vec_exp = sem("vec_exp")
        vec_ln = sem("vec_ln")
        composed = sem("composed")
        weights_ready = sem("weights_ready")
        late_ready = sem("late_ready")
        prepared = sem("prepared")
        s_dve = sem("dve_step")
        x_in = [sem("x_in0"), sem("x_in1")]
        ctx_in = [sem("ctx_in0"), sem("ctx_in1")]
        wparts_high = sem("wparts_high")
        mask_ready = sem("mask_ready")
        gate_ready = sem("gate_ready")
        gsb_ready = sem("gsb_ready")
        h_ready = sem("h_ready")
        hid_ready = sem("hid_ready")
        down_done = sem("down_done")
        x2c_ready = sem("x2c_ready")
        dt_ready = sem("dt_ready")
        zg_ready = sem("zg_ready")
        bt_ready = sem("bt_ready")
        edt_ready = sem("edt_ready")
        edt_held = sem("edt_held")
        soft_ready = sem("soft_ready")
        decay_ready = sem("decay_ready")
        egate_ready = sem("egate_ready")
        egate_held = sem("egate_held")
        lngate_ready = sem("lngate_ready")
        sig_ready = sem("sig_ready")
        states_ready = sem("states_ready")
        y_ready = sem("y_ready")
        mixed_ready = sem("mixed_ready")
        x1c_ready = sem("x1c_ready")
        sq1_ready = sem("sq1_ready")
        var1_ready = sem("var1_ready")
        ln1_ready = sem("ln1_ready")
        rstd1_ready = sem("rstd1_ready")
        x1_ready = sem("x1_ready")
        x1hi_ready = sem("x1hi_ready")
        x1lo_ready = sem("x1lo_ready")
        sq2_ready = sem("sq2_ready")
        var2_ready = sem("var2_ready")
        ln2_ready = sem("ln2_ready")
        rstd2_ready = sem("rstd2_ready")
        x2_ready = sem("x2_ready")
        x2_saved = [sem("x2_saved0"), sem("x2_saved1")]
        logits_ready = sem("logits_ready")
        logits_kept = sem("logits_kept")
        xinhi_ready = sem("xinhi_ready")
        xinlo_ready = sem("xinlo_ready")
        in_hi_ready = sem("in_hi_ready")
        out_centered = sem("out_centered")
        out_hi_ready = sem("out_hi_ready")
        out_ready = sem("out_ready")
        blank_zero = sem("blank_zero")
        mixer_in = sem("mixer_in")
        hid_hi_ready = sem("hid_hi_ready")
        hid_lo_ready = sem("hid_lo_ready")
        tails_out = sem("tails_out")
        raw12_in = sem("raw12_in")
        packed_out = sem("packed_out")
        blank_ready = sem("blank_ready")
        picked = sem("picked")
        exp_done = sem("exp_done")
        owners_ready = sem("owners_ready")
        xb_in = [sem(f"xb_in{u}") for u in range(4)]
        rows_ready = sem("rows_ready")
        xhi_ready = sem("xhi_ready")
        xlo_ready = sem("xlo_ready")
        up_ready = sem("up_ready")
        silu_ready = sem("silu_ready")
        glu_ready = sem("glu_ready")
        sum_ready = sem("sum_ready")
        total_ready = sem("total_ready")
        scattered = [sem(f"scattered{u}") for u in range(4)]
        addressed = sem("addressed")
        tallied = sem("tallied")
        tally_kept = sem("tally_kept")
        placing = sem("placing")
        rows_turned = sem("rows_turned")
        tails_blank = sem("tails_blank")
        ghi_ready = sem("ghi_ready")
        glo_ready = sem("glo_ready")
        y_kept = sem("y_kept")
        turned = sem("turned")
        raw12_hi = sem("raw12_hi")
        raw12_lo = sem("raw12_lo")
        begun = sem("begun")
        wb_in = [sem(f"wb_in{u}") for u in range(DEEP)]
        xr_in = [sem(f"xr_in{u}") for u in range(DEEP)]
        r_t_ready = sem("r_t_ready")
        r_hi_ready = sem("r_hi_ready")
        r_lo_ready = sem("r_lo_ready")
        r_up_ready = sem("r_up_ready")
        r_silu_ready = sem("r_silu_ready")
        r_glu_ready = sem("r_glu_ready")
        r_sum_ready = sem("r_sum_ready")
        r_res_ready = sem("r_res_ready")
        r_weighed = sem("r_weighed")
        returned = [sem(f"returned{u}") for u in range(DEEP)]
        y_in = [sem(f"y_in{u}") for u in range(4)]
        added = sem("added")
        squared = sem("squared")
        c_ln = sem("c_ln")
        c_rstd = sem("c_rstd")
        scaled = sem("scaled")
        out_done = [sem("out_done0"), sem("out_done1")]

        G, ACC, ZG, BT, DT, MISC = 2, 3, 4, 5, 6, 7
        TALLY = 64

        def bank(n):
            return ps[:, n, :]

        def sub3(ap):
            return ap.rearrange("p (s d) -> p s d", d=P)

        def every_fourth(x, s):
            return x.rearrange("f (p s) -> f s p", s=SUB)[:, s]

        block = ctx.enter_context(nc.Block())

        @block.sync
        def _(sp):
            mixer = [(w_u[:], a["w_u"]), (from_u[:, 0], a["w_state"]), (from_u[:, 1], a["w_dt"]),
                     (mix_w[:, GATE], a["w_gate"]), (w_c[:], a["w_c"]), (w_out[:], a["w_out"]),
                     (BDT, a["b_dt"].unsqueeze(1)), (DVEC, a["D"].unsqueeze(1)), (ALOG, a["A_log"].unsqueeze(1))]
            early = [(proj_in[:], a["proj_in"]), (router_w[:], a["gate_w"]), (router_b[:], a["gate_b"].unsqueeze(0).to_broadcast([P, NE]))]
            late = [(sw[:, :, 0], a["sw1"]), (sw[:, :, 1], a["sw2"]), (sw3[:], a["sw3"].rearrange("p e h d -> p (e h) d")),
                    (sb12[:, :, 0], a["sb1"]), (sb12[:, :, 1], a["sb2"]),
                    (sb3[:], a["sb3"].unsqueeze(0).to_broadcast([P, NS, D])),
                    (rw3[:], a["w3"].rearrange("p e h d -> p (e h) d")),
                    (rb12[:, :, 0], a["b1"]), (rb12[:, :, 1], a["b2"]),
                    (rb3[:], a["b3"].unsqueeze(0).to_broadcast([P, NE, D]))]
            assert len(mixer) == N_MIXER and len(early) == N_EARLY and len(late) == N_LATE

            def load_x(i, u):
                sp.dma_start(xin[:, u], xT[:, bass.ds(i * T, T)]).then_inc(x_in[u], 16)

            def load_ctx(i, u):
                for dst, src in ((wraw, w_ctx), (eraw, ens)):
                    for h in range(2):
                        sp.dma_start(dst[h * K:(h + 1) * K, u], src[:, bass.ds(i * T, T)]).then_inc(ctx_in[u], 16)

            for dst, src in mixer:
                sp.dma_start(dst, src).then_inc(mixer_in, 16)
            load_x(0, 0)
            sp.dma_start(proj_out[:], a["proj_out"].rearrange("p e h d -> p (e h) d")).then_inc(proj_out_in, 16)
            for dst, src in early:
                sp.dma_start(dst, src).then_inc(early_in, 16)
            load_ctx(0, 0)
            load_x(1, 1)
            load_ctx(1, 1)
            for dst, src in late:
                sp.dma_start(dst, src).then_inc(late_in, 16)
            def save_x2(i, u):
                dst = x2_dram[bass.ds(i, 1)].rearrange("a p t -> (a p) t")
                sp.wait_ge(x2_ready, i + 1)
                sp.dma_start(dst, x2[:, u]).then_inc(x2_saved[u], 16)

            def load_raw(e):
                w1, w2 = (a[n][:, bass.ds(e, 1)].rearrange("p a h -> p (a h)") for n in ("w1", "w2"))
                sp.dma_start(rw12[:, 0], w1).then_inc(raw12_in, 16)
                sp.dma_start(rw12[:, 1], w2).then_inc(raw12_in, 16)

            def save_pack(e, nxt):
                dst = pack_dram[bass.ds(e, 1)].rearrange("a p c -> (a p) c")[:, 0:4 * H]
                w1, w2 = (a[n][:, bass.ds(e + 1, 1)].rearrange("p a h -> p (a h)") if nxt else None for n in ("w1", "w2"))
                sp.wait_ge(raw12_lo, e + 1)
                sp.dma_start(dst, pack[:]).then_inc(packed_out, 16)
                if nxt:
                    sp.dma_start(rw12[:, 0], w1).then_inc(raw12_in, 16)
                    sp.dma_start(rw12[:, 1], w2).then_inc(raw12_in, 16)

            load_raw(0)
            sp.wait_ge(x1c_ready, 1)
            load_x(2, 0)
            sp.wait_ge(mask_ready, E)
            load_ctx(2, 0)
            with sp.Fori(0, (NT - 4) // 2) as j:
                for v in range(2):
                    i = j * 2 + (3 + v)
                    u = (3 + v) % 2
                    src = i * T
                    sx = xT[:, bass.ds(src, T)]
                    sp.wait_ge(x1c_ready, i - 1)
                    sp.dma_start(xin[:, u], sx).then_inc(x_in[u], 16)
                    c0, c1 = w_ctx[:, bass.ds(src, T)], ens[:, bass.ds(src, T)]
                    sp.wait_ge(mask_ready, E * (i - 1))
                    for dst, s in ((wraw, c0), (eraw, c1)):
                        for h in range(2):
                            sp.dma_start(dst[h * K:(h + 1) * K, u], s).then_inc(ctx_in[u], 16)
                    save_x2(j * 2 + v, v)
                    if v == 0:
                        save_pack(j, True)
            i = NT - 1
            sp.wait_ge(x1c_ready, i - 1)
            load_x(i, i % 2)
            sp.wait_ge(mask_ready, E * (i - 1))
            load_ctx(i, i % 2)
            save_pack(NE - 2, True)
            sp.wait_ge(late_ready, 1)
            packed = pack_dram.rearrange("e p c -> p e c")
            sp.dma_start(packed[:, :, W3AT:B1AT], rw3[:].rearrange("p (e h) d -> p e (h d)", h=HALF)).then_inc(tails_out, 16)
            sp.dma_start(packed[:, :, B1AT:B3AT], rb12[:].rearrange("p e k h -> p e (k h)")).then_inc(tails_out, 16)
            sp.dma_start(packed[:, :, B3AT:PACK], rb3[:]).then_inc(tails_out, 16)
            for i in range(2):
                sp.wait_ge(x2_saved[i], 16)
                sp.dma_start(xbs[i], x2_dram[i]).then_inc(xb_in[i], 16)
            for i in range(NT - 4, NT):
                save_x2(i, i % 2)
            for u in range(2):
                sp.wait_ge(x2_saved[u], 16 * (NT // 2))
            save_pack(NE - 1, False)
            sp.wait_ge(x2c_ready, NT)
            for i in range(2, 4):
                sp.dma_start(xbs[i], x2_dram[i]).then_inc(xb_in[i], 16)
            with sp.Fori(1, NT // 4) as j:
                for u in range(4):
                    i = j * 4 + u
                    src = x2_dram[bass.ds(i, 1)].rearrange("a p t -> (a p) t")
                    sp.wait_ge(sum_ready, i - 3)
                    sp.wait_ge(y_kept, i - 3)
                    sp.wait_ge(xlo_ready, i - 3)
                    sp.dma_start(xbs[u], src).then_inc(xb_in[u], 16)

            sp.wait_ge(owners_ready, 1)
            sp.wait_ge(packed_out, 16 * NE)
            sp.wait_ge(tails_out, 16 * 3)

            def load_weights(j):
                e = sp.value_load(owner_i[0:1, bass.ds(j, 1)], min_val=0, max_val=NE - 1)
                return pack_dram[bass.ds(e, 1)].rearrange("a p r -> (a p) r")

            def block_rows(j):
                at = sp.value_load(source_i[0:1, bass.ds(j, 1)], min_val=0, max_val=NE * CAP)
                return sorted_dram[bass.ds(at, T)].rearrange("(p s) r -> p s r", p=P)

            def send_block(j, u, w_src, x_src):
                sp.dma_start(xr[:, u], x_src).then_inc(xr_in[u], 16)
                sp.dma_start(wbs[u].bitcast(F32), w_src).then_inc(wb_in[u], 16)

            for j in range(EARLY_WB):
                sp.dma_start(wbs[j].bitcast(F32), load_weights(j)).then_inc(wb_in[j], 16)
            for u in range(4):
                sp.wait_ge(scattered[u], 16 * 2 * SUB * (NT // 2 - 1 if u < 2 else 1))
            sp.wait_ge(blank_ready, 1)
            blank_rows = blank[:].unsqueeze(1).to_broadcast([P, SUB, ROW])
            for e in range(NE):
                at = sp.value_load(ends_i[0:1, e:e + 1], min_val=0, max_val=NE * CAP - T)
                sp.dma_start(sorted_dram[bass.ds(at, T)].rearrange("(s p) r -> p s r", p=P), blank_rows).then_inc(tails_blank, 16)
            sp.dma_start(sorted_dram[NE * CAP:NE * CAP + T].rearrange("(s p) r -> p s r", p=P), blank_rows).then_inc(tails_blank, 16)
            sp.wait_ge(tails_blank, 16 * (NE + 1))
            for j in range(DEEP):
                sp.dma_start(xr[:, j], block_rows(j)).then_inc(xr_in[j], 16)
            sp.wait_ge(sum_ready, NT)
            for j in range(EARLY_WB, DEEP):
                sp.dma_start(wbs[j].bitcast(F32), load_weights(j)).then_inc(wb_in[j], 16)
            with sp.Fori(1, NBLK // DEEP) as jj:
                for u in range(DEEP):
                    j = jj * DEEP + u
                    w_src, x_src = load_weights(j), block_rows(j)
                    sp.wait_ge(returned[u], jj * (16 * SUB))
                    sp.dma_start(xr[:, u], x_src).then_inc(xr_in[u], 16)
                    sp.dma_start(wbs[u].bitcast(F32), w_src).then_inc(wb_in[u], 16)
            for j in range(NBLK // DEEP * DEEP, NBLK):
                u = j % DEEP
                w_src = load_weights(j)
                sp.wait_ge(returned[u], 16 * SUB * (NBLK // DEEP))
                send_block(j, u, w_src, block_rows(j))

            for u in range(DEEP):
                sp.wait_ge(returned[u], 16 * SUB * ((NBLK - 1 - u) // DEEP + 1))

            def routed_rows(i):
                tiles = routed_dram.rearrange("(k i p s) d -> i p k (s d)", k=2, p=P, s=SUB)
                return tiles[bass.ds(i, 1)].rearrange("a p k c -> (a p) k c")

            def y_buffer(u):
                return y12[:, u].rearrange("p k s d -> p k (s d)")

            def out_rows(i):
                return out[bass.ds(i * T, T)].rearrange("(p s) d -> p s d", p=P)

            for i in range(4):
                sp.dma_start(y_buffer(i), routed_rows(i)).then_inc(y_in[i], 16)
            with sp.Fori(0, NT // 4 - 1) as jj:
                for u in range(4):
                    i = jj * 4 + u
                    src, dst = routed_rows(i + 4), out_rows(i)
                    sp.wait_ge(added, 2 * i + 2)
                    sp.dma_start(y_buffer(u), src).then_inc(y_in[u], 16)
                    sp.wait_ge(scaled, i + 1)
                    sp.dma_start(dst, outb[:, u % 2]).then_inc(out_done[u % 2], 16)
            for i in range(NT - 4, NT):
                sp.wait_ge(scaled, i + 1)
                sp.dma_start(out_rows(i), outb[:, i % 2]).then_inc(out_done[i % 2], 16)
            for u in range(2):
                sp.wait_ge(out_done[u], 16 * (NT // 2))

        @block.gpsimd
        def _(pool):
            nc.gpsimd.iota(above_i[:], pattern=[[1, P]], base=0, channel_multiplier=-1).then_inc(iotas, 1)
            nc.gpsimd.iota(steps_i[:], pattern=[[1, 64]], base=0, channel_multiplier=0).then_inc(iotas, 1)
            nc.gpsimd.iota(prefer_i[:], pattern=[[-1, NE]], base=NE, channel_multiplier=0).then_inc(iotas, 1)
            nc.gpsimd.iota(goes_to[:].rearrange("p (i s) k -> p i s k", s=SUB), pattern=[[T, NT], [1, SUB], [TOK, 2]], base=0, channel_multiplier=SUB).then_inc(iotas, 1)
            nc.gpsimd.iota(starts_i[:], pattern=[[CAP, NE]], base=0, channel_multiplier=0).then_inc(iotas, 1)
            nc.gpsimd.memset(blank[:], 0.0).then_inc(blank_zero, 1)
            pool.wait_ge(blank_zero, 1)
            nc.gpsimd.iota(blank[:, D:D + 1].bitcast(U32), pattern=[[0, 1]], base=2 * TOK, channel_multiplier=1).then_inc(blank_ready, 1)

            def hid_low(i, e):
                if e >= 4 or not isinstance(i, int) or i > 0:
                    pool.wait_ge(down_done, E * i + e - 3)
                for h in range(HALF):
                    pool.wait_ge(hid_hi_ready, 16 * i + 2 * e + h + 1)
                    nc.gpsimd.tensor_tensor(hid_lo[:, e % 4, h], hid[:, e % 2, h], hid_hi[:, e % 4, h].bitcast(F32), ALU.subtract).then_inc(hid_lo_ready, 1)

            most = pool.to_reg(NE * CAP - 1)

            def address_rows(k, w, gone):
                if gone is not None:
                    pool.wait_ge(scattered[w], gone)
                nc.gpsimd.tensor_copy(row_bufs[w][:, :, :, D].bitcast(U32), goes_to[:, bass.ds(k * SUB, SUB), :]).then_inc(addressed, 1)
                pool.wait_ge(addressed, k + 1)
                pool.wait_ge(rows_ready, k * 2 + 2)
                pool.wait_ge(placing, k * PLACES + PLACES)
                pool.sem_inc(begun, 1)

            def scatter(w, c):
                nc.gpsimd.indirect_dma_start(
                    out=sorted_dram, out_offset=bass.IndirectOffsetOnAxis(ap=slots[:, w, c // 2, c % 2:c % 2 + 1], axis=0),
                    in_=row_bufs[w][:, c // 2, c % 2], in_offset=None, bounds_check=most, oob_is_err=False).then_inc(scattered[w], 16)

            def expert_tile(i, u):
                for e in range(E):
                    hid_low(i, e)
                    if e < 4 and (not isinstance(i, int) or i >= 4):
                        scatter(u, 4 + e)
                    if e >= 4 and not (isinstance(i, int) and (i < 3 or i == NT - 1)):
                        if e == 4:
                            address_rows(i - 3, 1 - u, None if isinstance(i, int) and i < 5 else (i + u) * 64 - 256)
                        scatter(1 - u, e - 4)

            pool.wait_ge(in_hi_ready, 1)
            nc.gpsimd.tensor_tensor(proj_in_lo[:], proj_in[:], proj_in_hi[:].bitcast(F32), ALU.subtract).then_inc(weights_ready, 1)
            pool.wait_ge(out_hi_ready, 1)
            nc.gpsimd.tensor_tensor(proj_out_lo[:], proj_out[:], proj_out_hi[:].bitcast(F32), ALU.subtract).then_inc(out_ready, 1)
            pool.wait_ge(out_ready, 1)
            for i in range(5):
                expert_tile(i, i % 2)
            with pool.Fori(2, (NT - 4) // 2) as j:
                expert_tile(j * 2 + 1, 1)
                expert_tile(j * 2 + 2, 0)
            for i in range(NT - 3, NT):
                expert_tile(i, i % 2)

            def shared_low(i, v):
                for n in range(NS * HALF):
                    pool.wait_ge(ghi_ready, 4 * i + n + 1)
                    nc.gpsimd.tensor_tensor(glu_lo[:, v % 2, n], glu[:, n], glu_hi[:, v % 2, n].bitcast(F32), ALU.subtract).then_inc(glo_ready, 1)

            def last_scatters():
                for k, w, gone in ((NT - 4, 0, 16 * 2 * SUB * (NT // 2 - 3 + 1) - 16 * 2 * SUB), (NT - 3, 1, 16 * 2 * SUB * (NT // 2 - 2)), (NT - 2, 2, None), (NT - 1, 3, None)):
                    address_rows(k, w, gone)
                    for c in range(2 * SUB):
                        scatter(w, c)
                        yield

            left = last_scatters()
            for i in range(12):
                for n in range(NS * HALF):
                    pool.wait_ge(ghi_ready, 4 * i + n + 1)
                    nc.gpsimd.tensor_tensor(glu_lo[:, i % 2, n], glu[:, n], glu_hi[:, i % 2, n].bitcast(F32), ALU.subtract).then_inc(glo_ready, 1)
                    if n > 0:
                        next(left, None)
            for _ in left:
                pass
            with pool.Fori(3, NT // 4) as jj:
                for v in range(4):
                    shared_low(jj * 4 + v, v)

            last = pool.to_reg(2 * TOK - 1)

            def return_block(j, u):
                pool.wait_ge(r_weighed, j + 1)
                pool.sem_inc(begun, 1)
                for s in range(SUB):
                    nc.gpsimd.indirect_dma_start(
                        out=routed_dram, out_offset=bass.IndirectOffsetOnAxis(ap=xr[:, u, s, D:D + 1].bitcast(U32), axis=0),
                        in_=weighed[:, u % 2, s], in_offset=None, bounds_check=last, oob_is_err=False).then_inc(returned[u], 16)

            with pool.Fori(0, NBLK // DEEP) as jj:
                for u in range(DEEP):
                    return_block(jj * DEEP + u, u)
            for j in range(NBLK // DEEP * DEEP, NBLK):
                return_block(j, j % DEEP)

            def c_scale(i, u, free):
                if free is not None:
                    pool.wait_ge(out_done[u % 2], free)
                pool.wait_ge(c_rstd, i + 1)
                nc.gpsimd.tensor_tensor(outb[:, u % 2], total[:, bass.ds(i * SUB, SUB), :],
                                        ssq[:, u, :].unsqueeze(2).to_broadcast([P, SUB, D]), ALU.mult).then_inc(scaled, 1)

            for i in range(4):
                c_scale(i, i, 16 if i >= 2 else None)
            with pool.Fori(1, NT // 4) as jj:
                for u in range(4):
                    c_scale(jj * 4 + u, u, jj * 32 + u // 2 * 16)

        @block.scalar
        def _(act):
            act.preload_act_table_set("natural_log_exp_and_others")
            act.wait_ge(vec_exp, 1)
            nc.scalar.activation(TMP2, TMP, ACT.Exp).then_inc(vec_ln, 1)
            act.wait_ge(vec_ln, 1)
            nc.scalar.activation(TMP3, TMP2, ACT.Ln, bias=1.0).then_inc(vec_ln, 1)
            act.wait_ge(vec_exp, 2)
            nc.scalar.activation(FLOOR, RATE, ACT.Exp, scale=DT_MAX).then_inc(vec_ln, 1)
            act.wait_ge(consts, 1)

            def x_high(n, u):
                act.wait_ge(x_in[u], (n - u) * 8 + 16)
                if not isinstance(n, int) or n >= 2:
                    act.wait_ge(x1c_ready, n - 1)
                nc.scalar.activation(xin_hi[:, u], xin[:, u], ACT.Identity).then_inc(xinhi_ready, 1)

            def context_high(n, u):
                act.wait_ge(ctx_in[u], (n - u) * 32 + 64)
                if not isinstance(n, int) or n >= 2:
                    act.wait_ge(mask_ready, E * n - E)
                nc.scalar.activation(wparts[:, u], wraw[:, u], ACT.Identity).then_inc(wparts_high, 1)

            def mix_exps(n):
                act.wait_ge(dt_ready, n + 1)
                nc.scalar.activation(e_dt[:], bank(DT), ACT.Exp, bias=BDT).then_inc(edt_ready, 1)
                act.wait_ge(zg_ready, n + 1)
                nc.scalar.activation(e_gate[:], bank(ZG), ACT.Exp, scale=-1.0).then_inc(egate_ready, 1)

            def mix_decay(n):
                act.wait_ge(edt_held, n + 1)
                nc.scalar.activation(e_dt[:], e_dt[:], ACT.Ln, bias=1.0).then_inc(soft_ready, 1)
                act.wait_ge(egate_held, n + 1)
                nc.scalar.activation(e_gate[:], e_gate[:], ACT.Ln, bias=1.0).then_inc(lngate_ready, 1)
                act.wait_ge(soft_ready, n + 1)
                nc.scalar.activation(decay[:], e_dt[:], ACT.Exp, scale=RATE).then_inc(decay_ready, 1)
                act.wait_ge(lngate_ready, n + 1)
                nc.scalar.activation(sgate[:], e_gate[:], ACT.Exp, scale=-1.0).then_inc(sig_ready, 1)

            def norm1_square(n):
                act.wait_ge(x1c_ready, n + 1)
                nc.scalar.activation(square[:], bank(BT), ACT.Square).then_inc(sq1_ready, 1)

            def norm1_rstd(n):
                act.wait_ge(var1_ready, n + 1)
                if not isinstance(n, int) or n > 0:
                    act.wait_ge(x1_ready, n)
                nc.scalar.activation(rstd1[:], bank(MISC), ACT.Ln, bias=EPSC).then_inc(ln1_ready, 1)
                act.wait_ge(ln1_ready, n + 1)
                nc.scalar.activation(rstd1[:], rstd1[:], ACT.Exp, scale=-0.5).then_inc(rstd1_ready, 1)

            def x1_high(n, u):
                act.wait_ge(x1_ready, n + 1)
                nc.scalar.activation(x1_hi[:, u], x1[:, u], ACT.Identity).then_inc(x1hi_ready, 1)

            def gate_copy(i, e):
                if e >= 2 or not isinstance(i, int) or i > 0:
                    act.wait_ge(hid_ready, 16 * i + 2 * (e - 2) + 2)
                act.wait_ge(gate_ready, E * i + e + 1)
                nc.scalar.activation(gsb[:, e % 2], bank(G), ACT.Identity).then_inc(gsb_ready, 1)

            def hid_high(i, e, last):
                for h in range(HALF):
                    if h == 0 and (e >= 4 or not isinstance(i, int) or i > 0):
                        act.wait_ge(down_done, E * i + e - 3)
                    act.wait_ge(hid_ready, 16 * i + 2 * e + h + 1)
                    nc.scalar.activation(hid_hi[:, e % 4, h], hid[:, e % 2, h], ACT.Identity).then_inc(hid_hi_ready, 1)
                    if h == 0 and e + 1 < E:
                        gate_copy(i, e + 1)
                    elif h == 0 and not last:
                        gate_copy(i + 1, 0)

            def turn_rows(k, w, c, gone):
                act.wait_ge(rows_turned, k + 1)
                if gone is not None:
                    act.wait_ge(scattered[w], gone)
                nc.scalar.activation(row_bufs[w][:, :, c, 0:D], sub3(bank(ZG if w < 2 else DT)), ACT.Identity).then_inc(rows_ready, 1)

            def router_exps(k, w):
                act.wait_ge(picked, (k + 1) * PICKS)
                if not isinstance(k, int) or k > 1:
                    act.wait_ge(placing, k * PLACES - PLACES)
                nc.scalar.activation(exps[:, w], score[:, w], ACT.Exp).then_inc(exp_done, 1)
                nc.scalar.activation(top_exps[:, w], top[:, w], ACT.Exp).then_inc(exp_done, 1)

            def pack_high(e):
                act.wait_ge(raw12_in, 32 * (e + 1))
                if not isinstance(e, int) or e > 0:
                    act.wait_ge(packed_out, e * 16)
                nc.scalar.activation(pack[:, 0:2 * H].bitcast(F32R), rw12[:].rearrange("p a h -> p (a h)"), ACT.Identity).then_inc(raw12_hi, 1)

            def norm2_square(i):
                act.wait_ge(x2c_ready, i + 1)
                nc.scalar.activation(square[:], x2c[:], ACT.Square).then_inc(sq2_ready, 1)

            def norm2_rstd(i):
                act.wait_ge(var2_ready, i + 1)
                if not isinstance(i, int) or i > 0:
                    act.wait_ge(x2_ready, i)
                nc.scalar.activation(rstd2[:], bank(MISC), ACT.Ln, bias=EPSC).then_inc(ln2_ready, 1)
                act.wait_ge(ln2_ready, i + 1)
                nc.scalar.activation(rstd2[:], rstd2[:], ACT.Exp, scale=-0.5).then_inc(rstd2_ready, 1)

            def body(i, u, mix, tail_of, ahead, pack=None):
                for e in range(E):
                    if e == 0 and mix:
                        mix_exps(i + 1)
                        mix_decay(i + 1)
                    if e == 6 and mix:
                        x1_high(i + 1, 1 - u)
                    hid_high(i, e, not mix)
                    if e == 2 and mix:
                        context_high(i + 1, 1 - u)
                    if e == 2 and tail_of:
                        norm2_square(i - 1)
                    if e == 3:
                        if mix:
                            norm1_square(i + 1)
                        if tail_of:
                            norm2_rstd(i - 1)
                    if e == 4 and mix:
                        norm1_rstd(i + 1)
                    if e == 5 and ahead:
                        x_high(i + 2, u)
                    if e == 0 and (not isinstance(i, int) or i >= 3):
                        router_exps(i - 3, 1 - u)
                    if e in (5, 6) and (not isinstance(i, int) or i >= 2):
                        turn_rows(i - 2, u, e - 5, None if isinstance(i, int) and i < 4 else (i - u) * 64 - 128)
                    if e == 1 and pack is not None:
                        pack_high(pack)

            x_high(0, 0)
            mix_exps(0)
            mix_decay(0)
            context_high(0, 0)
            act.wait_ge(early_in, 16 * N_EARLY)
            nc.scalar.activation(proj_in_hi[:], proj_in[:], ACT.Identity).then_inc(in_hi_ready, 1)
            norm1_square(0)
            act.wait_ge(out_centered, 1)
            nc.scalar.activation(proj_out_hi[:], proj_out[:], ACT.Identity).then_inc(out_hi_ready, 1)
            norm1_rstd(0)
            x1_high(0, 0)
            x_high(1, 1)
            gate_copy(0, 0)
            body(0, 0, True, False, True)
            body(1, 1, True, True, True, 0)
            body(2, 0, True, True, True)
            body(3, 1, True, True, True, 1)
            body(4, 0, True, True, True)
            with act.Fori(2, (NT - 4) // 2) as j:
                body(j * 2 + 1, 1, True, True, True, j)
                body(j * 2 + 2, 0, True, True, True)
            body(NT - 3, 1, True, True, True, NE - 2)
            body(NT - 2, 0, True, True, False)
            body(NT - 1, 1, False, True, False, NE - 1)

            def shared_silu(i, n):
                s, h = n // HALF, n % HALF
                if not isinstance(i, int) or 4 * i + n >= 2:
                    act.wait_ge(glu_ready, 4 * i + n - 1)
                act.wait_ge(up_ready, 4 * i + n + 1)
                nc.scalar.activation(silu[:, h], bank(2 * (n % 3)), ACT.Silu, bias=sb12[:, s, 0, h:h + 1]).then_inc(silu_ready, 1)

            def tile_high(i, v):
                act.wait_ge(xb_in[v], (i - v) * 4 + 16)
                if not isinstance(i, int) or i >= 2:
                    act.wait_ge(up_ready, 4 * i - 4)
                nc.scalar.activation(xs_hi[:, v % 2], xbs[v], ACT.Identity).then_inc(xhi_ready, 1)

            def glu_high(i, v, n):
                if n == 0 and (not isinstance(i, int) or i >= 2):
                    act.wait_ge(sum_ready, i - 1)
                act.wait_ge(glu_ready, 4 * i + n + 1)
                nc.scalar.activation(glu_hi[:, v % 2, n], glu[:, n], ACT.Identity).then_inc(ghi_ready, 1)

            def shared_tile(i, v, nxt):
                for n in range(NS * HALF):
                    shared_silu(i, n)
                    if n == 0 and nxt:
                        tile_high(i + 1, (v + 1) % 4)
                    if n > 0:
                        glu_high(i, v, n - 1)
                    if isinstance(i, int) and i == 0:
                        if n == 3:
                            turn_rows(NT - 1, 3, 0, None)
                            turn_rows(NT - 1, 3, 1, None)
                glu_high(i, v, 3)

            act.wait_ge(h_ready, 2 * E * NT)
            tile_high(0, 0)
            norm2_square(NT - 1)
            router_exps(NT - 3, 1)
            turn_rows(NT - 2, 2, 0, None)
            turn_rows(NT - 2, 2, 1, None)
            norm2_rstd(NT - 1)
            for i in range(4):
                shared_tile(i, i, True)
                if i == 1:
                    router_exps(NT - 2, 0)
                    router_exps(NT - 1, 1)
            with act.Fori(1, NT // 4 - 1) as jj:
                for v in range(4):
                    shared_tile(jj * 4 + v, v, True)
            for i in range(NT - 4, NT):
                shared_tile(i, i % 4, i + 1 < NT)

            def block_high(j, u):
                act.wait_ge(r_t_ready, j + 1)
                nc.scalar.activation(xs_hi[:, u % 2], bank(6), ACT.Identity).then_inc(r_hi_ready, 1)

            def block_weigh(j, u, free):
                if free is not None:
                    act.wait_ge(returned[(u - 2) % DEEP], free)
                act.wait_ge(r_res_ready, j + 1)
                for s in range(SUB):
                    ins = nc.scalar.activation(weighed[:, u % 2, s], res[:, s * P:(s + 1) * P], ACT.Identity, scale=xr[:, u, s, D + 1:D + 2])
                ins.then_inc(r_weighed, 1)

            def block_silu(j, u, h):
                if not isinstance(j, int) or j > 0:
                    act.wait_ge(r_glu_ready, 2 * j + h - 1)
                act.wait_ge(r_up_ready, 2 * j + h + 1)
                nc.scalar.activation(silu[:, h], bank(2 * h), ACT.Silu, bias=wbs[u][:, B1AT + h:B1AT + h + 1].bitcast(F32)).then_inc(r_silu_ready, 1)

            def routed(j, u, nxt, prev, free):
                block_silu(j, u, 0)
                if nxt:
                    block_high(j + 1, (u + 1) % DEEP)
                block_silu(j, u, 1)
                if prev:
                    block_weigh(j - 1, (u - 1) % DEEP, free)

            block_high(0, 0)
            for j in range(DEEP):
                routed(j, j, True, j > 0, 16 * SUB if j >= 3 else None)
            with act.Fori(1, NBLK // DEEP) as jj:
                for u in range(DEEP):
                    routed(jj * DEEP + u, u, True, True, jj * (16 * SUB) + (16 * SUB if u >= 3 else 0))
            for j in range(NBLK // DEEP * DEEP, NBLK):
                routed(j, j % DEEP, j + 1 < NBLK, True, 16 * SUB * ((j - 3) // DEEP + 1))
            block_weigh(NBLK - 1, (NBLK - 1) % DEEP, 16 * SUB * ((NBLK - 3) // DEEP + 1))

            def c_tile(i, u):
                act.wait_ge(added, 2 * i + 2)
                if not isinstance(i, int) or i >= 4:
                    act.wait_ge(scaled, i - 3)
                for s in range(SUB):
                    ins = nc.scalar.activation(sub3(res[:])[:, s], total[:, bass.ds(i * SUB + s, 1), :].rearrange("p a d -> p (a d)"), ACT.Square, accum_out=ssq[:, u, s:s + 1])
                ins.then_inc(squared, 1)
                act.wait_ge(squared, i + 1)
                nc.scalar.activation(ssq[:, 4, :], ssq[:, u, :], ACT.Ln, bias=EPSC, scale=1.0 / D).then_inc(c_ln, 1)
                act.wait_ge(c_ln, i + 1)
                nc.scalar.activation(ssq[:, u, :], ssq[:, 4, :], ACT.Exp, scale=-0.5).then_inc(c_rstd, 1)

            act.preload_act_table_set("natural_log_exp_and_others")
            for i in range(4):
                c_tile(i, i)
            with act.Fori(1, NT // 4) as jj:
                for u in range(4):
                    c_tile(jj * 4 + u, u)

        @block.vector
        def _(dve):
            v = nc.vector
            steps_done = [0]

            def link(ins):
                steps_done[0] += 1
                ins.then_inc(s_dve, 1)
                dve.wait_ge(s_dve, steps_done[0])

            link(v.memset(mean_mat[:], 1.0 / D))
            link(v.tensor_scalar(ones_r[:], mean_mat[:], float(D), None, ALU.mult))
            link(v.memset(EPSC, EPS))
            link(v.memset(top[:], 0.0))
            dve.wait_ge(iotas, 5)
            link(v.tensor_scalar(ident[:], above_i[:], 0.0, None, ALU.is_equal))
            dve.wait_ge(mixer_in, 16 * N_MIXER)
            link(v.tensor_scalar(TMP2, ALOG, -1.0, None, ALU.mult))
            v.tensor_tensor(TMP, ALOG, TMP2, ALU.min).then_inc(vec_exp, 1)
            dve.wait_ge(composed, 1)
            link(v.tensor_copy(mix_w[:, STATE:DELTA + 1], ps[:, 0, 0:2 * D].rearrange("p (a d) -> p a d", d=D)))
            link(v.tensor_copy(mix_hi[:, STATE:SKIP], mix_w[:, STATE:SKIP]))
            v.tensor_tensor(mix_lo[:, STATE:SKIP], mix_w[:, STATE:SKIP], mix_hi[:, STATE:SKIP].bitcast(F32), ALU.subtract).then_inc(consts, 1)
            dve.wait_ge(vec_ln, 2)
            link(v.scalar_tensor_tensor(out=RATE, in0=ALOG, scalar=0.0, in1=TMP3, op0=ALU.max, op1=ALU.add))
            link(v.tensor_scalar(RATE, RATE, -1.0, -RATE_EPS, ALU.mult, ALU.add))
            v.memset(TMP3, 0.0).then_inc(vec_exp, 1)

            prepared_by = [0]

            def then(ins):
                prepared_by[0] += 1
                ins.then_inc(prepared, 1)
                dve.wait_ge(prepared, prepared_by[0])

            def less_mean(w, scale=1.0):
                n = w.shape[1]
                m = means[:, 0:n]
                then(v.tensor_reduce(m, w, axis=AX.X, op=ALU.add))
                then(v.tensor_scalar(m, m, 1.0 / D, None, ALU.mult))
                then(v.tensor_tensor(w, w, m.unsqueeze(2).to_broadcast([P, n, D]), ALU.subtract))
                if scale != 1.0:
                    then(v.tensor_scalar(w, w, scale, None, ALU.mult))

            def prepare_first():
                then(v.scalar_tensor_tensor(out=mix_w[:, SKIP], in0=w_out[:], scalar=DVEC, in1=ident[:], op0=ALU.mult, op1=ALU.add))
                less_mean(mix_w[:, SKIP:SKIP + 1])
                less_mean(w_out[:].unsqueeze(1))
                then(v.tensor_copy(mix_hi[:, SKIP], mix_w[:, SKIP]))
                v.tensor_tensor(mix_lo[:, SKIP], mix_w[:, SKIP], mix_hi[:, SKIP].bitcast(F32), ALU.subtract).then_inc(skip_ready, 1)
                yield
                dve.wait_ge(proj_out_in, 16)
                for n in range(0, E * HALF, 4):
                    less_mean(proj_out[:, n:n + 4])
                    if n + 4 < E * HALF:
                        yield
                v.memset(TMP2, 0.0).then_inc(out_centered, 1)
                yield

            def x_low(n, u):
                dve.wait_ge(xinhi_ready, n + 1)
                v.tensor_tensor(xin_lo[:, u], xin[:, u], xin_hi[:, u].bitcast(F32), ALU.subtract).then_inc(xinlo_ready, 1)

            def mix_hold(n):
                dve.wait_ge(edt_ready, n + 1)
                v.tensor_scalar(e_dt[:], e_dt[:], 2.0 ** 30, None, ALU.min).then_inc(edt_held, 1)
                dve.wait_ge(egate_ready, n + 1)
                v.tensor_scalar(e_gate[:], e_gate[:], 2.0 ** 62, None, ALU.min).then_inc(egate_held, 1)

            def mix_drive(n, c):
                dve.wait_ge(decay_ready, n + 1)
                v.tensor_scalar(decay[:], decay[:], FLOOR, 1.0, ALU.max, ALU.min).then_inc(s_dve, 1)
                dve.wait_ge(s_dve, c + 1)
                dve.wait_ge(bt_ready, n + 1)
                v.scalar_tensor_tensor(out=drive[:], in0=decay[:], scalar=1.0, in1=bank(BT), op0=ALU.subtract, op1=ALU.mult).then_inc(s_dve, 1)
                dve.wait_ge(s_dve, c + 2)
                v.memset(decay[:].rearrange("p (b s) -> p b s", s=SEQ)[:, :, 0:1], 0.0).then_inc(s_dve, 1)
                dve.wait_ge(s_dve, c + 3)

            def mix_silu(n):
                dve.wait_ge(sig_ready, n + 1)
                v.tensor_tensor(sgate[:], sgate[:], bank(ZG), ALU.mult).then_inc(s_dve, 1)

            def mix_scan(n):
                v.tensor_tensor_scan(out=states[:], data0=decay[:], data1=drive[:], initial=0.0,
                                     op0=ALU.mult, op1=ALU.subtract).then_inc(states_ready, 1)

            def mix_gate(n, c):
                dve.wait_ge(s_dve, c + 4)
                dve.wait_ge(y_ready, n + 1)
                v.tensor_tensor(mixed[:], sgate[:], bank(DT), ALU.mult).then_inc(mixed_ready, 1)

            def norm1(n, u):
                dve.wait_ge(rstd1_ready, n + 1)
                v.tensor_tensor(x1[:, u], rstd1[:], bank(BT), ALU.mult).then_inc(x1_ready, 1)

            def x1_low(n, u):
                dve.wait_ge(x1hi_ready, n + 1)
                v.tensor_tensor(x1_lo[:, u], x1[:, u], x1_hi[:, u].bitcast(F32), ALU.subtract).then_inc(x1lo_ready, 1)

            def mask(i, e, u):
                if not isinstance(i, int) or E * i + e >= 2:
                    dve.wait_ge(gate_ready, E * i + e - 1)
                v.scalar_tensor_tensor(out=masked[:, e % 2], in0=eraw[:, u], scalar=float(e), in1=wparts[:, u].bitcast(F32),
                                       op0=ALU.is_equal, op1=ALU.mult).then_inc(mask_ready, 1)

            def context(i, u, c):
                dve.wait_ge(wparts_high, i + 1)
                v.tensor_tensor(wparts[K:2 * K, u], wraw[K:2 * K, u], wparts[K:2 * K, u].bitcast(F32), ALU.subtract).then_inc(s_dve, 1)
                dve.wait_ge(s_dve, c + 1)

            def expert(i, e, step):
                for h in range(HALF):
                    dve.wait_ge(h_ready, 16 * i + 2 * e + h + 1)
                    if h == 0:
                        dve.wait_ge(gsb_ready, E * i + e + 1)
                        if e >= 2 or not isinstance(i, int) or i > 0:
                            dve.wait_ge(hid_lo_ready, 16 * i + 2 * e - 2)
                    v.scalar_tensor_tensor(out=hid[:, e % 2, h], in0=bank(h), scalar=0.0, in1=gsb[:, e % 2],
                                           op0=ALU.max, op1=ALU.mult).then_inc(hid_ready, 1)
                    step()

            def residual2(i, u):
                dve.wait_ge(down_done, E * i + E)
                v.tensor_tensor(x2c[:], x1[:, u], bank(ACC), ALU.add).then_inc(x2c_ready, 1)

            def norm2(i, u, free):
                dve.wait_ge(rstd2_ready, i + 1)
                if free is not None:
                    dve.wait_ge(x2_saved[u], free)
                    dve.wait_ge(rows_turned, i - 1)
                v.tensor_tensor(x2[:, u], x2c[:], rstd2[:], ALU.mult).then_inc(x2_ready, 1)

            def logits(i):
                dve.wait_ge(logits_ready, i + 1)
                if not isinstance(i, int) or i > 0:
                    dve.wait_ge(tallied, i)
                v.tensor_tensor(fresh[:], bank(MISC)[:, 0:SUB * NE].rearrange("p (s e) -> p s e", e=NE),
                                router_b[:].unsqueeze(1).to_broadcast([P, SUB, NE]), ALU.add).then_inc(logits_kept, 1)

            def keep_tally(k, w):
                dve.wait_ge(tallied, k + 1)
                v.tensor_copy(tally[:, w].rearrange("p a s e -> p (a s e)"), bank(MISC)[:, TALLY:TALLY + 2 * SUB * NE]).then_inc(tally_kept, 1)

            def router(i, w):
                mine, hot1, hot2, second = score[:, w], hot[:, w, :, 0, :], hot[:, w, :, 1, :], top[:, w, :, 1]
                each = prefer[:].unsqueeze(1).to_broadcast([P, SUB, NE])
                most = best[:].unsqueeze(2).to_broadcast([P, SUB, NE])

                def after(n):
                    if not isinstance(i, int) or PICKS * i + n > 0:
                        dve.wait_ge(picked, i * PICKS + n)

                after(0)
                dve.wait_ge(logits_kept, i + 1)
                v.tensor_reduce(best[:], fresh[:], axis=AX.X, op=ALU.max).then_inc(picked, 1)
                yield
                after(1)
                if not isinstance(i, int) or i > 1:
                    dve.wait_ge(exp_done, i * 2 - 2)
                v.tensor_tensor(mine, fresh[:], most, ALU.subtract).then_inc(picked, 1)
                yield
                after(2)
                v.scalar_tensor_tensor(out=held[:], in0=mine, scalar=0.0, in1=each, op0=ALU.is_equal, op1=ALU.mult).then_inc(picked, 1)
                yield
                after(3)
                v.tensor_reduce(best[:], held[:], axis=AX.X, op=ALU.max).then_inc(picked, 1)
                yield
                after(4)
                if not isinstance(i, int) or i > 1:
                    dve.wait_ge(placing, i * PLACES - PLACES)
                v.tensor_tensor(hot1, held[:], most, ALU.is_equal).then_inc(picked, 1)
                yield
                after(5)
                v.scalar_tensor_tensor(out=rest[:], in0=hot1, scalar=-3e38, in1=mine, op0=ALU.mult, op1=ALU.add).then_inc(picked, 1)
                yield
                after(6)
                v.tensor_reduce(second, rest[:], axis=AX.X, op=ALU.max).then_inc(picked, 1)
                yield
                after(7)
                v.tensor_tensor(held[:], rest[:], second.unsqueeze(2).to_broadcast([P, SUB, NE]), ALU.is_equal).then_inc(picked, 1)
                yield
                after(8)
                v.tensor_tensor(held[:], held[:], each, ALU.mult).then_inc(picked, 1)
                yield
                after(9)
                v.tensor_reduce(best[:], held[:], axis=AX.X, op=ALU.max).then_inc(picked, 1)
                yield
                after(10)
                v.tensor_tensor(hot2, held[:], most, ALU.is_equal).then_inc(picked, 1)
                yield
                after(11)
                if not isinstance(i, int) or i > 1:
                    dve.wait_ge(tallied, i - 1)
                v.tensor_tensor(chosen[:, w], hot1, hot2, ALU.add).then_inc(picked, 1)
                yield

            def place(k, w, b, gone):
                def after(n):
                    if not isinstance(k, int) or PLACES * k + n > 0:
                        dve.wait_ge(placing, k * PLACES + n)

                dve.wait_ge(tally_kept, k + 1)
                for n in range(SUB):
                    after(n)
                    v.tensor_tensor(reach[:, n + 1], reach[:, n], tally[:, w, 1, n], ALU.add).then_inc(placing, 1)
                    yield
                after(4)
                v.tensor_tensor(place_of[:], tally[:, w, 0], reach[:, 0:SUB], ALU.add).then_inc(placing, 1)
                yield
                after(5)
                v.tensor_copy(reach[:, 0], reach[:, SUB]).then_inc(placing, 1)
                yield
                after(6)
                dve.wait_ge(picked, k * PICKS + PICKS)
                v.tensor_tensor(spread[:], hot[:, w], place_of[:].unsqueeze(2).to_broadcast([P, SUB, 2, NE]), ALU.mult).then_inc(placing, 1)
                yield
                after(7)
                v.tensor_reduce(place_f[:], spread[:], axis=AX.X, op=ALU.add).then_inc(placing, 1)
                yield
                after(8)
                if gone is not None:
                    dve.wait_ge(scattered[b], gone)
                v.tensor_copy(slots[:, b], place_f[:]).then_inc(placing, 1)
                yield
                after(9)
                dve.wait_ge(exp_done, k * 2 + 2)
                v.tensor_reduce(sums[:, 0], exps[:, w], axis=AX.X, op=ALU.add).then_inc(placing, 1)
                yield
                after(10)
                v.reciprocal(sums[:, 1], sums[:, 0]).then_inc(placing, 1)
                yield
                after(11)
                v.tensor_tensor(row_bufs[b][:, :, :, D + 1], top_exps[:, w], sums[:, 1].unsqueeze(2).to_broadcast([P, SUB, 2]), ALU.mult).then_inc(placing, 1)
                yield

            def pack_low(e):
                dve.wait_ge(raw12_hi, e + 1)
                v.tensor_tensor(pack[:, 2 * H:4 * H].bitcast(F32R), rw12[:].rearrange("p a h -> p (a h)"), pack[:, 0:2 * H], ALU.subtract).then_inc(raw12_lo, 1)

            STEPS = 5

            def body(i, u, mix, tail_of, ahead, free, c, prep=None, pack=None):
                late = not isinstance(i, int)
                picks = router(i - 2, u) if late or i >= 2 else None
                places = place(i - 3, 1 - u, 1 - u, None if not late and i < 5 else (i + u) * 64 - 256) if late or i >= 3 else None
                for e in range(E):
                    left = [(0, 2, 4, 4, 2, 0, 0, 0)[e] if places else 0, (0, 0, 2, 2, 4, 4, 0, 0)[e] if picks else 0]

                    def step():
                        for n, steps in enumerate((places, picks)):
                            if left[n]:
                                left[n] -= 1
                                next(steps)

                    if e == 3 and mix:
                        mix_gate(i + 1, c)
                        step()
                    if e == 0 and mix:
                        mix_hold(i + 1)
                    expert(i, e, step)
                    if e < E - 2:
                        mask(i, e + 2, u)
                    elif mix:
                        mask(i + 1, e + 2 - E, 1 - u)
                    step()
                    if e == 0 and mix:
                        mix_drive(i + 1, c)
                    if e == 1:
                        if tail_of:
                            residual2(i - 1, 1 - u)
                        if mix:
                            mix_scan(i + 1)
                    if e == 2 and mix:
                        mix_silu(i + 1)
                        step()
                    if e == 4 and pack is not None:
                        pack_low(pack)
                        step()
                    if e == 3 and mix:
                        context(i + 1, 1 - u, c + 4)
                        step()
                    if e == 4 and tail_of:
                        norm2(i - 1, 1 - u, free)
                    if e == 5 and mix:
                        norm1(i + 1, 1 - u)
                    if e == 6:
                        if mix:
                            x1_low(i + 1, 1 - u)
                        if ahead:
                            x_low(i + 2, u)
                    while any(left):
                        step()
                    if e == 7 and tail_of:
                        logits(i - 1)
                        if late or i >= 2:
                            keep_tally(i - 2, u)
                    if prep and e in (2, 3, 5, 7):
                        next(prep, None)

            x_low(0, 0)
            dve.wait_ge(vec_ln, 3)
            c0 = steps_done[0]
            first_steps = prepare_first()
            next(first_steps)
            mix_hold(0)
            next(first_steps)
            mix_drive(0, c0)
            mix_silu(0)
            mix_scan(0)
            next(first_steps)
            mix_gate(0, c0)
            next(first_steps)
            next(first_steps)
            context(0, 0, c0 + 4)
            mask(0, 0, 0)
            mask(0, 1, 0)
            norm1(0, 0)
            x1_low(0, 0)
            steps_done[0] += STEPS
            x_low(1, 1)
            body(0, 0, True, False, True, None, steps_done[0])
            steps_done[0] += STEPS

            def prepare():
                then(v.tensor_copy(steps[:], steps_i[:]))
                then(v.tensor_copy(prefer[:], prefer_i[:]))
                then(v.tensor_copy(starts[:], starts_i[:]))
                then(v.tensor_copy(reach[:, 0], starts[:]))
                then(v.memset(ones_f[:], 1.0))
                then(v.memset(ones_b[:], 1.0))
                then(v.tensor_scalar(before[:], above_i[:], 0.0, None, ALU.is_gt))
                dve.wait_ge(late_in, 16 * N_LATE)
                for n in range(0, NE * HALF, 4):
                    yield
                    less_mean(rw3[:, n:n + 4])
                for n in range(0, NE, 4):
                    yield
                    less_mean(rb3[:, n:n + 4])
                v.memset(TMP, 0.0).then_inc(late_ready, 1)
                for e in range(NS):
                    yield
                    then(v.tensor_copy(sw_hi[:, e], sw[:, e]))
                    yield
                    then(v.tensor_tensor(sw_lo[:, e], sw[:, e], sw_hi[:, e].bitcast(F32), ALU.subtract))
                yield
                less_mean(sw3[:], 1.0 / NS)
                yield
                then(v.tensor_copy(sw3_hi[:], sw3[:]))
                then(v.tensor_tensor(sw3_lo[:], sw3[:], sw3_hi[:].bitcast(F32), ALU.subtract))
                yield
                less_mean(sb3[:], 1.0 / NS)
                then(v.tensor_tensor(sb3[:, 0], sb3[:, 0], sb3[:, 1], ALU.add))

            prep = prepare()
            c1 = steps_done[0]
            body(1, 1, True, True, True, None, c1, prep, 0)
            body(2, 0, True, True, True, None, c1 + STEPS, prep)
            body(3, 1, True, True, True, 16, c1 + 2 * STEPS, prep, 1)
            body(4, 0, True, True, True, 16, c1 + 3 * STEPS, prep)
            for _ in prep:
                pass
            with dve.Fori(2, (NT - 4) // 2) as j:
                body(j * 2 + 1, 1, True, True, True, j * 16, j * (2 * STEPS) + c1, None, j)
                body(j * 2 + 2, 0, True, True, True, j * 16, j * (2 * STEPS) + (c1 + STEPS))
            steps_done[0] += STEPS * (NT - 4)
            body(NT - 3, 1, True, True, True, 16 * (NT // 2 - 2), steps_done[0], None, NE - 2)
            body(NT - 2, 0, True, True, False, 16 * (NT // 2 - 2), steps_done[0] + STEPS)
            steps_done[0] += STEPS * 2
            body(NT - 1, 1, False, True, False, 16 * (NT // 2 - 1), None, None, NE - 1)

            def tables():
                ended, started, whole = owner, inside, blocks[:, 0]
                dve.wait_ge(placing, PLACES * NT)
                link(v.tensor_copy(ends_i[:], reach[:, 0]))
                yield
                link(v.tensor_tensor(whole, reach[:, 0], starts[:], ALU.subtract))
                link(v.tensor_scalar(whole, whole, 1.0 / T, None, ALU.mult))
                yield
                link(v.tensor_tensor(over[:], whole.unsqueeze(2).to_broadcast([P, NE, 16]),
                                     steps[:, 0:16].unsqueeze(1).to_broadcast([P, NE, 16]), ALU.is_gt))
                link(v.tensor_reduce(blocks[:, 1], over[:], axis=AX.X, op=ALU.add))
                yield
                link(v.tensor_tensor_scan(out=blocks[:, 2], data0=ones_f[:, 0:NE], data1=blocks[:, 1], initial=0.0, op0=ALU.mult, op1=ALU.add))
                link(v.tensor_tensor(blocks[:, 3], blocks[:, 2], blocks[:, 1], ALU.subtract))
                yield
                at = steps[:, 0:40].unsqueeze(2).to_broadcast([P, 40, NE])
                link(v.tensor_tensor(ended[:], blocks[:, 2].unsqueeze(1).to_broadcast([P, 40, NE]), at, ALU.is_le))
                link(v.tensor_reduce(owner_f[:], ended[:], axis=AX.X, op=ALU.add))
                yield
                link(v.tensor_scalar(owner_f[:], owner_f[:], float(NE - 1), None, ALU.min))
                link(v.tensor_copy(owner_i[:], owner_f[:]))
                yield
                link(v.tensor_tensor(started[:], blocks[:, 3].unsqueeze(1).to_broadcast([P, 40, NE]), at, ALU.is_le))
                link(v.tensor_tensor(inside[:], started[:], ended[:], ALU.subtract))
                yield
                link(v.tensor_reduce(source_f[:, 0], inside[:], axis=AX.X, op=ALU.add))
                link(v.tensor_scalar(shift[:], blocks[:, 3], -float(T), -float(NE * CAP), ALU.mult, ALU.add))
                yield
                link(v.tensor_tensor(shift[:], shift[:], starts[:], ALU.add))
                link(v.tensor_tensor(inside[:], inside[:], shift[:].unsqueeze(1).to_broadcast([P, 40, NE]), ALU.mult))
                yield
                link(v.tensor_reduce(source_f[:, 1], inside[:], axis=AX.X, op=ALU.add))
                link(v.tensor_tensor(source_f[:, 2], source_f[:, 0], steps[:, 0:40], ALU.mult))
                yield
                link(v.tensor_scalar(source_f[:, 2], source_f[:, 2], float(T), float(NE * CAP), ALU.mult, ALU.add))
                link(v.tensor_tensor(source_f[:, 2], source_f[:, 2], source_f[:, 1], ALU.add))
                yield
                v.tensor_copy(source_i[:], source_f[:, 2]).then_inc(owners_ready, 1)

            def tile_low(i, v4):
                dve.wait_ge(xhi_ready, i + 1)
                v.tensor_tensor(xs_lo[:, v4 % 2], xbs[v4], xs_hi[:, v4 % 2].bitcast(F32), ALU.subtract).then_inc(xlo_ready, 1)

            def shared_y(i, v4):
                if not isinstance(i, int) or i >= 2:
                    dve.wait_ge(turned, i - 1)
                dve.wait_ge(sum_ready, i + 1)
                v.tensor_tensor(y_sum[:, v4 % 2], bank(7), xbs[v4], ALU.add).then_inc(y_kept, 1)

            def shared_rows(i, b=6):
                if isinstance(i, int) and i == 0:
                    dve.wait_ge(rows_turned, NT)
                    for u in range(2):
                        dve.wait_ge(x2_saved[u], 16 * (NT // 2))
                dve.wait_ge(turned, i + 1)
                v.tensor_tensor(total[:, bass.ds(i * SUB, SUB), :], sub3(bank(b)), sb3[:, 0].unsqueeze(1).to_broadcast([P, SUB, D]), ALU.add).then_inc(total_ready, 1)

            def shared_glu(i, n):
                s, h = n // HALF, n % HALF
                dve.wait_ge(silu_ready, 4 * i + n + 1)
                if not isinstance(i, int) or i > 0:
                    dve.wait_ge(ghi_ready, 4 * i + n - 3)
                    dve.wait_ge(glo_ready, 4 * i + n - 3)
                v.scalar_tensor_tensor(out=glu[:, n], in0=bank(2 * (n % 3) + 1), scalar=sb12[:, s, 1, h:h + 1], in1=silu[:, h],
                                       op0=ALU.add, op1=ALU.mult).then_inc(glu_ready, 1)

            def shared_tile(i, v4, nxt, steps=None):
                late = not isinstance(i, int)
                for n in range(NS * HALF):
                    if n == 0 and (late or i >= 2):
                        shared_y(i - 2, (v4 - 2) % 4)
                    shared_glu(i, n)
                    if n == 0 and nxt:
                        tile_low(i + 1, (v4 + 1) % 4)
                    if n == 3 and (late or i >= 2):
                        shared_rows(i - 2)
                    if steps:
                        for _ in range((3, 3, 3, 4, 0, 3, 3, 3)[4 * i + n] if i < 2 else 2):
                            next(steps, None)

            tile_low(0, 0)
            residual2(NT - 1, 1)
            for _ in place(NT - 3, 1, 1, 16 * 2 * SUB * (NT // 2 - 2)):
                pass
            for _ in router(NT - 2, 0):
                pass
            norm2(NT - 1, 1, 16 * (NT // 2 - 1))

            def last_places():
                logits(NT - 1)
                keep_tally(NT - 2, 0)
                yield
                yield from router(NT - 1, 1)
                keep_tally(NT - 1, 1)
                yield
                yield from place(NT - 2, 0, 2, None)
                yield from place(NT - 1, 1, 3, None)
                yield from tables()

            more = last_places()
            for i in range(8):
                shared_tile(i, i % 4, True, more)
            for _ in more:
                pass
            with dve.Fori(2, NT // 4 - 1) as jj:
                for v4 in range(4):
                    shared_tile(jj * 4 + v4, v4, True)
            for i in range(NT - 4, NT):
                shared_tile(i, i % 4, i + 1 < NT)
            shared_y(NT - 2, 2)
            shared_rows(NT - 2)
            shared_y(NT - 1, 3)

            def block_low(j, u):
                dve.wait_ge(r_hi_ready, j + 1)
                v.tensor_tensor(xs_lo[:, u % 2], bank(6), xs_hi[:, u % 2].bitcast(F32), ALU.subtract).then_inc(r_lo_ready, 1)

            def block_glu(j, u, h):
                dve.wait_ge(r_silu_ready, 2 * j + h + 1)
                v.scalar_tensor_tensor(out=glu[:, u % 2 * HALF + h], in0=bank(2 * h + 1), scalar=wbs[u][:, B2AT + h:B2AT + h + 1].bitcast(F32), in1=silu[:, h],
                                       op0=ALU.add, op1=ALU.mult).then_inc(r_glu_ready, 1)

            def block_bias(j, u):
                if not isinstance(j, int) or j > 0:
                    dve.wait_ge(r_weighed, j)
                dve.wait_ge(r_sum_ready, j + 1)
                v.tensor_tensor(sub3(res[:]), sub3(bank(7)), wbs[u][:, B3AT:PACK].bitcast(F32).unsqueeze(1).to_broadcast([P, SUB, D]),
                                ALU.add).then_inc(r_res_ready, 1)

            def routed(j, u, nxt, prev):
                block_glu(j, u, 0)
                if nxt:
                    block_low(j + 1, (u + 1) % DEEP)
                if prev:
                    block_bias(j - 1, (u - 1) % DEEP)
                block_glu(j, u, 1)

            block_low(0, 0)
            shared_rows(NT - 1, 4)
            for j in range(DEEP):
                routed(j, j, True, j > 0)
            with dve.Fori(1, NBLK // DEEP) as jj:
                for u in range(DEEP):
                    routed(jj * DEEP + u, u, True, True)
            for j in range(NBLK // DEEP * DEEP, NBLK):
                routed(j, j % DEEP, j + 1 < NBLK, True)
            block_bias(NBLK - 1, (NBLK - 1) % DEEP)

            def c_add(i, u):
                mine = total[:, bass.ds(i * SUB, SUB), :]
                dve.wait_ge(y_in[u], (i - u) * 4 + 16)
                v.tensor_tensor(mine, mine, y12[:, u, 0], ALU.add).then_inc(added, 1)
                dve.wait_ge(added, 2 * i + 1)
                v.tensor_tensor(mine, mine, y12[:, u, 1], ALU.add).then_inc(added, 1)

            with dve.Fori(0, NT // 4) as jj:
                for u in range(4):
                    c_add(jj * 4 + u, u)

        @block.tensor
        def _(pe):
            def mm(o, w, x, start=True, stop=True):
                return nc.tensor.matmul(o, w, x, start=start, stop=stop)

            def split_mm(o, w_hi, w_lo, x_hi, x_lo):
                mm(o, w_hi, x_hi, True, False)
                mm(o, w_lo, x_hi, False, False)
                return mm(o, w_hi, x_lo, False, True)

            pe.wait_ge(mixer_in, 16 * N_MIXER)
            mm(ps[:, 0, 0:D], w_u[:], from_u[:, 0])
            mm(ps[:, 0, D:2 * D], w_u[:], from_u[:, 1]).then_inc(composed, 1)
            pe.wait_ge(consts, 1)

            def x_mm(w, n, u, start=True, stop=True):
                mm(bank(n), mix_hi[:, w], xin_hi[:, u], start, False)
                mm(bank(n), mix_lo[:, w], xin_hi[:, u], False, False)
                return mm(bank(n), mix_hi[:, w], xin_lo[:, u], False, stop)

            def mix_in(n, u):
                pe.wait_ge(xinlo_ready, n + 1)
                if not isinstance(n, int) or n > 0:
                    pe.wait_ge(x1_ready, n)
                x_mm(DELTA, DT, u).then_inc(dt_ready, 1)
                x_mm(GATE, ZG, u).then_inc(zg_ready, 1)
                x_mm(STATE, BT, u).then_inc(bt_ready, 1)

            def mix_y(n):
                pe.wait_ge(states_ready, n + 1)
                mm(bank(DT), w_c[:], states[:]).then_inc(y_ready, 1)

            def mix_skip(n, u):
                x_mm(SKIP, BT, u, True, False)

            def mix_out(n):
                pe.wait_ge(mixed_ready, n + 1)
                mm(bank(BT), w_out[:], mixed[:], False, True).then_inc(x1c_ready, 1)

            def var1(n):
                pe.wait_ge(sq1_ready, n + 1)
                mm(bank(MISC), mean_mat[:], square[:]).then_inc(var1_ready, 1)

            def var2(i):
                pe.wait_ge(sq2_ready, i + 1)
                mm(bank(MISC), mean_mat[:], square[:]).then_inc(var2_ready, 1)

            def gate(i, e):
                pe.wait_ge(mask_ready, E * i + e + 1)
                if not isinstance(i, int) or E * i + e > 0:
                    pe.wait_ge(gsb_ready, E * i + e)
                mm(bank(G), ones_r[:], masked[:, e % 2]).then_inc(gate_ready, 1)

            def up(i, e, u):
                if e == 0:
                    pe.wait_ge(x1hi_ready, i + 1)
                    pe.wait_ge(x1lo_ready, i + 1)
                for h in range(HALF):
                    if not isinstance(i, int) or E * i + e > 0:
                        pe.wait_ge(hid_ready, 16 * i + 2 * e + h - 1)
                    c = slice(h * P, (h + 1) * P)
                    split_mm(bank(h), proj_in_hi[:, e, c], proj_in_lo[:, e, c], x1_hi[:, u], x1_lo[:, u]).then_inc(h_ready, 1)

            def down(i, e):
                if e == 0:
                    if not isinstance(i, int) or i > 0:
                        pe.wait_ge(x2c_ready, i)
                    else:
                        pe.wait_ge(out_ready, 1)
                for h in range(HALF):
                    n = e * HALF + h
                    pe.wait_ge(hid_hi_ready, 16 * i + 2 * e + h + 1)
                    mm(bank(ACC), proj_out_hi[:, n], hid_hi[:, e % 4, h], n == 0, False)
                    mm(bank(ACC), proj_out_lo[:, n], hid_hi[:, e % 4, h], False, False)
                    pe.wait_ge(hid_lo_ready, 16 * i + 2 * e + h + 1)
                    last = mm(bank(ACC), proj_out_hi[:, n], hid_lo[:, e % 4, h], False, n == E * HALF - 1)
                last.then_inc(down_done, 1)

            def logit(i, u):
                pe.wait_ge(x2_ready, i + 1)
                for s in range(SUB):
                    last = mm(bank(MISC)[:, s * NE:(s + 1) * NE], every_fourth(x2[:, u], s), router_w[:])
                last.then_inc(logits_ready, 1)

            def turn_rows(k, x, n):
                pe.wait_ge(x2_ready, k + 1)
                for s in range(SUB):
                    last = nc.tensor.transpose(bank(n)[:, s * P:(s + 1) * P], every_fourth(x, s), ident[:])
                last.then_inc(rows_turned, 1)

            def count(k, w):
                pe.wait_ge(picked, k * PICKS + PICKS)
                flat = chosen[:, w].rearrange("p s e -> p (s e)")
                mm(bank(MISC)[:, TALLY:TALLY + SUB * NE], before[:], flat)
                mm(bank(MISC)[:, TALLY + SUB * NE:TALLY + 2 * SUB * NE], ones_b[:], flat).then_inc(tallied, 1)

            def body(i, u, mix, tail_of, ahead):
                late = not isinstance(i, int)
                for e in range(E):
                    up(i, e, u)
                    if e + 1 < E:
                        gate(i, e + 1)
                    elif mix:
                        gate(i + 1, 0)
                    if e == 3:
                        if mix:
                            mix_skip(i + 1, 1 - u)
                        if tail_of:
                            if not isinstance(i, int) or i > 1:
                                pe.wait_ge(logits_kept, i - 1)
                            if late or i > 2:
                                pe.wait_ge(tally_kept, i - 2)
                            var2(i - 1)
                        if mix:
                            mix_out(i + 1)
                    if e == 4 and mix:
                        if tail_of:
                            pe.wait_ge(ln2_ready, i)
                        var1(i + 1)
                    if e >= 2:
                        down(i, e - 2)
                    elif tail_of:
                        down(i - 1, E - 2 + e)
                    if e == 2 and mix:
                        mix_y(i + 1)
                    if e == 6 and tail_of:
                        if mix:
                            pe.wait_ge(ln1_ready, i + 2)
                        logit(i - 1, 1 - u)
                        if late or i >= 2:
                            count(i - 2, u)
                    if e == 5 and (late or i >= 2):
                        turn_rows(i - 2, x2[:, u], ZG)
                    if e == 7 and ahead:
                        if late or i >= 2:
                            pe.wait_ge(rows_ready, i * 2 - 2)
                        mix_in(i + 2, u)

            mix_in(0, 0)
            mix_y(0)
            pe.wait_ge(skip_ready, 1)
            mix_skip(0, 0)
            mix_out(0)
            var1(0)
            gate(0, 0)
            mix_in(1, 1)
            pe.wait_ge(weights_ready, 1)
            body(0, 0, True, False, True)
            body(1, 1, True, True, True)
            body(2, 0, True, True, True)
            with pe.Fori(1, (NT - 4) // 2) as j:
                body(j * 2 + 1, 1, True, True, True)
                body(j * 2 + 2, 0, True, True, True)
            body(NT - 3, 1, True, True, True)
            body(NT - 2, 0, True, True, False)
            body(NT - 1, 1, False, True, False)
            down(NT - 1, E - 2)
            down(NT - 1, E - 1)

            def shared_down(i, v4):
                if not isinstance(i, int) or i > 0:
                    pe.wait_ge(y_kept, i)
                for n in range(NS * HALF):
                    pe.wait_ge(ghi_ready, 4 * i + n + 1)
                    mm(bank(7), sw3_hi[:, n], glu_hi[:, v4 % 2, n], n == 0, False)
                    mm(bank(7), sw3_lo[:, n], glu_hi[:, v4 % 2, n], False, False)
                    pe.wait_ge(glo_ready, 4 * i + n + 1)
                    last = mm(bank(7), sw3_hi[:, n], glu_lo[:, v4 % 2, n], False, n == NS * HALF - 1)
                last.then_inc(sum_ready, 1)

            def shared_turn(i, v4, b=6):
                if not isinstance(i, int) or 0 < i < NT - 1:
                    pe.wait_ge(total_ready, i)
                pe.wait_ge(y_kept, i + 1)
                for s in range(SUB):
                    last = nc.tensor.transpose(bank(b)[:, s * P:(s + 1) * P], every_fourth(y_sum[:, v4 % 2], s), ident[:])
                last.then_inc(turned, 1)

            def shared_tile(i, v4, between=(None,) * 4):
                late = not isinstance(i, int)
                pe.wait_ge(xhi_ready, i + 1)
                pe.wait_ge(xlo_ready, i + 1)
                for n in range(NS * HALF):
                    s, h = n // HALF, n % HALF
                    if n == 3:
                        pe.wait_ge(glu_ready, 4 * i + 1)
                    elif late or i > 0:
                        pe.wait_ge(glu_ready, 4 * i if n == 0 else 4 * i - 3 + n)
                    c = slice(h * P, (h + 1) * P)
                    for k in range(2):
                        last = split_mm(bank(2 * (n % 3) + k), sw_hi[:, s, k, c], sw_lo[:, s, k, c], xs_hi[:, v4 % 2], xs_lo[:, v4 % 2])
                    last.then_inc(up_ready, 1)
                    if between[n]:
                        between[n]()
                    if n == 2 and (late or i >= 2):
                        shared_turn(i - 2, v4)
                    if n == 3 and (late or i >= 1):
                        shared_down(i - 1, (v4 - 1) % 4)

            def last_var():
                pe.wait_ge(logits_kept, NT - 1)
                pe.wait_ge(tally_kept, NT - 2)
                var2(NT - 1)

            def last_logit():
                pe.wait_ge(ln2_ready, NT)
                logit(NT - 1, 1)
                count(NT - 2, 0)

                last_rows()

            def last_rows():
                pe.wait_ge(rows_ready, 2 * NT - 2)
                turn_rows(NT - 1, x2[:, 1], DT)

            def last_count():
                pe.wait_ge(logits_kept, NT)
                pe.wait_ge(tally_kept, NT - 1)
                count(NT - 1, 1)

            def banks_left():
                pe.wait_ge(rows_ready, 2 * NT)
                pe.wait_ge(tally_kept, NT)

            turn_rows(NT - 2, x2[:, 0], DT)
            shared_tile(0, 0, (last_var, None, last_logit, None))
            shared_tile(1, 1, (None, last_count, banks_left, None))
            for i in range(2, 4):
                shared_tile(i, i)
            with pe.Fori(1, NT // 4) as jj:
                for v4 in range(4):
                    shared_tile(jj * 4 + v4, v4)
            shared_turn(NT - 2, 2)
            shared_down(NT - 1, 3)
            def block_turn(j, u, round):
                pe.wait_ge(xr_in[u], round * 16 + 16)
                if not isinstance(j, int) or j > 0:
                    pe.wait_ge(r_lo_ready, j)
                for s in range(SUB):
                    last = nc.tensor.transpose(bank(6)[:, s * P:(s + 1) * P], xr[:, u, s, 0:D], ident[:])
                last.then_inc(r_t_ready, 1)

            def block_up(j, u, round, h):
                if h == 0:
                    pe.wait_ge(wb_in[u], round * 16 + 16)
                    pe.wait_ge(r_hi_ready, j + 1)
                    pe.wait_ge(r_lo_ready, j + 1)
                if not isinstance(j, int) or j > 0:
                    pe.wait_ge(r_glu_ready, 2 * j - 1 + h)
                for k in range(2):
                    c = slice(k * H + h * P, k * H + (h + 1) * P)
                    d = slice(2 * H + k * H + h * P, 2 * H + k * H + (h + 1) * P)
                    last = split_mm(bank(2 * h + k), wbs[u][:, c], wbs[u][:, d], xs_hi[:, u % 2], xs_lo[:, u % 2])
                last.then_inc(r_up_ready, 1)

            def block_down(j, u):
                pe.wait_ge(r_glu_ready, 2 * j + 2)
                if not isinstance(j, int) or j > 0:
                    pe.wait_ge(r_res_ready, j)
                for s in range(SUB):
                    for h in range(HALF):
                        last = mm(bank(7)[:, s * P:(s + 1) * P], glu[:, u % 2 * HALF + h, s * P:(s + 1) * P],
                                  wbs[u][:, W3AT + h * D:W3AT + (h + 1) * D].bitcast(F32), h == 0, h == HALF - 1)
                last.then_inc(r_sum_ready, 1)

            def routed(j, u, round, nxt, prev):
                block_up(j, u, round, 0)
                if nxt:
                    block_turn(j + 1, (u + 1) % DEEP, round + (u + 1) // DEEP)
                if prev:
                    block_down(j - 1, (u - 1) % DEEP)
                block_up(j, u, round, 1)

            pe.wait_ge(total_ready, NT - 1)
            block_turn(0, 0, 0)
            shared_turn(NT - 1, 3, 4)
            for j in range(DEEP):
                routed(j, j, 0, True, j > 0)
            with pe.Fori(1, NBLK // DEEP) as jj:
                for u in range(DEEP):
                    routed(jj * DEEP + u, u, jj, True, True)
            for j in range(NBLK // DEEP * DEEP, NBLK):
                routed(j, j % DEEP, j // DEEP, j + 1 < NBLK, True)
            block_down(NBLK - 1, (NBLK - 1) % DEEP)


PICKS = 12
PLACES = 12
N_MIXER = 9
N_EARLY = 3
N_LATE = 10


def kernel(**inputs):
    import numpy as np
    import concourse.bacc as bacc
    from concourse.bass_utils import run_bass_kernel_spmd

    def lay(x):
        return np.ascontiguousarray(x)

    g = {k: np.asarray(v) for k, v in inputs.items()}
    B, S, D = g["x"].shape
    NE, _, H = g["L0_ffn_rw1"].shape
    E = g["L0_xattn_proj_in"].shape[0]
    K = g["ctx_512"].shape[1]
    W_in = g["L0_attn_W_in"]

    def up(w):
        return lay(w.transpose(1, 0, 2))

    def down(w):
        n, h, d = w.shape
        return lay(w.reshape(n, h // 128, 128, d).transpose(2, 0, 1, 3))

    def bias(b):
        n, h = b.shape
        return lay(b.reshape(n, h // 128, 128).transpose(2, 0, 1))

    arrays = {
        "xT": lay(g["x"].reshape(B * S, D).T),
        "w_ctx": lay(g["ctx_512"].transpose(1, 0, 2).reshape(K, B * S)),
        "ens": lay(g["itok_BxS2xS_0_7"].transpose(1, 0, 2).reshape(K, B * S)),
        "w_u": lay(W_in[:D]),
        "w_gate": lay(W_in[D:].T),
        "w_state": lay(g["L0_attn_W_state"].T),
        "w_dt": lay(g["L0_attn_W_dt"].T),
        "w_c": lay(g["L0_attn_W_C"].T),
        "w_out": lay(g["L0_attn_W_out"].T),
        "b_dt": g["L0_attn_b_dt"], "D": g["L0_attn_D"], "A_log": g["L0_attn_A_log"],
        "proj_in": lay(g["L0_xattn_proj_in"].transpose(2, 0, 1)),
        "proj_out": down(lay(g["L0_xattn_proj_out"].transpose(0, 2, 1))),
        "gate_w": g["L0_ffn_gate_w"], "gate_b": g["L0_ffn_gate_b"],
        "w1": up(g["L0_ffn_rw1"]), "w2": up(g["L0_ffn_rw2"]), "w3": down(g["L0_ffn_rw3"]),
        "b1": bias(g["L0_ffn_rb1"]), "b2": bias(g["L0_ffn_rb2"]), "b3": g["L0_ffn_rb3"],
        "sw1": up(g["L0_ffn_sw1"]), "sw2": up(g["L0_ffn_sw2"]), "sw3": down(g["L0_ffn_sw3"]),
        "sb1": bias(g["L0_ffn_sb1"]), "sb2": bias(g["L0_ffn_sb2"]), "sb3": g["L0_ffn_sb3"],
    }
    nc = bacc.Bacc("TRN2", target_bir_lowering=False, num_devices=1)
    aps = {n: nc.dram_tensor(f"in_{n}", x.shape, mybir.dt.from_np(x.dtype), kind="ExternalInput").ap() for n, x in arrays.items()}
    aps["seq"] = S
    out = nc.dram_tensor("out_0", (B * S, D), F32, kind="ExternalOutput").ap()
    decoder_layer(nc, aps, out)
    r = run_bass_kernel_spmd(nc, [{f"in_{n}": x for n, x in arrays.items()}], core_ids=[0])
    return r.results[0]["out_0"].reshape(B, S, D)
```
